# Optimizing a Trainium2 kernel written in Bass

```python
import numpy as np
import jax
import jax.numpy as jnp

def _softmax(x, axis=-1):
    return jax.nn.softmax(x, axis=axis)

def _gelu(x):
    return jax.nn.gelu(x, approximate=True)

def _silu(x):
    return jax.nn.silu(x)

def _sigmoid(x):
    return jax.nn.sigmoid(x)

def _layernorm(x, axis=-1, eps=1e-05):
    m = jnp.mean(x, axis=axis, keepdims=True)
    v = jnp.var(x, axis=axis, keepdims=True)
    return (x - m) / jnp.sqrt(v + eps)

def _scatter_add(tgt, idx, src, axis=0):
    return tgt.at[idx].add(src)

def _segment_sum(src, seg, n):
    return jax.ops.segment_sum(src, seg, n)
kernel_name = 'mk_gps_d1_gnn_r32_078129'

def setup_inputs(seed: int=0):
    np.random.seed(seed)
    _w = jnp.asarray

    def _rec_inputs():
        import jax
        import jax.numpy as jnp
        _gk = jax.random.key(seed)
        x = -6.415e-05 + 1 * jax.random.normal(jax.random.fold_in(_gk, 1), (625, 512), jnp.float32)
        _s = jax.random.randint(jax.random.fold_in(_gk, 2), (5000,), 0, 625, jnp.int32)
        _d = jax.random.randint(jax.random.fold_in(_gk, 3), (5000,), 0, 625, jnp.int32)
        _loop = jnp.arange(625, dtype=jnp.int32)
        src = jnp.concatenate([_s, _d, _loop])
        dst = jnp.concatenate([_d, _s, _loop])
        _o = jnp.argsort(dst, stable=True)
        src = src[_o]
        dst = dst[_o]
        edge_type_3 = jax.random.randint(jax.random.fold_in(_gk, 12), (10625,), 0, 3, jnp.int32)
        node_type_3 = jax.random.randint(jax.random.fold_in(_gk, 13), (625,), 0, 3, jnp.int32)
        return (x, src, dst, edge_type_3, node_type_3)
    x, src, dst, edge_type_3, node_type_3 = _rec_inputs()

    def _L0_gnn_setup():
        import jax, jax.numpy as jnp
        import numpy as np
        N_NODES = 625
        N_EDGES = 150000
        D_IN = 512
        D_OUT = 512
        N_REL = 3
        N_NT = 3
        key = jax.random.key(seed)
        ks = jax.random.split(key, 8)
        x = jax.random.normal(ks[0], (N_NODES, D_IN), dtype=jnp.float32)
        W_rel = jax.random.normal(ks[1], (N_REL, D_IN, D_OUT), dtype=jnp.float32) * 0.02
        b_rel = jnp.zeros((N_REL, D_OUT), dtype=jnp.float32)
        W_self = jax.random.normal(ks[2], (N_NT, D_IN, D_OUT), dtype=jnp.float32) * 0.02
        b_self = jnp.zeros((N_NT, D_OUT), dtype=jnp.float32)
        edge_src = jax.random.randint(ks[3], (N_EDGES,), 0, N_NODES, dtype=jnp.int32)
        edge_dst = jax.random.randint(ks[4], (N_EDGES,), 0, N_NODES, dtype=jnp.int32)
        edge_type = jax.random.randint(ks[5], (N_EDGES,), 0, N_REL, dtype=jnp.int32)
        node_type = jax.random.randint(ks[6], (N_NODES,), 0, N_NT, dtype=jnp.int32)
        return {'x': x, 'W_rel': W_rel, 'b_rel': b_rel, 'W_self': W_self, 'b_self': b_self, 'edge_src': edge_src, 'edge_dst': edge_dst, 'edge_type': edge_type, 'node_type': node_type}
    _L0_gnn_all = _L0_gnn_setup()
    _L0_gnn_in = {k: v for k, v in _L0_gnn_all.items() if k in ('W_rel', 'b_rel', 'W_self', 'b_self')}
    del _L0_gnn_all

    def _L0_mix_setup():
        import jax, jax.numpy as jnp
        import numpy as np
        DIM = 512
        HEADS = 8

        def _reference_tuple_inner(x, Wqkv, temperature, Wproj, bproj):
            B, N, C = x.shape
            H = temperature.shape[0]
            D = C // H
            qkv = (x @ Wqkv.T).reshape(B, N, 3, H, D).transpose(2, 0, 3, 1, 4)
            q, k, v = (qkv[0], qkv[1], qkv[2])
            q = jax.nn.relu(q)
            k = jax.nn.relu(k)
            ksum = k.sum(axis=2)
            denom = jnp.clip(jnp.einsum('bhnd,bhd->bhn', q, ksum), 100.0)[..., None]
            attn = jnp.einsum('bhnd,bhne->bhde', k, v) * temperature
            attn1 = jnp.einsum('bhnd,bhde->bhne', q, attn)
            out = attn1 / denom
            y = out.transpose(0, 2, 1, 3).reshape(B, N, C) @ Wproj.T + bproj
            return (y, attn1)
        key = jax.random.key(seed)
        k1, k2, k3, k4 = jax.random.split(key, 4)
        head_dim = DIM // HEADS
        scale = head_dim ** (-0.5)
        x = jax.random.normal(k1, (4, 128, DIM), dtype=jnp.float32)
        Wqkv = jax.random.normal(k2, (3 * DIM, DIM), dtype=jnp.float32) * DIM ** (-0.5)
        temperature = jnp.ones((HEADS, 1, 1), dtype=jnp.float32) * scale
        Wproj = jax.random.normal(k3, (DIM, DIM), dtype=jnp.float32) * DIM ** (-0.5)
        bproj = jnp.zeros((DIM,), dtype=jnp.float32)
        return {'x': x, 'Wqkv': Wqkv, 'temperature': temperature, 'Wproj': Wproj, 'bproj': bproj}
    _L0_mix_all = _L0_mix_setup()
    _L0_mix_in = {k: v for k, v in _L0_mix_all.items() if k in ('Wqkv', 'temperature', 'Wproj', 'bproj')}
    del _L0_mix_all

    def _L0_ffn_setup():
        import jax, jax.numpy as jnp
        import numpy as np
        CAPACITY_FACTOR = 1.2
        key = jax.random.key(seed)
        k1, k2, k3 = jax.random.split(key, 3)
        B, S, D, E = (8, 128, 512, 16)
        x = jax.random.normal(k1, (B, S, D), dtype=jnp.float32)
        switch_w = jax.random.normal(k2, (E, D), dtype=jnp.float32) * 0.02
        switch_b = jnp.zeros((E,), dtype=jnp.float32)
        expert_w = jax.random.normal(k3, (E, D, D), dtype=jnp.float32) * 0.02
        expert_b = jnp.zeros((E, D), dtype=jnp.float32)
        return {'x': x, 'switch_w': switch_w, 'switch_b': switch_b, 'expert_w': expert_w, 'expert_b': expert_b}
    _L0_ffn_all = _L0_ffn_setup()
    _L0_ffn_in = {k: v for k, v in _L0_ffn_all.items() if k in ('switch_w', 'switch_b', 'expert_w', 'expert_b')}
    del _L0_ffn_all
    return {'x': x, 'src': src, 'dst': dst, 'edge_type_3': edge_type_3, 'node_type_3': node_type_3, 'L0_gnn_W_rel': _L0_gnn_in['W_rel'], 'L0_gnn_b_rel': _L0_gnn_in['b_rel'], 'L0_gnn_W_self': _L0_gnn_in['W_self'], 'L0_gnn_b_self': _L0_gnn_in['b_self'], 'L0_mix_Wqkv': _L0_mix_in['Wqkv'], 'L0_mix_temperature': _L0_mix_in['temperature'], 'L0_mix_Wproj': _L0_mix_in['Wproj'], 'L0_mix_bproj': _L0_mix_in['bproj'], 'L0_ffn_switch_w': _L0_ffn_in['switch_w'], 'L0_ffn_switch_b': _L0_ffn_in['switch_b'], 'L0_ffn_expert_w': _L0_ffn_in['expert_w'], 'L0_ffn_expert_b': _L0_ffn_in['expert_b']}

def reference(x, src, dst, edge_type_3, node_type_3, L0_gnn_W_rel, L0_gnn_b_rel, L0_gnn_W_self, L0_gnn_b_self, L0_mix_Wqkv, L0_mix_temperature, L0_mix_Wproj, L0_mix_bproj, L0_ffn_switch_w, L0_ffn_switch_b, L0_ffn_expert_w, L0_ffn_expert_b):
    import jax
    import jax.numpy as jnp

    def _L0_gnn_ref(x, W_rel, b_rel, W_self, b_self, edge_src, edge_dst, edge_type, node_type):
        import jax, jax.numpy as jnp
        import numpy as np
        N_NODES = 625
        N_EDGES = 150000
        D_IN = 512
        D_OUT = 512
        N_REL = 3
        N_NT = 3
        xr = jnp.einsum('nd,rde->rne', x, W_rel)
        msg = xr[edge_type, edge_src] + b_rel[edge_type]
        agg = jax.ops.segment_sum(msg, edge_dst, num_segments=N_NODES)
        xs = jnp.einsum('nd,tde->tne', x, W_self)
        h_self = xs[node_type, jnp.arange(N_NODES)] + b_self[node_type]
        return jax.nn.relu(h_self + agg)

    def _L0_mix_ref(x, Wqkv, temperature, Wproj, bproj):
        import jax, jax.numpy as jnp
        import numpy as np
        DIM = 512
        HEADS = 8

        def _reference_tuple_inner(x, Wqkv, temperature, Wproj, bproj):
            B, N, C = x.shape
            H = temperature.shape[0]
            D = C // H
            qkv = (x @ Wqkv.T).reshape(B, N, 3, H, D).transpose(2, 0, 3, 1, 4)
            q, k, v = (qkv[0], qkv[1], qkv[2])
            q = jax.nn.relu(q)
            k = jax.nn.relu(k)
            ksum = k.sum(axis=2)
            denom = jnp.clip(jnp.einsum('bhnd,bhd->bhn', q, ksum), 100.0)[..., None]
            attn = jnp.einsum('bhnd,bhne->bhde', k, v) * temperature
            attn1 = jnp.einsum('bhnd,bhde->bhne', q, attn)
            out = attn1 / denom
            y = out.transpose(0, 2, 1, 3).reshape(B, N, C) @ Wproj.T + bproj
            return (y, attn1)
        return _reference_tuple_inner(x, Wqkv, temperature, Wproj, bproj)[0]

    def _L0_ffn_ref(x, switch_w, switch_b, expert_w, expert_b):
        import jax, jax.numpy as jnp
        import numpy as np
        CAPACITY_FACTOR = 1.2
        B, S, D = x.shape
        E = switch_w.shape[0]
        N = B * S
        xf = x.reshape(N, D)
        logits = xf @ switch_w.T + switch_b
        probs = jax.nn.softmax(logits, axis=-1)
        route_probs = jnp.max(probs, axis=-1)
        routes = jnp.argmax(probs, axis=-1)
        oh = jax.nn.one_hot(routes, E, dtype=jnp.int32)
        pos = jnp.take_along_axis(jnp.cumsum(oh, axis=0), routes[:, None], axis=1)[:, 0] - 1
        capacity = int(CAPACITY_FACTOR * N / E)
        keep = pos < capacity
        buf = jnp.zeros((E, capacity, D), dtype=xf.dtype).at[routes, pos].set(xf)
        y = jnp.einsum('ecd,efd->ecf', buf, expert_w) + expert_b[:, None, :]
        gathered = y[routes, jnp.minimum(pos, capacity - 1)]
        out = jnp.where(keep[:, None], gathered, xf) * route_probs[:, None]
        return out.reshape(B, S, D)
    xn = _layernorm(x, axis=-1)
    x = x + _L0_gnn_ref(xn, L0_gnn_W_rel, L0_gnn_b_rel, L0_gnn_W_self, L0_gnn_b_self, src, dst, edge_type_3, node_type_3) + _L0_mix_ref(xn[None], L0_mix_Wqkv, L0_mix_temperature, L0_mix_Wproj, L0_mix_bproj)[0]
    x = x + _L0_ffn_ref(_layernorm(x, axis=-1)[None], L0_ffn_switch_w, L0_ffn_switch_b, L0_ffn_expert_w, L0_ffn_expert_b)[0]
    return x

_drawn_inputs = setup_inputs


def setup_inputs(seed=0):
    import zlib

    import numpy as np

    out = dict(_drawn_inputs(seed))
    spreads = {'L0_gnn_b_rel': (0.0, 0.1),
     'L0_gnn_b_self': (0.0, 0.1),
     'L0_mix_temperature': (0.125, 0.6),
     'L0_mix_bproj': (0.0, 0.1),
     'L0_ffn_switch_b': (0.0, 0.289),
     'L0_ffn_expert_b': (0.0, 0.752)}
    factors = {'L0_mix_Wqkv': 8.0, 'L0_mix_Wproj': 8.0}
    for name, (base, spread) in spreads.items():
        noise = np.random.default_rng([zlib.crc32(name.encode()), seed]).standard_normal(out[name].shape)
        drawn = base * np.exp(spread * noise) if base else spread * noise
        out[name] = jnp.asarray(drawn.astype(out[name].dtype))
    for name, factor in factors.items():
        out[name] = (out[name] * factor).astype(out[name].dtype)
    return out
```

```python
import concourse.bass as bass
from concourse import mybir
from contextlib import ExitStack


def gps_layer_kernel(
    nc: bass.Bass,
    x: bass.AP,
    src: bass.AP,
    dst: bass.AP,
    edge_type: bass.AP,
    node_type: bass.AP,
    W_rel: bass.AP,
    b_rel: bass.AP,
    W_self: bass.AP,
    b_self: bass.AP,
    Wqkv: bass.AP,
    temperature: bass.AP,
    Wproj: bass.AP,
    bproj: bass.AP,
    switch_w: bass.AP,
    switch_b: bass.AP,
    expert_w: bass.AP,
    expert_b: bass.AP,
    out: bass.AP,
):
    F32, F16, I32, U32 = mybir.dt.float32, mybir.dt.float16, mybir.dt.int32, mybir.dt.uint32
    ALU = mybir.AluOpType
    ACT = mybir.ActivationFunctionType
    AX = mybir.AxisListType

    P = 128
    N, D = x.shape
    NE = src.shape[0]
    R = W_rel.shape[0]
    NTY = W_self.shape[0]
    H = temperature.shape[0]
    DH = D // H
    EX = switch_w.shape[0]
    CAP = int(1.2 * N / EX)
    NT = (N + P - 1) // P
    TAIL = N - (NT - 1) * P
    NP = NT * P
    KC = D // P
    HP = D // P
    EPS = 1e-5
    WS = 256.0
    RS = 1.0 / WS

    WIN = 32
    NW = NP // WIN
    J = 5
    GE = J * P
    NG = -(-NE // GE)
    NG += NG % 2
    EPAD = NG * GE
    EC = 85
    EP = NE // EC
    assert EP * EC == NE and EP <= P and NE + GE <= EPAD
    NOKEY = 5000.0

    CS = 48
    HALF = 64
    NBT = EX // 2
    OOB = 100000.0

    ctx = ExitStack()
    with ctx:
        def sb(name, shape, dt):
            return ctx.enter_context(nc.sbuf_tensor(name, shape, dt))

        def sem(name):
            return ctx.enter_context(nc.semaphore(name))

        NSTAGE, NSPLIT = 3, 4
        x_sb = sb("x_sb", [P, NT, D], F32)
        xs = sb("xs", [P, NT, D], F32)
        xhi = sb("xhi", [P, KC, NP], F16)
        xlo = sb("xlo", [P, KC, NP], F16)
        stage = [sb(f"stage{i}", [P, KC, D], F32) for i in range(NSTAGE)]
        whi = [sb(f"whi{i}", [P, KC, D], F16) for i in range(NSPLIT)]
        wlo = [sb(f"wlo{i}", [P, KC, D], F16) for i in range(NSPLIT)]
        early = sb("early", [P, 12288], F32)
        k_sb = early[:, 0:2560].rearrange("p (t d) -> p t d", t=NT)
        v_sb = early[:, 2560:5120].rearrange("p (t d) -> p t d", t=NT)
        q_sb = early[:, 5120:7680].rearrange("p (t d) -> p t d", t=NT)
        qnT = early[:, 7680:10240].rearrange("p (g n) -> p g n", g=HP)
        projT = early[:, 10240:12288].rearrange("p (g n) -> p g n", g=HP)
        onehot_s = early[:, 0:3200].bitcast(F16).rearrange("p (b j n) -> p b j n", b=2, j=J)
        onehot_d = early[:, 3200:3680].bitcast(F16).rearrange("p (b j r d) -> p b j r d", b=2, j=J, r=R)
        bias_tok = early[:, 0:2560].rearrange("p (t d) -> p t d", t=NT)
        gath = early[:, 2560:5120].rearrange("p (t d) -> p t d", t=NT)
        xfT = early[:, 5120:6144].rearrange("p (b k n) -> p b k n", b=2, k=KC)
        ylow = early[:, 6144:7168].rearrange("p (b d) -> p b d", b=2)
        yexp = early[:, 7168:8192].rearrange("p (b d) -> p b d", b=2)
        prod = xs[:, 0:2, :]
        Pm = xs[:, 0:HP, :]
        xr = sb("xr", [P, 2, R * NT, D], F16)
        buf_sb = xr[:].rearrange("p h t d -> p (h t d)")[:, 0:NBT * D * 2].bitcast(F32)\
            .rearrange("p (i d) -> p i d", i=NBT)
        at_sb = sb("at_sb", [P, R * NT, NP], F16)
        bT = at_sb[:].rearrange("p t n -> p (t n)")[:, 0:KC * EX * P]\
            .rearrange("p (k e c) -> p k e c", k=KC, e=EX)
        attnT = sb("attnT", [P, HP, P], F32)
        ksumB = xs[:, NT - 1, :]
        pre = at_sb[:].rearrange("p t n -> p (t n)").bitcast(F32)
        zero = pre[:, 0:D]
        edges = pre[:, D:D + 4 * EC].bitcast(I32).rearrange("p (a c) -> p a c", a=4)
        ef = pre[:, D + 4 * EC:D + 8 * EC].rearrange("p (a c) -> p a c", a=4)
        cmp = pre[:, D + 8 * EC:D + 10 * EC].rearrange("p (a c) -> p a c", a=2)
        padk = pre[0:1, D + 10 * EC:D + 10 * EC + EPAD - NE]
        ident = sb("ident", [P, P], F32)
        onesf = sb("onesf", [P, P], F32)
        ones16 = sb("ones16", [P, P], F16)
        tri16 = sb("tri16", [P, P], F16)
        iota_s = sb("iota_s", [P, NP], F16)
        iota_d = sb("iota_d", [P, R, NP], F16)
        iota_e = sb("iota_e", [P, EX], F32)
        sel_rel = sb("sel_rel", [P, R, P], F16)
        sel_row = sb("sel_row", [P, NTY + 1, P], F16)
        brow = sb("brow", [P, D], F32)
        brow_hi = sb("brow_hi", [P, D], F16)
        brow_lo = sb("brow_lo", [P, D], F16)
        temp = sb("temp", [P, HP], F32)
        swb = sb("swb", [P, EX], F32)
        sw_sb = sb("sw_sb", [EX, D], F32)
        swT = sb("swT", [P, KC, EX], F32)
        cnt = sb("cnt", [P, NW], F32)
        lim = sb("lim", [1, NW + 4], F32)
        num = sb("num", [1, NW], F32)
        limi = sb("limi", [1, NW + 1], I32)
        wkeys = sb("wkeys", [P, NW, 2, J], F32)
        gkeys = sb("gkeys", [P, 2, NG, J], F32)
        nt_i = sb("nt_i", [P, NT], I32)
        nmask = sb("nmask", [P, NTY, NT], F32)
        stats = sb("stats", [P, NT, 6], F32)
        mv = sb("mv", [P, NT, 2], F32)
        sd = sb("sd", [P, 4, NT], F32)
        den = sb("den", [P, 2, NT, H], F32)
        lg = sb("lg", [P, 4, NT, EX], F32)
        oh16 = sb("oh16", [P, NT, EX], F16)
        rt = sb("rt", [P, 12, NT], F32)
        slots = sb("slots", [P, 3, NT], I32)

        tbank = [ctx.enter_context(nc.psum_tensor(f"tbank{i}", [P, KC, P], F32)) for i in range(3)]
        mbank = [ctx.enter_context(nc.psum_tensor(f"mbank{i}", [P, D], F32)) for i in range(3)]
        abank = [ctx.enter_context(nc.psum_tensor(f"abank{i}", [P, D], F32)) for i in range(2)]

        key_dram = nc.dram_tensor("key_scratch", (2, EPAD), F32, kind="Internal").ap()
        buf_dram = nc.dram_tensor("buf_scratch", (EX * CS, D), F32, kind="Internal").ap()
        y_dram = nc.dram_tensor("y_scratch", (EX * CS, D), F32, kind="Internal").ap()

        DENSE = ["k", "v", "q", "r0", "r1", "r2", "p", "s0", "s1", "s2"]
        MATS = DENSE + [f"e{e}" for e in range(EX)]
        TURNED = {"k", "v", "q", "p"} | {f"e{e}" for e in range(EX)}
        SPLIT = [m for m in MATS if m != "p"]
        LEAD = 3
        TASKS = [("W", "k"), ("XT",), ("W", "v"), ("MM", "k"), ("W", "q"), ("MM", "v"), ("W", "r0"),
                 ("KV",), ("MM", "q"), ("W", "r1"), ("QN",), ("MM", "r0"), ("W", "p"), ("W", "r2"),
                 ("QT",), ("MM", "r1"), ("P",), ("Y",), ("W", "s0"), ("MM", "r2"), ("W", "s1"), ("W", "s2"),
                 ("AB",), ("MM", "s0"), ("W", "e0"), ("MM", "s1"), ("W", "e1"), ("MM", "s2"), ("W", "e2"),
                 ("SW",), ("AGG",)] + [("W", "e3"), ("CUM",), ("ROUTE",), ("BT",)]
        for e in range(EX):
            TASKS.append(("MM", f"e{e}"))
            if e + LEAD + 1 < EX:
                TASKS.append(("W", f"e{e + LEAD + 1}"))

        class Ring:

            def __init__(self, banks, name):
                self.banks, self.readers, self.first = banks, [], {}
                self.filled, self.act, self.dve = sem(name + "_filled"), sem(name + "_act"), sem(name + "_dve")

            def add(self, key, readers):
                self.first[key] = len(self.readers)
                self.readers += readers

            def act_count(self, u):
                return sum("A" in r for r in self.readers[:u + 1])

            def dve_count(self, u):
                return sum("D" in r for r in self.readers[:u + 1])

            def wait_free(self, eng, u):
                self.wait_emptied(eng, u - len(self.banks)) if u >= len(self.banks) else None

            def wait_emptied(self, eng, u):
                if "D" in self.readers[u]:
                    eng.wait_ge(self.dve, self.dve_count(u))
                else:
                    eng.wait_ge(self.act, self.act_count(u))

        tr, mr = Ring(tbank, "turn"), Ring(mbank, "prod")
        for task in TASKS:
            kind, m = task[0], task[-1]
            if kind == "W" and m in TURNED:
                tr.add(task, ["A" if m == "p" else "AD"] * KC)
            elif kind == "MM":
                mr.add(task, {"k": ["A"], "q": ["A"], "v": ["D"], "r": ["AD"], "s": ["D"]}.get(m[0], []) * NT
                       or ["AD"])
            elif kind in ("XT", "QT"):
                tr.add(task, ["AD" if kind == "XT" else "A"] * NT)
            elif kind == "KV":
                mr.add(task, ["D", "A"])
            elif kind == "P":
                mr.add(task, ["A"] * HP)
            elif kind == "Y":
                mr.add(task, ["D"] * NT)
            elif kind == "SW":
                tr.add(task, ["A"])
            elif kind == "AGG":
                mr.add(task, ["D"] * NT)
                tr.add(task, ["A"] * NT)
            elif kind == "BT":
                tr.add(task, ["AD"] * NBT)
        DIRECT = [m for _, m in [t for t in TASKS if t[0] == "W"] if m not in TURNED]

        s_x = [sem(f"x_in{t}") for t in range(NT)]
        s_w = [sem(f"weights_in{i}") for i in range(NSTAGE)]
        s_par = sem("params_in")
        s_const = sem("constants")
        s_edge = sem("edges_in")
        s_step = sem("dve_step")
        s_mv = sem("variance_ready")
        s_sd = sem("deviation_ready")
        s_ln = sem("normalised")
        s_dhi = sem("direct_hi")
        s_dlo = sem("direct_lo")
        s_bhi = sem("bias_hi")
        s_blo = sem("bias_lo")
        s_ekey = sem("edge_keys")
        s_cnt = sem("edge_counts")
        s_cntp = sem("edge_totals")
        s_lim = sem("window_limits")
        s_kst = sem("keys_stored")
        s_wk = sem("window_keys_in")
        s_gk = sem("group_keys_in")
        s_oh = sem("onehots_ready")
        s_ohf = sem("onehots_free")
        s_ab = sem("window_summed")
        s_abf = sem("window_bank_free")
        s_qn = sem("queries_scaled")
        s_lgp = sem("logits_ready")
        s_oh16 = sem("routes_ready")
        s_cum = sem("positions_ready")
        s_exd = sem("logits_shifted")
        s_exp = sem("exp_ready")
        s_slot = sem("slots_ready")
        s_zero = sem("buffers_zeroed")
        s_scat = sem("tokens_scattered")
        s_buf = sem("buffers_in")
        s_bt = sem("token_bias_in")
        s_yst = [sem(f"expert_out{i}") for i in range(2)]
        s_g = sem("tokens_gathered")
        s_fin = sem("result_ready")
        s_out = sem("stored")

        s_pool = sem("pool_step")
        N_CONST = 6

        block = ctx.enter_context(nc.Block())

        def rows(t):
            return TAIL if t == NT - 1 else P

        def stage_of(m):
            return MATS.index(m) % NSTAGE, 16 * (MATS.index(m) // NSTAGE + 1)

        def slot_of(m):
            return SPLIT.index(m) % NSPLIT

        def wait_split(eng, m):
            if m in TURNED:
                tr.wait_emptied(eng, tr.first[("W", m)] + KC - 1)
            else:
                eng.wait_ge(s_dlo, DIRECT.index(m) + 1)

        def wait_slot(eng, m):
            i = SPLIT.index(m) - NSPLIT
            if i >= 0:
                old = ("MM", SPLIT[i])
                eng.wait_ge(mr.filled, mr.first[old] + (1 if old[1][0] == "e" else NT))

        def store_expert(eng, e):
            mr.wait_emptied(eng, mr.first[("MM", f"e{e}")])
            eng.dma_start(y_dram[e * CS:(e + 1) * CS, :], yexp[0:CS, e % 2, :]).then_inc(s_yst[e % 2], 16)

        @block.sync
        def _(sp):
            for t in range(NT):
                if t == NT - 1:
                    sp.wait_ge(s_const, 1)
                sp.dma_start(x_sb[0:rows(t), t, :], x[t * P:t * P + rows(t), :]).then_inc(s_x[t], 16)
            source = {"k": Wqkv[D:2 * D], "v": Wqkv[2 * D:3 * D], "q": Wqkv[0:D], "p": Wproj}
            for r in range(R):
                source[f"r{r}"] = W_rel[r]
            for r in range(NTY):
                source[f"s{r}"] = W_self[r]
            for e in range(EX):
                source[f"e{e}"] = expert_w[e]
            for i, m in enumerate(MATS):
                if i >= NSTAGE:
                    old = MATS[i - NSTAGE]
                    if old in TURNED:
                        sp.wait_ge(tr.filled, tr.first[("W", old)] + KC)
                    else:
                        sp.wait_ge(s_dlo, DIRECT.index(old) + 1)
                sp.dma_start(stage[i % NSTAGE][:], source[m].rearrange("(k p) n -> p k n", p=P))\
                  .then_inc(s_w[i % NSTAGE], 16)
            for t in range(NT):
                sp.wait_ge(s_fin, t + 1)
                sp.dma_start(out[t * P:t * P + rows(t), :], gath[0:rows(t), t, :]).then_inc(s_out, 16)
            sp.wait_ge(s_out, 16 * NT)

        @block.gpsimd
        def _(pool):
            steps = [0]

            def link(ins):
                steps[0] += 1
                ins.then_inc(s_pool, 1)
                pool.wait_ge(s_pool, steps[0])

            nc.gpsimd.memset(x_sb[:, NT - 1, :], 0.0).then_inc(s_const, 1)
            link(nc.gpsimd.memset(edges[:, 2, :], 2 ** 20))
            flat = "(p c) -> p c"
            pool.dma_start(edges[0:EP, 1, :], dst.rearrange(flat, c=EC)).then_inc(s_edge, 16)
            pool.dma_start(edges[0:EP - 1, 2, :], dst[1:1 + (EP - 1) * EC].rearrange(flat, c=EC)).then_inc(s_edge, 16)
            pool.dma_start(edges[EP - 1:EP, 2, 0:EC - 1], dst[1 + (EP - 1) * EC:NE].unsqueeze(0)).then_inc(s_edge, 16)
            pool.dma_start(edges[0:EP, 0, :], src.rearrange(flat, c=EC)).then_inc(s_edge, 16)
            pool.dma_start(edges[0:EP, 3, :], edge_type.rearrange(flat, c=EC)).then_inc(s_edge, 16)
            link(nc.gpsimd.memset(ident[:], 0.0))
            nc.gpsimd.affine_select(out=ident[:], in_=ident[:], compare_op=ALU.not_equal, fill=1.0, base=0,
                                    pattern=[[-1, P]], channel_multiplier=1).then_inc(s_const, 1)
            link(nc.gpsimd.memset(brow[:], 0.0))
            link(nc.gpsimd.memset(nt_i[:], 0))
            pool.dma_start(brow[0:R, :], b_rel).then_inc(s_par, 16)
            pool.dma_start(brow[R:R + NTY, :], b_self).then_inc(s_par, 16)
            pool.dma_start(brow[R + NTY:R + NTY + 1, :], bproj.unsqueeze(0)).then_inc(s_par, 16)
            pool.dma_start(nt_i[:, 0:NT - 1], node_type[0:(NT - 1) * P].rearrange("(t p) -> p t", p=P),
                           allow_slow_non_contiguous=True).then_inc(s_par, 16)
            pool.dma_start(nt_i[0:TAIL, NT - 1:NT], node_type[(NT - 1) * P:N].unsqueeze(1)).then_inc(s_par, 16)
            tv = temperature.rearrange("(g h) a b -> h (a b g)", h=2)
            for h in range(2):
                pool.dma_start(temp[h * DH:(h + 1) * DH, :], tv[h:h + 1, :].to_broadcast([DH, HP]),
                               allow_slow_non_contiguous=True).then_inc(s_par, 16)
            pool.dma_start(swb[:], switch_b.unsqueeze(0).to_broadcast([P, EX])).then_inc(s_par, 16)
            pool.dma_start(sw_sb[:], switch_w).then_inc(s_par, 16)
            link(nc.gpsimd.memset(sel_rel[:], 0.0))
            link(nc.gpsimd.memset(sel_row[:], 0.0))
            nc.gpsimd.affine_select(out=sel_rel[:], in_=sel_rel[:], compare_op=ALU.not_equal, fill=WS,
                                    base=-(N - (NT - 1) * P), pattern=[[-1000, R], [1, P]], channel_multiplier=1000)
            nc.gpsimd.affine_select(out=sel_row[:, 0:NTY, :], in_=sel_row[:, 0:NTY, :], compare_op=ALU.not_equal,
                                    fill=WS, base=-R, pattern=[[-1, NTY], [0, P]], channel_multiplier=1)
            nc.gpsimd.affine_select(out=sel_row[:, NTY, :], in_=sel_row[:, NTY, :], compare_op=ALU.not_equal,
                                    fill=RS, base=-R - NTY, pattern=[[0, P]], channel_multiplier=1)
            nc.gpsimd.memset(attnT[:], 0.0)
            nc.gpsimd.memset(onesf[:], 1.0).then_inc(s_const, 1)
            nc.gpsimd.iota(iota_s[:], [[1, NP]], base=0, channel_multiplier=0, allow_small_or_imprecise_dtypes=True)
            nc.gpsimd.iota(iota_d[:], [[NP, R], [1, NP]], base=0, channel_multiplier=0,
                           allow_small_or_imprecise_dtypes=True).then_inc(s_const, 1)
            link(nc.gpsimd.memset(padk, NOKEY))
            pool.wait_ge(s_ekey, 1)
            pool.dma_start(key_dram[0, 0:NE].rearrange(flat, c=EC), ef[0:EP, 0, :]).then_inc(s_kst, 16)
            pool.dma_start(key_dram[1, 0:NE].rearrange(flat, c=EC), ef[0:EP, 3, :]).then_inc(s_kst, 16)
            for k in range(2):
                pool.dma_start(key_dram[k:k + 1, NE:EPAD], padk).then_inc(s_kst, 16)
            pool.wait_ge(s_kst, 64)
            for k in range(2):
                pool.dma_start(gkeys[:, k, :, :], key_dram[k].rearrange("(g p j) -> p g j", p=P, j=J))\
                    .then_inc(s_gk, 16)
            pool.wait_ge(s_lim, 1)
            with pool.Fori(0, NW) as w:
                start = pool.value_load(limi[0:1, bass.ds(w, 1)], min_val=0, max_val=NE)
                pool.dma_start(wkeys[:, bass.ds(w, 1), :, :].rearrange("p w k j -> p (w k) j"),
                               key_dram[:, bass.ds(start, GE)].rearrange("k (p j) -> p k j", j=J))\
                    .then_inc(s_wk, 16)
            nc.gpsimd.iota(iota_e[:], [[1, EX]], base=-EX, channel_multiplier=0,
                           allow_small_or_imprecise_dtypes=True)
            link(nc.gpsimd.memset(ones16[:], 1.0))
            nc.gpsimd.affine_select(out=tri16[:], in_=ones16[:], compare_op=ALU.is_gt, fill=0.0, base=0,
                                    pattern=[[1, P]], channel_multiplier=-1)
            nc.gpsimd.memset(zero, 0.0).then_inc(s_const, 1)
            pool.wait_ge(s_const, 5)
            for i in range(EX * CS // P):
                pool.dma_start(buf_dram[i * P:(i + 1) * P, :], zero).then_inc(s_zero, 16)
            mr.wait_emptied(pool, mr.first[("AGG",)] + NT - 1)
            nc.gpsimd.memset(buf_sb[:], 0.0).then_inc(s_const, 1)
            pool.wait_ge(s_zero, 16 * (EX * CS // P))
            pool.wait_ge(s_slot, 1)
            for t in range(NT):
                n = rows(t)
                pool.indirect_dma_start(buf_dram, bass.IndirectOffsetOnAxis(ap=slots[0:n, 0, t:t + 1].bitcast(U32), axis=0),
                                        xs[0:n, t, :], None, bounds_check=EX * CS - 1, oob_is_err=False)\
                    .then_inc(s_scat, 16)
            pool.wait_ge(s_scat, 16 * NT)
            pool.wait_ge(s_const, N_CONST)
            bv = buf_dram.rearrange("(i two c) d -> two c i d", two=2, c=CS)
            for h in range(2):
                pool.dma_start(buf_sb[h * HALF:h * HALF + CS, :, :], bv[h]).then_inc(s_buf, 16)
            for t in range(NT):
                n = rows(t)
                pool.indirect_dma_start(bias_tok[0:n, t, :], None, expert_b,
                                        bass.IndirectOffsetOnAxis(ap=slots[0:n, 2, t:t + 1].bitcast(U32), axis=0),
                                        bounds_check=EX - 1, oob_is_err=False).then_inc(s_bt, 16)
            for i in range(2):
                pool.wait_ge(s_yst[i], 16 * EX // 2)
            for t in range(NT):
                n = rows(t)
                pool.indirect_dma_start(gath[0:n, t, :], None, y_dram,
                                        bass.IndirectOffsetOnAxis(ap=slots[0:n, 1, t:t + 1].bitcast(U32), axis=0),
                                        bounds_check=EX * CS - 1, oob_is_err=False).then_inc(s_g, 16)

        @block.tensor
        def _(pe):
            def turn_weights(m):
                g, full = stage_of(m)
                pe.wait_ge(s_w[g], full)
                for kc in range(KC):
                    u = tr.first[("W", m)] + kc
                    tr.wait_free(pe, u)
                    for oc in range(KC):
                        last = nc.tensor.transpose(tbank[u % 3][:, oc, :], stage[g][:, oc, kc * P:(kc + 1) * P],
                                                   ident[:])
                    last.then_inc(tr.filled, 1)

            def turn_rows(key, i, rows_of):
                u = tr.first[key] + i
                tr.wait_free(pe, u)
                for kc in range(KC):
                    last = nc.tensor.transpose(tbank[u % 3][:, kc, :], rows_of[:, kc * P:(kc + 1) * P], ident[:])
                last.then_inc(tr.filled, 1)

            def split_product(bank, m, t):
                s, first = slot_of(m), True
                for kc in range(KC):
                    a, b = xhi[:, kc, t * P:(t + 1) * P], xlo[:, kc, t * P:(t + 1) * P]
                    for lhs, rhs in ((a, whi[s]), (a, wlo[s]), (b, whi[s])):
                        last = nc.tensor.matmul(bank, lhs, rhs[:, kc, :], start=first, stop=False,
                                                skip_group_check=True)
                        first = False
                bias = None
                if m[0] == "r" and t == NT - 1:
                    bias = sel_rel[:, int(m[1]), :]
                elif m[0] == "s":
                    bias = sel_row[:, int(m[1]), :]
                if bias is not None:
                    for part in (brow_hi, brow_lo):
                        last = nc.tensor.matmul(bank, bias, part[:], start=False, stop=False, skip_group_check=True)
                return last

            pe.wait_ge(s_const, 2)
            for task in TASKS:
                kind, m = task[0], task[-1]
                if kind == "W" and m in TURNED:
                    turn_weights(m)
                elif kind == "XT":
                    for t in range(NT):
                        pe.wait_ge(s_ln, t + 1)
                        turn_rows(task, t, xs[:, t, :])
                elif kind == "MM" and m[0] != "e":
                    if m == "k":
                        tr.wait_emptied(pe, tr.first[("XT",)] + NT - 1)
                    if m == "r0":
                        pe.wait_ge(s_blo, 1)
                        pe.wait_ge(s_const, 3)
                    wait_split(pe, m)
                    for t in range(NT):
                        u = mr.first[task] + t
                        mr.wait_free(pe, u)
                        split_product(mbank[u % 3][:], m, t).then_inc(mr.filled, 1)
                elif kind == "KV":
                    u = mr.first[task]
                    pe.wait_ge(s_const, 3)
                    mr.wait_free(pe, u)
                    mr.wait_emptied(pe, mr.first[("MM", "k")] + NT - 1)
                    mr.wait_emptied(pe, mr.first[("MM", "v")] + NT - 1)
                    for g in range(HP):
                        c = slice(g * P, (g + 1) * P)
                        for t in range(NT):
                            last = nc.tensor.matmul(mbank[u % 3][:, c], v_sb[:, t, c], k_sb[:, t, c],
                                                    start=(t == 0), stop=(t == NT - 1))
                    last.then_inc(mr.filled, 1)
                    mr.wait_free(pe, u + 1)
                    for t in range(NT):
                        last = nc.tensor.matmul(mbank[(u + 1) % 3][:], onesf[:], k_sb[:, t, :],
                                                start=(t == 0), stop=(t == NT - 1))
                    last.then_inc(mr.filled, 1)
                    pe.wait_ge(s_cnt, 1)
                    nc.tensor.matmul(abank[0][:, 0:NW], onesf[:], cnt[:], start=True, stop=True).then_inc(s_cntp, 1)
                elif kind == "QT":
                    for t in range(NT):
                        pe.wait_ge(s_qn, t + 1)
                        turn_rows(task, t, q_sb[:, t, :])
                elif kind == "P":
                    mr.wait_emptied(pe, mr.first[("KV",)])
                    tr.wait_emptied(pe, tr.first[("W", "p")] + KC - 1)
                    for g in range(HP):
                        u = mr.first[task] + g
                        mr.wait_free(pe, u)
                        nc.tensor.matmul(mbank[u % 3][:], attnT[:, g, :], projT[:, g, :], start=True,
                                         stop=True).then_inc(mr.filled, 1)
                elif kind == "Y":
                    mr.wait_emptied(pe, mr.first[("P",)] + HP - 1)
                    tr.wait_emptied(pe, tr.first[("QT",)] + NT - 1)
                    for t in range(NT):
                        u = mr.first[task] + t
                        mr.wait_free(pe, u)
                        for g in range(HP):
                            nc.tensor.matmul(mbank[u % 3][:], qnT[:, g, t * P:(t + 1) * P], Pm[:, g, :],
                                             start=(g == 0), stop=False, skip_group_check=True)
                        for part in (brow_hi, brow_lo):
                            last = nc.tensor.matmul(mbank[u % 3][:], sel_row[:, NTY, :], part[:],
                                                    start=False, stop=False, skip_group_check=True)
                        last.then_inc(mr.filled, 1)
                elif kind == "AB":
                    def window_group(b, first):
                        for st in range(NT):
                            for j in range(J):
                                last = nc.tensor.matmul(
                                    bank_of[0][:, st * R * WIN:(st + 1) * R * WIN],
                                    onehot_s[:, b, j, st * P:(st + 1) * P],
                                    onehot_d[:, b, j, :, :].rearrange("p r d -> p (r d)"),
                                    start=(first and st == 0 and j == 0), stop=False, skip_group_check=True)
                        return last

                    bank_of = [None]
                    pe.wait_ge(s_lim, 1)
                    ordered = pe.value_load(limi[0:1, NW:NW + 1], min_val=0, max_val=1)
                    with pe.If(ordered > 0):
                        with pe.Fori(0, NW // 2) as pair:
                            for b in range(2):
                                bank_of[0] = abank[b]
                                pe.wait_ge(s_abf, pair * 2 + b + 1)
                                pe.wait_ge(s_oh, pair * 2 + b + 1)
                                window_group(b, True).then_inc(s_ohf, 1)
                    with pe.Else():
                        with pe.Fori(0, NW // 2) as pair:
                            for b in range(2):
                                bank_of[0] = abank[b]
                                pe.wait_ge(s_abf, pair * 2 + b + 1)
                                for o in range(2):
                                    pe.wait_ge(s_oh, (pair * 2 + b) * NG + o + 1)
                                    window_group(o, o == 0).then_inc(s_ohf, 1)
                                with pe.Fori(1, NG // 2) as gp:
                                    for o in range(2):
                                        pe.wait_ge(s_oh, (pair * 2 + b) * NG + gp * 2 + o + 1)
                                        window_group(o, False).then_inc(s_ohf, 1)
                elif kind == "SW":
                    u = tr.first[task]
                    tr.wait_free(pe, u)
                    pe.wait_ge(s_par, 9 * 16)
                    for kc in range(KC):
                        last = nc.tensor.transpose(tbank[u % 3][:, 0, kc * EX:(kc + 1) * EX],
                                                   sw_sb[:, kc * P:(kc + 1) * P], ident[0:EX, 0:EX])
                    last.then_inc(tr.filled, 1)
                elif kind == "AGG":
                    def logits(t):
                        pe.wait_ge(s_ln, NT + t + 1)
                        turn_rows(task, t, xs[:, t, :])
                        tr.wait_emptied(pe, tr.first[task] + t)
                        for kc in range(KC):
                            last = nc.tensor.matmul(abank[0][:, t * EX:(t + 1) * EX], xfT[:, t % 2, kc, :],
                                                    swT[:, kc, :], start=(kc == 0), stop=(kc == KC - 1))
                        last.then_inc(s_lgp, 1)

                    mr.wait_emptied(pe, mr.first[("MM", f"r{R - 1}")] + NT - 1)
                    pe.wait_ge(s_abf, NW + 2)
                    for t in range(NT):
                        u = mr.first[task] + t
                        mr.wait_free(pe, u)
                        for i in range(R * NT):
                            for part in range(2):
                                last = nc.tensor.matmul(mbank[u % 3][:], at_sb[:, i, t * P:(t + 1) * P],
                                                        xr[:, part, i, :], start=(i == 0 and part == 0),
                                                        stop=(i == R * NT - 1 and part == 1))
                        last.then_inc(mr.filled, 1)
                        if t > 0:
                            logits(t - 1)
                    logits(NT - 1)
                elif kind == "CUM":
                    pe.wait_ge(s_oh16, 1)
                    for t in range(NT):
                        for o in range(t + 1):
                            last = nc.tensor.matmul(abank[1][:, t * EX:(t + 1) * EX],
                                                    tri16[:] if o == t else ones16[:], oh16[:, o, :],
                                                    start=(o == 0), stop=(o == t))
                    last.then_inc(s_cum, 1)
                elif kind == "BT":
                    pe.wait_ge(s_buf, 32)
                    for i in range(NBT):
                        turn_rows(task, i, buf_sb[:, i, :])
                elif kind == "MM":
                    e, s, u = int(m[1:]), slot_of(m), mr.first[task]
                    if e == 0:
                        tr.wait_emptied(pe, tr.first[("BT",)] + NBT - 1)
                    wait_split(pe, m)
                    mr.wait_free(pe, u)
                    for kc in range(KC):
                        for w in (whi[s], wlo[s]):
                            last = nc.tensor.matmul(mbank[u % 3][:], bT[:, kc, e, :], w[:, kc, :],
                                                    start=(kc == 0 and w is whi[s]),
                                                    stop=(kc == KC - 1 and w is wlo[s]))
                    last.then_inc(mr.filled, 1)

        @block.scalar
        def _(act):
            def empties_turn(u):
                act.wait_ge(tr.filled, u + 1)

            def empties_prod(u):
                act.wait_ge(mr.filled, u + 1)

            act.wait_ge(s_mv, 1)
            nc.scalar.activation(sd[:, 1, :], sd[:, 0, :], ACT.Sqrt).then_inc(s_sd, 1)
            for task in TASKS:
                kind, m = task[0], task[-1]
                if kind == "W" and m in TURNED:
                    if m != "p":
                        wait_slot(act, m)
                    for kc in range(KC):
                        u = tr.first[task] + kc
                        empties_turn(u)
                        if m == "p":
                            nc.scalar.activation(projT[:, kc, :], tbank[u % 3][:].rearrange("p k n -> p (k n)"),
                                                 ACT.Copy).then_inc(tr.act, 1)
                        else:
                            nc.scalar.activation(whi[slot_of(m)][:, kc, :],
                                                 tbank[u % 3][:].rearrange("p k n -> p (k n)"),
                                                 ACT.Copy, scale=WS).then_inc(tr.act, 1)
                elif kind == "W":
                    g, full = stage_of(m)
                    wait_slot(act, m)
                    act.wait_ge(s_w[g], full)
                    nc.scalar.activation(whi[slot_of(m)][:], stage[g][:], ACT.Copy, scale=WS).then_inc(s_dhi, 1)
                elif kind == "XT":
                    for t in range(NT):
                        u = tr.first[task] + t
                        empties_turn(u)
                        nc.scalar.activation(xhi[:, :, t * P:(t + 1) * P], tbank[u % 3][:], ACT.Copy)\
                            .then_inc(tr.act, 1)
                    act.wait_ge(s_par, 9 * 16)
                    nc.scalar.activation(brow_hi[:], brow[:], ACT.Copy, scale=WS).then_inc(s_bhi, 1)
                elif kind == "QT":
                    for t in range(NT):
                        u = tr.first[task] + t
                        empties_turn(u)
                        nc.scalar.activation(qnT[:, :, t * P:(t + 1) * P], tbank[u % 3][:], ACT.Copy)\
                            .then_inc(tr.act, 1)
                elif kind == "MM" and m in ("k", "q"):
                    for t in range(NT):
                        u = mr.first[task] + t
                        empties_prod(u)
                        nc.scalar.activation((k_sb if m == "k" else q_sb)[:, t, :], mbank[u % 3][:], ACT.Relu,
                                             scale=RS * RS).then_inc(mr.act, 1)
                elif kind == "MM" and m[0] == "r":
                    for t in range(NT):
                        u = mr.first[task] + t
                        empties_prod(u)
                        nc.scalar.activation(xr[:, 0, int(m[1]) * NT + t, :], mbank[u % 3][:], ACT.Copy,
                                             scale=RS).then_inc(mr.act, 1)
                elif kind == "KV":
                    u = mr.first[task] + 1
                    empties_prod(u)
                    nc.scalar.activation(ksumB, mbank[u % 3][:], ACT.Copy).then_inc(mr.act, 1)
                elif kind == "P":
                    for g in range(HP):
                        u = mr.first[task] + g
                        empties_prod(u)
                        nc.scalar.activation(Pm[:, g, :], mbank[u % 3][:], ACT.Copy).then_inc(mr.act, 1)
                elif kind == "AB":
                    act.sem_inc(s_abf, 2)
                    act.wait_ge(s_zero, 16 * (EX * CS // P))
                    act.wait_ge(s_kst, 64)
                    counts = at_sb[:].rearrange("p (r s) n -> p s r n", s=NT)

                    def empty_window(w, b):
                        v = abank[b][:, 0:NT * R * WIN].rearrange("p (s r d) -> p s r d", s=NT, r=R)
                        nc.scalar.activation(counts[:, :, :, bass.ds(w * WIN, WIN)], v, ACT.Copy)\
                            .then_inc(s_abf, 1)

                    act.wait_ge(s_lim, 1)
                    ordered = act.value_load(limi[0:1, NW:NW + 1], min_val=0, max_val=1)
                    with act.If(ordered > 0):
                        with act.Fori(0, NW // 2) as pair:
                            for b in range(2):
                                act.wait_ge(s_ohf, pair * 2 + b + 1 + 2)
                                empty_window(pair * 2 + b, b)
                    with act.Else():
                        with act.Fori(0, NW // 2) as pair:
                            for b in range(2):
                                act.wait_ge(s_ohf, (pair * 2 + b + 1) * NG + 2)
                                empty_window(pair * 2 + b, b)
                elif kind == "SW":
                    u = tr.first[task]
                    empties_turn(u)
                    nc.scalar.activation(swT[:].rearrange("p k e -> p (k e)"), tbank[u % 3][:, 0, 0:KC * EX],
                                         ACT.Copy).then_inc(tr.act, 1)
                elif kind == "AGG":
                    def turned(t):
                        u = tr.first[task] + t
                        empties_turn(u)
                        if t >= 2:
                            act.wait_ge(s_lgp, t - 1)
                        nc.scalar.activation(xfT[:, t % 2, :, :], tbank[u % 3][:], ACT.Copy).then_inc(tr.act, 1)

                    for t in range(NT):
                        act.wait_ge(s_mv, t + 2)
                        nc.scalar.activation(sd[:, 1, t:t + 1], sd[:, 0, t:t + 1], ACT.Sqrt).then_inc(s_sd, 1)
                        if t > 0:
                            turned(t - 1)
                    turned(NT - 1)
                elif kind == "ROUTE":
                    act.wait_ge(s_exd, 1)
                    nc.scalar.activation(lg[:, 3, :, :], lg[:, 2, :, :], ACT.Exp).then_inc(s_exp, 1)
                elif kind == "BT":
                    mr.wait_emptied(act, mr.first[("AGG",)] + NT - 1)
                    for i in range(NBT):
                        u = tr.first[task] + i
                        empties_turn(u)
                        nc.scalar.activation(bT[:, :, 2 * i:2 * i + 2, 0:HALF],
                                             tbank[u % 3][:].rearrange("p k (e c) -> p k e c", e=2),
                                             ACT.Copy, scale=WS).then_inc(tr.act, 1)
                elif kind == "MM" and m[0] == "e":
                    e, u = int(m[1:]), mr.first[task]
                    if e >= 2:
                        mr.wait_emptied(act, u - 2)
                    empties_prod(u)
                    nc.scalar.activation(ylow[0:CS, e % 2, :], mbank[u % 3][HALF:HALF + CS, :], ACT.Copy,
                                         scale=RS * RS).then_inc(mr.act, 1)
                    if e >= 1:
                        store_expert(act, e - 1)
            store_expert(act, EX - 1)

        @block.vector
        def _(dve):
            steps = [0]

            def link(ins):
                steps[0] += 1
                ins.then_inc(s_step, 1)
                dve.wait_ge(s_step, steps[0])

            V = nc.vector

            def deviation(c, n):
                link(V.reciprocal(sd[:, 2, c:c + n], sd[:, 1, c:c + n]))
                link(V.tensor_tensor(sd[:, 2, c:c + n], sd[:, 2, c:c + n], sd[:, 0, c:c + n], ALU.mult))
                link(V.tensor_tensor(sd[:, 2, c:c + n], sd[:, 2, c:c + n], sd[:, 1, c:c + n], ALU.add))
                link(V.reciprocal(sd[:, 3, c:c + n], sd[:, 2, c:c + n]))

            def turned_low(u, low, high, scale):
                dve.wait_ge(tr.act, tr.act_count(u))
                V.scalar_tensor_tensor(out=low, in0=tbank[u % 3][:], scalar=scale, in1=high, op0=ALU.mult,
                                       op1=ALU.subtract).then_inc(tr.dve, 1)

            def kcn(ap):
                return ap.rearrange("p (k n) -> p k n", k=KC)

            for t in range(NT):
                dve.wait_ge(s_x[t], 16)
                link(V.bn_stats(stats[:, t, :], x_sb[:, t, :]))
                V.bn_aggr(mv[:, t, :], stats[:, t, :]).then_inc(s_step, 1)
                steps[0] += 1
            dve.wait_ge(s_step, steps[0])
            V.tensor_scalar(sd[:, 0, :], mv[:, :, 1], EPS, None, ALU.add).then_inc(s_mv, 1)
            dve.wait_ge(s_sd, 1)
            deviation(0, NT)
            link(V.tensor_scalar(sd[:, 3, :], sd[:, 3, :], 2.0 * WS, None, ALU.mult))
            for t in range(NT):
                V.tensor_scalar(xs[:, t, :], x_sb[:, t, :], mv[:, t, 0:1], sd[:, 3, t:t + 1], ALU.subtract,
                                ALU.mult).then_inc(s_ln, 1)

            def edge_keys():
                link(V.memset(cnt[:], 0.0))
                dve.wait_ge(s_edge, 5 * 16)
                V.tensor_copy(ef[0:EP, 0, :], edges[0:EP, 0, :])
                V.tensor_copy(ef[0:EP, 1, :], edges[0:EP, 1, :])
                V.tensor_copy(ef[0:EP, 2, :], edges[0:EP, 2, :])
                link(V.tensor_copy(cmp[0:EP, 0, :], edges[0:EP, 3, :]))
                V.scalar_tensor_tensor(out=ef[0:EP, 3, :], in0=cmp[0:EP, 0, :], scalar=float(NP),
                                       in1=ef[0:EP, 1, :], op0=ALU.mult, op1=ALU.add).then_inc(s_ekey, 1)
                for w in range(NW - 1):
                    link(V.tensor_scalar(cmp[0:EP, 1, :], ef[0:EP, 1, :], float(WIN * (w + 1)), 0.0, ALU.is_lt,
                                         ALU.add, accum_out=cnt[0:EP, w:w + 1]))
                dve.wait_ge(s_ekey, 1)
                link(V.tensor_tensor(cmp[0:EP, 0, :], ef[0:EP, 1, :], ef[0:EP, 2, :], ALU.is_gt))
                V.tensor_reduce(cnt[0:EP, NW - 1:NW], cmp[0:EP, 0, :], AX.X, ALU.add).then_inc(s_cnt, 1)

            def edge_limits():
                link(V.memset(lim[:], 0.0))
                dve.wait_ge(s_cntp, 1)
                link(V.tensor_copy(lim[:, 1:NW], abank[0][0:1, 0:NW - 1]))
                link(V.memset(lim[:, NW:NW + 1], float(NE)))
                link(V.tensor_tensor(num[:], lim[:, 1:NW + 1], lim[:, 0:NW], ALU.subtract))
                link(V.tensor_reduce(lim[:, NW + 1:NW + 2], num[:], AX.X, ALU.max))
                link(V.tensor_scalar(lim[:, NW + 2:NW + 3], lim[:, NW + 1:NW + 2], float(GE), None, ALU.is_le))
                link(V.tensor_scalar(lim[:, NW + 3:NW + 4], abank[0][0:1, NW - 1:NW], 0.0, None, ALU.is_equal))
                link(V.tensor_tensor(lim[:, NW:NW + 1], lim[:, NW + 2:NW + 3], lim[:, NW + 3:NW + 4], ALU.mult))
                V.tensor_copy(limi[:], lim[:, 0:NW + 1]).then_inc(s_lim, 1)

            for task in TASKS:
                kind, m = task[0], task[-1]
                if kind == "W" and m in TURNED and m != "p":
                    for kc in range(KC):
                        s = slot_of(m)
                        turned_low(tr.first[task] + kc, kcn(wlo[s][:, kc, :]), kcn(whi[s][:, kc, :]), WS)
                elif kind == "W" and m != "p":
                    s, (g, _) = slot_of(m), stage_of(m)
                    dve.wait_ge(s_dhi, DIRECT.index(m) + 1)
                    V.scalar_tensor_tensor(out=wlo[s][:], in0=stage[g][:], scalar=WS, in1=whi[s][:],
                                           op0=ALU.mult, op1=ALU.subtract).then_inc(s_dlo, 1)
                elif kind == "XT":
                    for t in range(NT):
                        c = slice(t * P, (t + 1) * P)
                        turned_low(tr.first[task] + t, xlo[:, :, c], xhi[:, :, c], 1.0)
                    dve.wait_ge(s_bhi, 1)
                    V.scalar_tensor_tensor(out=brow_lo[:], in0=brow[:], scalar=WS, in1=brow_hi[:], op0=ALU.mult,
                                           op1=ALU.subtract).then_inc(s_blo, 1)
                    link(V.tensor_copy(rt[:, 0, :], nt_i[:]))
                    for r in range(NTY):
                        V.tensor_scalar(nmask[:, r, :], rt[:, 0, :], float(r), RS * RS, ALU.is_equal, ALU.mult)\
                            .then_inc(s_step, 1)
                        steps[0] += 1
                    dve.wait_ge(s_step, steps[0])
                    edge_keys()
                elif kind == "MM" and m == "v":
                    for t in range(NT):
                        u = mr.first[task] + t
                        dve.wait_ge(mr.filled, u + 1)
                        V.tensor_scalar(v_sb[:, t, :], mbank[u % 3][:], RS * RS, None, ALU.mult).then_inc(mr.dve, 1)
                elif kind == "MM" and m[0] == "r":
                    for t in range(NT):
                        u, i = mr.first[task] + t, int(m[1]) * NT + t
                        dve.wait_ge(mr.act, mr.act_count(u))
                        V.scalar_tensor_tensor(out=xr[:, 1, i, :], in0=mbank[u % 3][:], scalar=RS,
                                               in1=xr[:, 0, i, :], op0=ALU.mult, op1=ALU.subtract)\
                            .then_inc(mr.dve, 1)
                elif kind == "MM" and m[0] == "s":
                    r = int(m[1])
                    for t in range(NT):
                        u = mr.first[task] + t
                        dve.wait_ge(mr.filled, u + 1)
                        if r == 0:
                            V.tensor_scalar(xs[:, t, :], mbank[u % 3][:], nmask[:, r, t:t + 1], None, ALU.mult)\
                                .then_inc(mr.dve, 1)
                        else:
                            mr.wait_emptied(dve, mr.first[("MM", f"s{r - 1}")] + t)
                            V.scalar_tensor_tensor(out=xs[:, t, :], in0=mbank[u % 3][:],
                                                   scalar=nmask[:, r, t:t + 1], in1=xs[:, t, :], op0=ALU.mult,
                                                   op1=ALU.add).then_inc(mr.dve, 1)
                elif kind == "KV":
                    dve.wait_ge(s_const, 3)
                    u = mr.first[task]
                    dve.wait_ge(mr.filled, u + 1)
                    for h in range(2):
                        c = slice(h * DH, (h + 1) * DH)
                        last = V.tensor_tensor(attnT[c, :, c], kcn(mbank[u % 3][:])[c, :, c],
                                               temp[c, :].unsqueeze(2).to_broadcast([DH, HP, DH]), ALU.mult)
                    last.then_inc(mr.dve, 1)
                    edge_limits()
                elif kind == "QN":
                    dve.wait_ge(mr.act, mr.act_count(mr.first[("KV",)] + 1))
                    dve.wait_ge(mr.act, mr.act_count(mr.first[("MM", "q")] + NT - 1))
                    for t in range(NT):
                        link(V.tensor_tensor(prod[:, t % 2, :], q_sb[:, t, :], ksumB, ALU.mult))
                        link(V.tensor_reduce(den[:, 0, t, :], prod[:, t % 2, :].rearrange("p (h d) -> p h d", h=H),
                                             AX.X, ALU.add))
                    link(V.tensor_scalar(den[:, 0, :, :], den[:, 0, :, :], 100.0, None, ALU.max))
                    link(V.reciprocal(den[:, 1, :, :], den[:, 0, :, :]))
                    for t in range(NT):
                        qv = q_sb[:, t, :].rearrange("p (h d) -> p h d", h=H)
                        V.tensor_tensor(qv, qv, den[:, 1, t, :].unsqueeze(2).to_broadcast([P, H, DH]), ALU.mult)\
                            .then_inc(s_qn, 1)
                elif kind == "Y":
                    for t in range(NT):
                        u = mr.first[task] + t
                        dve.wait_ge(mr.filled, u + 1)
                        V.tensor_tensor(x_sb[:, t, :], mbank[u % 3][:], x_sb[:, t, :], ALU.add).then_inc(mr.dve, 1)
                elif kind == "AB":
                    link(V.memset(onehot_s[:, :, :, N:N + 1], 1.0))
                    V.memset(onehot_s[:, :, :, N + 1:NP], 0.0).then_inc(s_ohf, 2)

                    def onehots(b, w, keys_s, keys_d):
                        V.tensor_tensor(onehot_d[:, b], iota_d[:, :, bass.ds(w * WIN, WIN)].unsqueeze(1)
                                        .to_broadcast([P, J, R, WIN]),
                                        keys_d.unsqueeze(3).to_broadcast([P, J, R, WIN]), ALU.is_equal)
                        for j in range(J):
                            last = V.tensor_scalar(onehot_s[:, b, j, 0:N], iota_s[:, 0:N], keys_s[:, :, j], None,
                                                   ALU.is_equal)
                        last.then_inc(s_oh, 1)

                    dve.wait_ge(s_const, 4)
                    dve.wait_ge(s_wk, 16 * NW)
                    dve.wait_ge(s_gk, 32)
                    ordered = dve.value_load(limi[0:1, NW:NW + 1], min_val=0, max_val=1)
                    with dve.If(ordered > 0):
                        with dve.Fori(0, NW // 2) as pair:
                            for b in range(2):
                                dve.wait_ge(s_ohf, pair * 2 + b + 1)
                                kw = wkeys[:, bass.ds(pair * 2 + b, 1), :, :]
                                onehots(b, pair * 2 + b, kw[:, :, 0, :], kw[:, :, 1, :].rearrange("p w j -> p j w"))
                    with dve.Else():
                        with dve.Fori(0, NW) as w:
                            with dve.Fori(0, NG // 2) as gp:
                                for o in range(2):
                                    dve.wait_ge(s_ohf, w * NG + gp * 2 + o + 1)
                                    kg = gkeys[:, :, bass.ds(gp * 2 + o, 1), :]
                                    onehots(o, w, kg[:, 0], kg[:, 1].rearrange("p w j -> p j w"))
                elif kind == "AGG":
                    for t in range(NT):
                        u = mr.first[task] + t
                        dve.wait_ge(mr.filled, u + 1)
                        mr.wait_emptied(dve, mr.first[("MM", f"s{NTY - 1}")] + t)
                        V.scalar_tensor_tensor(out=xs[:, t, :], in0=mbank[u % 3][:], scalar=RS, in1=xs[:, t, :],
                                               op0=ALU.mult, op1=ALU.add).then_inc(mr.dve, 1)
                        mr.wait_emptied(dve, u)
                        link(V.scalar_tensor_tensor(out=x_sb[:, t, :], in0=xs[:, t, :], scalar=0.0,
                                                    in1=x_sb[:, t, :], op0=ALU.max, op1=ALU.add))
                        link(V.bn_stats(stats[:, t, :], x_sb[:, t, :]))
                        link(V.bn_aggr(mv[:, t, :], stats[:, t, :]))
                        V.tensor_scalar(sd[:, 0, t:t + 1], mv[:, t, 1:2], EPS, None, ALU.add).then_inc(s_mv, 1)
                        dve.wait_ge(s_sd, t + 2)
                        deviation(t, 1)
                        link(V.tensor_scalar(sd[:, 3, t:t + 1], sd[:, 3, t:t + 1], 2.0, None, ALU.mult))
                        V.tensor_scalar(xs[:, t, :], x_sb[:, t, :], mv[:, t, 0:1], sd[:, 3, t:t + 1],
                                        ALU.subtract, ALU.mult).then_inc(s_ln, 1)
                elif kind == "CUM":
                    dve.wait_ge(s_lgp, NT)
                    link(V.tensor_tensor(lg[:, 0, :, :],
                                         abank[0][:, 0:NT * EX].rearrange("p (t e) -> p t e", t=NT),
                                         swb[:].unsqueeze(1).to_broadcast([P, NT, EX]), ALU.add))
                    link(V.tensor_reduce(rt[:, 1, :], lg[:, 0, :, :], AX.X, ALU.max))
                    top = rt[:, 1, :].unsqueeze(2).to_broadcast([P, NT, EX])
                    V.tensor_tensor(lg[:, 2, :, :], lg[:, 0, :, :], top, ALU.subtract).then_inc(s_exd, 1)
                    link(V.tensor_tensor(lg[:, 1, :, :], lg[:, 0, :, :], top, ALU.is_equal))
                    ie = iota_e[:].unsqueeze(1).to_broadcast([P, NT, EX])
                    link(V.tensor_tensor(lg[:, 1, :, :], lg[:, 1, :, :], ie, ALU.mult))
                    link(V.tensor_reduce(rt[:, 2, :], lg[:, 1, :, :], AX.X, ALU.min))
                    V.tensor_tensor(oh16[:], ie, rt[:, 2, :].unsqueeze(2).to_broadcast([P, NT, EX]),
                                    ALU.is_equal).then_inc(s_oh16, 1)
                elif kind == "ROUTE":
                    dve.wait_ge(s_cum, 1)
                    dve.wait_ge(s_oh16, 1)
                    link(V.tensor_tensor(lg[:, 1, :, :], oh16[:],
                                         abank[1][:, 0:NT * EX].rearrange("p (t e) -> p t e", t=NT), ALU.mult))
                    link(V.tensor_reduce(rt[:, 3, :], lg[:, 1, :, :], AX.X, ALU.add))
                    link(V.tensor_scalar(rt[:, 4, :], rt[:, 3, :], float(CAP), None, ALU.is_lt))
                    link(V.tensor_scalar(rt[:, 5, :], rt[:, 2, :], float(EX), None, ALU.add))
                    link(V.tensor_scalar(rt[:, 6, :], rt[:, 3, :], float(CAP - 1), None, ALU.min))
                    link(V.scalar_tensor_tensor(out=rt[:, 7, :], in0=rt[:, 5, :], scalar=float(CS),
                                                in1=rt[:, 6, :], op0=ALU.mult, op1=ALU.add))
                    link(V.tensor_scalar(rt[:, 8, :], rt[:, 4, :], -OOB, OOB, ALU.mult, ALU.add))
                    link(V.tensor_tensor(rt[:, 9, :], rt[:, 8, :], rt[:, 7, :], ALU.add))
                    V.tensor_copy(slots[:, 1, :], rt[:, 7, :])
                    V.tensor_copy(slots[:, 2, :], rt[:, 5, :])
                    V.tensor_copy(slots[:, 0, :], rt[:, 9, :]).then_inc(s_slot, 1)
                    dve.wait_ge(s_exp, 1)
                    link(V.tensor_reduce(rt[:, 10, :], lg[:, 3, :, :], AX.X, ALU.add))
                    link(V.reciprocal(rt[:, 11, :], rt[:, 10, :]))
                    link(V.tensor_tensor(rt[:, 0, :], rt[:, 11, :], rt[:, 4, :], ALU.mult))
                    link(V.tensor_tensor(rt[:, 1, :], rt[:, 11, :], rt[:, 0, :], ALU.subtract))
                    for t in range(NT):
                        link(V.scalar_tensor_tensor(out=x_sb[:, t, :], in0=xs[:, t, :], scalar=rt[:, 1, t:t + 1],
                                                    in1=x_sb[:, t, :], op0=ALU.mult, op1=ALU.add))
                elif kind == "BT":
                    for i in range(NBT):
                        u = tr.first[task] + i
                        dve.wait_ge(tr.act, tr.act_count(u))
                        for h in range(2):
                            last = V.scalar_tensor_tensor(
                                out=bT[:, :, 2 * i + h, HALF:P], in0=tbank[u % 3][:, :, h * HALF:(h + 1) * HALF],
                                scalar=WS, in1=bT[:, :, 2 * i + h, 0:HALF], op0=ALU.mult, op1=ALU.subtract)
                        last.then_inc(tr.dve, 1)
                elif kind == "MM" and m[0] == "e":
                    e, u = int(m[1:]), mr.first[task]
                    if e >= 2:
                        dve.wait_ge(s_yst[e % 2], 16 * (e // 2))
                    dve.wait_ge(mr.act, mr.act_count(u))
                    V.scalar_tensor_tensor(out=yexp[0:CS, e % 2, :], in0=mbank[u % 3][0:CS, :], scalar=RS * RS,
                                           in1=ylow[0:CS, e % 2, :], op0=ALU.mult, op1=ALU.add)\
                        .then_inc(mr.dve, 1)
            dve.wait_ge(s_bt, 16 * NT)
            for t in range(NT):
                n = rows(t)
                link(V.scalar_tensor_tensor(out=x_sb[0:n, t, :], in0=bias_tok[0:n, t, :], scalar=rt[0:n, 0, t:t + 1],
                                            in1=x_sb[0:n, t, :], op0=ALU.mult, op1=ALU.add))
            dve.wait_ge(s_g, 16 * NT)
            for t in range(NT):
                n = rows(t)
                V.scalar_tensor_tensor(out=gath[0:n, t, :], in0=gath[0:n, t, :], scalar=rt[0:n, 0, t:t + 1],
                                       in1=x_sb[0:n, t, :], op0=ALU.mult, op1=ALU.add).then_inc(s_fin, 1)


_INS = ['x', 'src', 'dst', 'edge_type_3', 'node_type_3', 'L0_gnn_W_rel', 'L0_gnn_b_rel', 'L0_gnn_W_self',
        'L0_gnn_b_self', 'L0_mix_Wqkv', 'L0_mix_temperature', 'L0_mix_Wproj', 'L0_mix_bproj', 'L0_ffn_switch_w',
        'L0_ffn_switch_b', 'L0_ffn_expert_w', 'L0_ffn_expert_b']


def kernel(**inputs):
    import numpy as _np
    import concourse.bacc as _bacc
    from concourse import mybir as _mybir
    from concourse.bass_utils import run_bass_kernel_spmd as _run

    nc = _bacc.Bacc("TRN2", target_bir_lowering=False, num_devices=1)
    arrays, args = {}, []
    for name in _INS:
        a = _np.ascontiguousarray(inputs[name])
        arrays[f"in_{name}_dram"] = a
        args.append(nc.dram_tensor(f"in_{name}_dram", a.shape, _mybir.dt.from_np(a.dtype), kind="ExternalInput").ap())
    shape = inputs['x'].shape
    args.append(nc.dram_tensor("out_0_dram", shape, _mybir.dt.float32, kind="ExternalOutput").ap())
    gps_layer_kernel(nc, *args)
    r = _run(nc, [arrays], core_ids=[0])
    return r.results[0]["out_0_dram"]
```

```python
import concourse.bass as bass
from concourse import mybir
from contextlib import ExitStack


def gps_layer_kernel(
    nc: bass.Bass,
    x: bass.AP,
    src: bass.AP,
    dst: bass.AP,
    edge_type: bass.AP,
    node_type: bass.AP,
    W_rel: bass.AP,
    b_rel: bass.AP,
    W_self: bass.AP,
    b_self: bass.AP,
    Wqkv: bass.AP,
    temperature: bass.AP,
    Wproj: bass.AP,
    bproj: bass.AP,
    switch_w: bass.AP,
    switch_b: bass.AP,
    expert_w: bass.AP,
    expert_b: bass.AP,
    out: bass.AP,
):
    F32, F16, I32, U32 = mybir.dt.float32, mybir.dt.float16, mybir.dt.int32, mybir.dt.uint32
    ALU = mybir.AluOpType
    ACT = mybir.ActivationFunctionType
    AX = mybir.AxisListType

    P = 128
    N, D = x.shape
    NE = src.shape[0]
    R = W_rel.shape[0]
    NTY = W_self.shape[0]
    H = temperature.shape[0]
    DH = D // H
    EX = switch_w.shape[0]
    CAP = int(1.2 * N / EX)
    NT = (N + P - 1) // P
    TAIL = N - (NT - 1) * P
    NP = NT * P
    KC = D // P
    HP = D // P
    EPS = 1e-5
    WS = 256.0
    RS = 1.0 / WS

    WIN = 32
    NW = NP // WIN
    WT = NW // NT
    J = 5
    GE = J * P
    NG = -(-NE // GE)
    NG += NG % 2
    EPAD = NG * GE
    EC = 85
    EP = NE // EC
    assert EP * EC == NE and EP <= P and NE + GE <= EPAD
    NOKEY = 5000.0

    CS = 48
    HALF = 64
    NBT = EX // 2
    EH = EX // 2
    assert CAP <= CS and EH * CS <= D
    OOB = 100000

    ctx = ExitStack()
    with ctx:
        def sb(name, shape, dt):
            return ctx.enter_context(nc.sbuf_tensor(name, shape, dt))

        def sem(name):
            return ctx.enter_context(nc.semaphore(name))

        NSTAGE, NSPLIT = 3, 4
        x_sb = sb("x_sb", [P, NT, D], F32)
        xs = sb("xs", [P, NT, D], F32)
        xhi = sb("xhi", [P, KC, NP], F16)
        xlo = sb("xlo", [P, KC, NP], F16)
        stage = [sb(f"stage{i}", [P, KC, D], F32) for i in range(NSTAGE)]
        whi = [sb(f"whi{i}", [P, KC, D], F16) for i in range(NSPLIT)]
        wlo = [sb(f"wlo{i}", [P, KC, D], F16) for i in range(NSPLIT)]
        early = sb("early", [P, 12288], F32)
        k_sb = early[:, 0:2560].rearrange("p (t d) -> p t d", t=NT)
        v_sb = early[:, 2560:5120].rearrange("p (t d) -> p t d", t=NT)
        q_sb = early[:, 5120:7680].rearrange("p (t d) -> p t d", t=NT)
        qnT = early[:, 7680:10240].rearrange("p (g n) -> p g n", g=HP)
        projT = early[:, 10240:12288].rearrange("p (g n) -> p g n", g=HP)
        onehot_s = early[:, 0:3200].bitcast(F16).rearrange("p (b j n) -> p b j n", b=2, j=J)
        onehot_d = early[:, 3200:3680].bitcast(F16).rearrange("p (b j r d) -> p b j r d", b=2, j=J, r=R)
        slot_of = early[:, 0:NT * EX * CS // 2].bitcast(F16).rearrange("p (t s) -> p t s", t=NT)
        xf = early[:, 2560:5120].bitcast(F16).rearrange("p (h t d) -> p h t d", h=2, t=NT)
        xfT = early[:, 5120:6144].rearrange("p (b k n) -> p b k n", b=2, k=KC)
        ylow = early[:, 6144:7168].rearrange("p (b d) -> p b d", b=2)
        yexp = early[:, 7168:8192].rearrange("p (b d) -> p b d", b=2)
        prod = xs[:, 0:2, :]
        Pm = xs[:, 0:HP, :]
        xr = sb("xr", [P, 2, R * NT, D], F16)
        bias_tok = xr[:].rearrange("p h t d -> p (h t d)")[:, 0:NT * D * 2].bitcast(F32)\
            .rearrange("p (t d) -> p t d", t=NT)
        at_sb = sb("at_sb", [P, R * NT, NP], F16)
        bT = at_sb[:].rearrange("p t n -> p (t n)")[:, 0:KC * EX * P]\
            .rearrange("p (k e c) -> p k e c", k=KC, e=EX)
        attnT = sb("attnT", [P, HP, P], F32)
        ksumB = xs[:, NT - 1, :]
        k_sum = xs[:, NT - 2, :]
        pre = at_sb[:].rearrange("p t n -> p (t n)").bitcast(F32)
        edges = pre[:, 0:4 * EC].bitcast(I32).rearrange("p (a c) -> p a c", a=4)
        ef = pre[:, 4 * EC:8 * EC].rearrange("p (a c) -> p a c", a=4)
        cmp = pre[:, 8 * EC:10 * EC].rearrange("p (a c) -> p a c", a=2)
        padk = pre[0:1, 10 * EC:10 * EC + EPAD - NE]
        ident = sb("ident", [P, P], F32)
        onesf = sb("onesf", [P, P], F32)
        ones16 = sb("ones16", [P, P], F16)
        tri16 = sb("tri16", [P, P], F16)
        iota_s = sb("iota_s", [P, EX * CS], F16)
        iota_d = sb("iota_d", [P, R, NP], F16)
        iota_e = sb("iota_e", [P, EX], F32)
        sel_rel = sb("sel_rel", [P, R, P], F16)
        sel_row = sb("sel_row", [P, NTY + 1, P], F16)
        brow = sb("brow", [P, D], F32)
        brow_hi = sb("brow_hi", [P, D], F16)
        brow_lo = sb("brow_lo", [P, D], F16)
        temp = sb("temp", [P, HP], F32)
        swb = sb("swb", [P, EX], F32)
        sw_sb = sb("sw_sb", [EX, D], F32)
        swT = sb("swT", [P, KC, EX], F32)
        cnt = sb("cnt", [P, NW], F32)
        lim = sb("lim", [1, NW + 4], F32)
        num = sb("num", [1, NW], F32)
        limi = sb("limi", [1, NW + 1], I32)
        wkeys = sb("wkeys", [P, NW, 2, J], F32)
        gkeys = sb("gkeys", [P, 2, NG, J], F32)
        nt_i = sb("nt_i", [P, NT], I32)
        nmask = sb("nmask", [P, NTY, NT], F32)
        stats = sb("stats", [P, NT, 6], F32)
        mv = sb("mv", [P, NT, 2], F32)
        sd = sb("sd", [P, 4, NT], F32)
        den = sb("den", [P, 2, NT, H], F32)
        lg = sb("lg", [P, 4, NT, EX], F32)
        oh16 = sb("oh16", [P, NT, EX], F16)
        rt = sb("rt", [P, 12, NT], F32)
        slots = sb("slots", [P, 2, NT], I32)
        token = sb("token", [P, NT, 2], F32)
        owner = sb("owner", [P, NBT, 2], F32)
        nobody = sb("nobody", [P, NBT, 2], I32)

        tbank = [ctx.enter_context(nc.psum_tensor(f"tbank{i}", [P, KC, P], F32)) for i in range(3)]
        mbank = [ctx.enter_context(nc.psum_tensor(f"mbank{i}", [P, D], F32)) for i in range(3)]
        abank = [ctx.enter_context(nc.psum_tensor(f"abank{i}", [P, D], F32)) for i in range(2)]

        key_dram = nc.dram_tensor("key_scratch", (2, EPAD), F32, kind="Internal").ap()
        owner_dram = nc.dram_tensor("owner_scratch", (NBT * P, 2), F32, kind="Internal").ap()

        EXPERTS = [f"e{e}" for e in range(EX)]
        MATS = ["k", "v", "q", "r0", "p", "r1", "r2", "s0", "s1", "s2"] + EXPERTS

        def turns(m):
            return [("turn", m, kc) for kc in range(KC)]

        def directs(m):
            return [("direct", m, h) for h in range(2)]

        def tiles(kind, *rest):
            return [(kind, *rest, t) for t in range(NT)]

        def weave(main, between):
            done, mixed = 0, []
            for i, task in enumerate(main):
                upto = -(-len(between) * (i + 1) // len(main))
                mixed += [task] + between[done:upto]
                done = upto
            return mixed

        def expert(e):
            return [("ex", e, kc) for kc in range(KC)]

        AHEAD = 9
        TASKS = turns("k") + tiles("x") + weave(tiles("mm", "k"), turns("v"))
        TASKS += weave(tiles("mm", "v"), turns("q") + [("bias",)])
        TASKS += [("ks",), ("kv",)]
        TASKS += weave(tiles("mm", "q"), directs("r0") + [("edge",)] + turns("p"))
        TASKS += weave(tiles("mm", "r0"), directs("r1") + tiles("den"))
        TASKS += weave(tiles("mm", "r1"), directs("r2") + tiles("qt") + [("lim",)])
        TASKS += [("p", g) for g in range(HP)]
        TASKS += weave(tiles("y"), directs("s0"))
        TASKS += weave(tiles("mm", "r2"), directs("s1") + directs("s2") + turns("e0") + [("sw",)] + turns("e1"))
        TASKS += turns("e2")
        TASKS += [("ab",)]
        AGGPARTS = 5
        BATCHES = [(0, 3), (3, NT)]
        slots_turn = {0: 3, 1: 3, 2: 3, 3: 3, 4: 4}
        between = turns("e3") + turns("e4") + turns("e5") + turns("e6")
        for t in range(NT):
            for part in range(AGGPARTS):
                TASKS += [("agg", t, part)]
                if part >= AGGPARTS - slots_turn[t]:
                    TASKS += between[0:1]
                    between = between[1:]
                if t >= 1 and part == 0:
                    TASKS += [("dev", t - 1)]
                if 1 <= t < NT - 1 and part == 3:
                    TASKS += [("lx", t - 1), ("xl", t - 1)]
                if 1 <= t < NT - 1 and part == 4:
                    TASKS += [("lo", t - 1)]
                if t == NT - 1:
                    TASKS += {0: [("cum", 0)], 2: [("pos", 0)], 3: [("route", 0)]}.get(part, [])
        E7, E8 = turns("e7"), turns("e8")
        TASKS += [("lx", NT - 2), E7[0], ("lo", NT - 2), ("dev", NT - 1), ("xl", NT - 2), E7[1], E7[2],
                  ("lx", NT - 1), ("lo", NT - 1), ("xl", NT - 1), E7[3], ("cum", 1), E8[0], ("pos", 1),
                  ("route", 1), E8[1], E8[2]]

        def dispatch(half):
            return [("dp", half, part, kc) for kc in range(KC) for part in range(2)]

        TASKS += dispatch(0)[0:2] + turns("e8")[3:4] + dispatch(0)[2:]
        beside = dispatch(1)
        for e in range(EX):
            later = (e + 1) // 2 - 1 + AHEAD
            other = turns(f"e{later}")[(1 - e % 2) * 2:][:2] if 1 <= e and later < EX else []
            if e < 4:
                other = other + beside[2 * e:2 * e + 2]
            TASKS += weave(expert(e), other)
            TASKS += [("base", t) for t in range(NT) if (t == 0) + 2 * (t in (1, 2)) + 3 * (t > 2) == e]

        class Ring:

            def __init__(self, banks, name):
                self.banks, self.readers, self.first = banks, [], {}
                self.filled, self.act, self.dve = sem(name + "_filled"), sem(name + "_act"), sem(name + "_dve")

            def add(self, task, readers):
                self.first[task] = len(self.readers)
                self.readers.append(readers)

            def bank(self, task):
                return self.banks[self.first[task] % len(self.banks)]

            def count(self, u, reader):
                return sum(reader in r for r in self.readers[:u + 1])

            def wait_filled(self, eng, task):
                eng.wait_ge(self.filled, self.first[task] + 1)

            def wait_act(self, eng, task):
                eng.wait_ge(self.act, self.count(self.first[task], "A"))

            def wait_free(self, eng, task):
                u = self.first[task] - len(self.banks)
                if u >= 0:
                    self.wait_use(eng, u)

            def wait_emptied(self, eng, task):
                self.wait_use(eng, self.first[task])

            def wait_use(self, eng, u):
                if "D" in self.readers[u]:
                    eng.wait_ge(self.dve, self.count(u, "D"))
                else:
                    eng.wait_ge(self.act, self.count(u, "A"))

        tr, mr = Ring(tbank, "turn"), Ring(mbank, "prod")
        MM_READERS = {"k": "A", "q": "A", "v": "D", "r": "AD", "s": "D"}
        for task in TASKS:
            kind = task[0]
            if kind == "turn":
                tr.add(task, "A" if task[1] == "p" else "AD")
            elif kind == "x":
                tr.add(task, "AD")
            elif kind == "dp":
                tr.add(task, "D" if task[1:3] == (0, 1) else "A")
            elif kind in ("qt", "sw", "lx"):
                tr.add(task, "A")
            elif kind == "mm":
                mr.add(task, MM_READERS[task[1][0]])
            elif kind in ("kv", "y"):
                mr.add(task, "D")
            elif kind == "agg" and task[2] == AGGPARTS - 1:
                mr.add(("agg", task[1]), "D")
            elif kind in ("ks", "p"):
                mr.add(task, "A")
            elif kind == "ab":
                for t in range(NT):
                    for r in range(NTY):
                        mr.add(("self", t, r), "D")
            elif kind == "ex" and task[2] == KC - 1:
                mr.add(("ex", task[1]), "AD")
        DIRECT = [task for task in TASKS if task[0] == "direct"]

        place = [(whi[i][:], wlo[i][:]) for i in range(NSPLIT)]

        def kdn(ap):
            return ap.rearrange("p (k n) -> p k n", k=KC)

        for o in (8192, 10240):
            place.append((kdn(early[:, o:o + 1024].bitcast(F16)), kdn(early[:, o + 1024:o + 2048].bitcast(F16))))
        place.append((kdn(xhi[:].rearrange("p k n -> p (k n)")[:, 0:KC * D]),
                      kdn(xlo[:].rearrange("p k n -> p (k n)")[:, 0:KC * D])))
        xr_flat = xr[:].rearrange("p h t d -> p (h t d)")
        for i in range(2):
            o = NT * D * 2 + i * 2 * KC * D
            place.append((kdn(xr_flat[:, o:o + KC * D]), kdn(xr_flat[:, o + KC * D:o + 2 * KC * D])))
        PLACE = {"k": 0, "v": 1, "q": 2, "r0": 3, "r1": 0, "r2": 1, "s0": 2, "s1": 3, "s2": 4,
                 "e0": 5, "e1": 0, "e2": 1, "e3": 2, "e4": 3, "e5": 4, "e6": 6, "e7": 7, "e8": 8}
        for e in range(AHEAD, EX):
            PLACE[f"e{e}"] = PLACE[f"e{e - AHEAD}"]
        FREED = {4: ("y", NT - 1), 5: ("y", NT - 1), 6: ("self", NT - 1, NTY - 1), 7: ("agg", NT - 1),
                 8: ("agg", NT - 1)}

        def last_use(m):
            if m[0] == "e":
                return ("ex", int(m[1:]))
            return ("self", NT - 1, int(m[1])) if m[0] == "s" else ("mm", m, NT - 1)

        BEFORE = {}
        for m in MATS:
            if m != "p":
                BEFORE[m] = FREED.get(PLACE[m])
                FREED[PLACE[m]] = last_use(m)

        s_x = [sem(f"x_in{t}") for t in range(NT)]
        s_w = [sem(f"weights_in{i}") for i in range(NSTAGE)]
        s_par = sem("params_in")
        s_const = sem("constants")
        s_edge = sem("edges_in")
        s_step = sem("dve_step")
        s_mv = sem("variance_ready")
        s_sd = sem("deviation_ready")
        s_ln = sem("normalised")
        s_dhi = sem("direct_hi")
        s_dlo = sem("direct_lo")
        s_bhi = sem("bias_hi")
        s_blo = sem("bias_lo")
        s_ekey = sem("edge_keys")
        s_cnt = sem("edge_counts")
        s_cntp = sem("edge_totals")
        s_lim = sem("window_limits")
        s_kst = sem("keys_stored")
        s_wk = sem("window_keys_in")
        s_gk = sem("group_keys_in")
        s_oh = sem("onehots_ready")
        s_ohf = sem("onehots_free")
        s_ab = sem("window_summed")
        s_abf = sem("window_bank_free")
        s_ksum = sem("keys_summed")
        s_qn = sem("queries_scaled")
        s_lgp = sem("logits_ready")
        s_oh16 = sem("routes_ready")
        s_cum = sem("positions_ready")
        s_exd = sem("logits_shifted")
        s_exp = sem("exp_ready")
        s_slot = sem("slots_ready")
        s_xhi = sem("tokens_hi")
        s_xlo = sem("tokens_lo")
        s_sel = sem("slot_onehots_ready")
        s_init = sem("owners_cleared")
        s_scat = sem("owners_scattered")
        s_own = sem("owners_in")
        s_bt = sem("token_bias_in")
        s_base = sem("base_ready")
        s_add = [sem(f"results_added{i}") for i in range(2)]
        s_scaled = sem("results_scaled")
        s_out = sem("stored")

        s_pool = sem("pool_step")
        block = ctx.enter_context(nc.Block())

        def rows(t):
            return TAIL if t == NT - 1 else P

        def stage_of(m):
            return stage[MATS.index(m) % NSTAGE]

        def wait_stage(eng, m):
            i = MATS.index(m)
            eng.wait_ge(s_w[i % NSTAGE], 16 * (i // NSTAGE + 1))

        def hi_of(m):
            return place[PLACE[m]][0]

        def lo_of(m):
            return place[PLACE[m]][1]

        def wait_split(eng, m):
            if ("turn", m, KC - 1) in tr.first:
                tr.wait_emptied(eng, ("turn", m, KC - 1))
            else:
                eng.wait_ge(s_dlo, DIRECT.index(("direct", m, 1)) + 1)

        def wait_place(eng, m):
            if BEFORE[m] is not None:
                mr.wait_filled(eng, BEFORE[m])

        def slots_in(task):
            return tr.bank(task)[:].rearrange("p k n -> p (k n)")[:, 0:EH * CS]

        def dispatched(task):
            _, half, part, kc = task
            return bT[:, kc, half * EH:(half + 1) * EH, part * HALF:part * HALF + CS]

        @block.sync
        def _(sp):
            for t in range(NT):
                if t == NT - 1:
                    sp.wait_ge(s_const, 2)
                sp.dma_start(x_sb[0:rows(t), t, :], x[t * P:t * P + rows(t), :]).then_inc(s_x[t], 16)
            source = {"k": Wqkv[D:2 * D], "v": Wqkv[2 * D:3 * D], "q": Wqkv[0:D], "p": Wproj}
            for r in range(R):
                source[f"r{r}"] = W_rel[r]
            for r in range(NTY):
                source[f"s{r}"] = W_self[r]
            for e in range(EX):
                source[f"e{e}"] = expert_w[e]
            for i, m in enumerate(MATS):
                if i >= NSTAGE:
                    old = MATS[i - NSTAGE]
                    if ("turn", old, KC - 1) in tr.first:
                        tr.wait_filled(sp, ("turn", old, KC - 1))
                    else:
                        sp.wait_ge(s_dlo, DIRECT.index(("direct", old, 1)) + 1)
                if m == f"e{EX - 3}":
                    for t in range(NT):
                        sp.wait_ge(s_base, t + 1)
                        sp.dma_start(out[t * P:t * P + rows(t), :], x_sb[0:rows(t), t, :]).then_inc(s_out, 16)
                sp.dma_start(stage_of(m)[:], source[m].rearrange("(k p) n -> p k n", p=P))\
                  .then_inc(s_w[i % NSTAGE], 16)
            sp.wait_ge(s_out, 16 * NT)
            for i in range(2):
                sp.wait_ge(s_add[i], 16 * NBT // 2)

        @block.gpsimd
        def _(pool):
            steps = [0]

            def link(ins):
                steps[0] += 1
                ins.then_inc(s_pool, 1)
                pool.wait_ge(s_pool, steps[0])

            link(nc.gpsimd.memset(ident[:], 0.0))
            nc.gpsimd.affine_select(out=ident[:], in_=ident[:], compare_op=ALU.not_equal, fill=1.0, base=0,
                                    pattern=[[-1, P]], channel_multiplier=1).then_inc(s_const, 1)
            nc.gpsimd.memset(x_sb[:, NT - 1, :], 0.0).then_inc(s_const, 1)
            link(nc.gpsimd.memset(edges[:, 2, :], 2 ** 20))
            flat = "(p c) -> p c"
            pool.dma_start(edges[0:EP, 1, :], dst.rearrange(flat, c=EC)).then_inc(s_edge, 16)
            pool.dma_start(edges[0:EP - 1, 2, :], dst[1:1 + (EP - 1) * EC].rearrange(flat, c=EC)).then_inc(s_edge, 16)
            pool.dma_start(edges[EP - 1:EP, 2, 0:EC - 1], dst[1 + (EP - 1) * EC:NE].unsqueeze(0)).then_inc(s_edge, 16)
            pool.dma_start(edges[0:EP, 0, :], src.rearrange(flat, c=EC)).then_inc(s_edge, 16)
            pool.dma_start(edges[0:EP, 3, :], edge_type.rearrange(flat, c=EC)).then_inc(s_edge, 16)
            link(nc.gpsimd.memset(brow[:], 0.0))
            link(nc.gpsimd.memset(nt_i[:], 0))
            pool.dma_start(brow[0:R, :], b_rel).then_inc(s_par, 16)
            pool.dma_start(brow[R:R + NTY, :], b_self).then_inc(s_par, 16)
            pool.dma_start(brow[R + NTY:R + NTY + 1, :], bproj.unsqueeze(0)).then_inc(s_par, 16)
            pool.dma_start(nt_i[:, 0:NT - 1], node_type[0:(NT - 1) * P].rearrange("(t p) -> p t", p=P),
                           allow_slow_non_contiguous=True).then_inc(s_par, 16)
            pool.dma_start(nt_i[0:TAIL, NT - 1:NT], node_type[(NT - 1) * P:N].unsqueeze(1)).then_inc(s_par, 16)
            tv = temperature.rearrange("(g h) a b -> h (a b g)", h=2)
            for h in range(2):
                pool.dma_start(temp[h * DH:(h + 1) * DH, :], tv[h:h + 1, :].to_broadcast([DH, HP]),
                               allow_slow_non_contiguous=True).then_inc(s_par, 16)
            pool.dma_start(swb[:], switch_b.unsqueeze(0).to_broadcast([P, EX])).then_inc(s_par, 16)
            pool.dma_start(sw_sb[:], switch_w).then_inc(s_par, 16)
            link(nc.gpsimd.memset(sel_rel[:], 0.0))
            link(nc.gpsimd.memset(sel_row[:], 0.0))
            nc.gpsimd.affine_select(out=sel_rel[:], in_=sel_rel[:], compare_op=ALU.not_equal, fill=WS,
                                    base=-(N - (NT - 1) * P), pattern=[[-1000, R], [1, P]], channel_multiplier=1000)
            nc.gpsimd.affine_select(out=sel_row[:, 0:NTY, :], in_=sel_row[:, 0:NTY, :], compare_op=ALU.not_equal,
                                    fill=WS, base=-R, pattern=[[-1, NTY], [0, P]], channel_multiplier=1)
            nc.gpsimd.affine_select(out=sel_row[:, NTY, :], in_=sel_row[:, NTY, :], compare_op=ALU.not_equal,
                                    fill=RS, base=-R - NTY, pattern=[[0, P]], channel_multiplier=1)
            nc.gpsimd.memset(attnT[:], 0.0)
            nc.gpsimd.memset(onesf[:], 1.0).then_inc(s_const, 1)
            nc.gpsimd.iota(iota_s[:], [[1, EX * CS]], base=0, channel_multiplier=0, allow_small_or_imprecise_dtypes=True)
            nc.gpsimd.iota(iota_d[:], [[NP, R], [1, NP]], base=0, channel_multiplier=0,
                           allow_small_or_imprecise_dtypes=True).then_inc(s_const, 1)
            for t in range(1, NT):
                mr.wait_emptied(pool, ("mm", "k", t))
                link(nc.gpsimd.tensor_tensor(k_sum, k_sb[:, 0, :] if t == 1 else k_sum, k_sb[:, t, :], ALU.add))
            pool.sem_inc(s_ksum, 1)
            nc.gpsimd.iota(iota_e[:], [[1, EX]], base=-EX, channel_multiplier=0,
                           allow_small_or_imprecise_dtypes=True)
            link(nc.gpsimd.memset(ones16[:], 1.0))
            nc.gpsimd.affine_select(out=tri16[:], in_=ones16[:], compare_op=ALU.is_gt, fill=0.0, base=0,
                                    pattern=[[1, P]], channel_multiplier=-1).then_inc(s_const, 1)
            link(nc.gpsimd.memset(padk, NOKEY))
            pool.wait_ge(s_ekey, 1)
            pool.dma_start(key_dram[0, 0:NE].rearrange(flat, c=EC), ef[0:EP, 0, :]).then_inc(s_kst, 16)
            pool.dma_start(key_dram[1, 0:NE].rearrange(flat, c=EC), ef[0:EP, 3, :]).then_inc(s_kst, 16)
            for k in range(2):
                pool.dma_start(key_dram[k:k + 1, NE:EPAD], padk).then_inc(s_kst, 16)
            pool.wait_ge(s_kst, 64)
            for k in range(2):
                pool.dma_start(gkeys[:, k, :, :], key_dram[k].rearrange("(g p j) -> p g j", p=P, j=J))\
                    .then_inc(s_gk, 16)
            pool.wait_ge(s_lim, 1)
            with pool.Fori(0, NW) as w:
                start = pool.value_load(limi[0:1, bass.ds(w, 1)], min_val=0, max_val=NE)
                pool.dma_start(wkeys[:, bass.ds(w, 1), :, :].rearrange("p w k j -> p (w k) j"),
                               key_dram[:, bass.ds(start, GE)].rearrange("k (p j) -> p k j", j=J))\
                    .then_inc(s_wk, 16)
            nc.gpsimd.memset(nobody[:], OOB).then_inc(s_const, 1)
            nc.gpsimd.iota(token[:, :, 0].bitcast(I32), [[P, NT]], base=0, channel_multiplier=1)\
                .then_inc(s_const, 1)
            pool.wait_ge(s_const, 7)
            pool.dma_start(owner_dram.rearrange("(i p) c -> p i c", p=P), nobody[:].bitcast(F32))\
                .then_inc(s_init, 16)
            pool.wait_ge(s_init, 16)
            pool.wait_ge(s_slot, len(BATCHES))
            for t in range(NT):
                n = rows(t)
                pool.indirect_dma_start(bias_tok[0:n, t, :], None, expert_b,
                                        bass.IndirectOffsetOnAxis(ap=slots[0:n, 1, t:t + 1].bitcast(U32), axis=0),
                                        bounds_check=EX - 1, oob_is_err=False).then_inc(s_bt, 16)
            for t in range(NT):
                n = rows(t)
                pool.indirect_dma_start(owner_dram, bass.IndirectOffsetOnAxis(ap=slots[0:n, 0, t:t + 1].bitcast(U32), axis=0),
                                        token[0:n, t, :], None, bounds_check=NBT * P - 1, oob_is_err=False)\
                    .then_inc(s_scat, 16)
            pool.wait_ge(s_scat, 16 * NT)
            pool.dma_start(owner[:], owner_dram.rearrange("(i p) c -> p i c", p=P)).then_inc(s_own, 16)
            pool.wait_ge(s_own, 16)
            for i in range(NBT):
                if i == 0:
                    pool.wait_ge(s_out, 16 * NT)
                pool.wait_ge(s_scaled, i + 1)
                pool.indirect_dma_start(out, bass.IndirectOffsetOnAxis(
                    ap=owner[0:HALF + CS, i, 0:1].bitcast(U32), axis=0), yexp[0:HALF + CS, i % 2, :], None, bounds_check=N - 1,
                    oob_is_err=False, compute_op=ALU.add).then_inc(s_add[i % 2], 16)

        @block.tensor
        def _(pe):
            def turn(task, chunks):
                tr.wait_free(pe, task)
                for i, chunk in enumerate(chunks):
                    last = nc.tensor.transpose(tr.bank(task)[:, i, :], chunk, ident[:])
                last.then_inc(tr.filled, 1)

            def row_chunks(rows_of):
                return [rows_of[:, kc * P:(kc + 1) * P] for kc in range(KC)]

            def split_product(bank, m, cols, bias):
                first = True
                for kc in range(KC):
                    a, b = xhi[:, kc, cols], xlo[:, kc, cols]
                    for lhs, rhs in ((a, hi_of(m)), (a, lo_of(m)), (b, hi_of(m))):
                        last = nc.tensor.matmul(bank, lhs, rhs[:, kc, :], start=first, stop=False,
                                                skip_group_check=True)
                        first = False
                if bias is not None:
                    for part in (brow_hi, brow_lo):
                        last = nc.tensor.matmul(bank, bias, part[:], start=False, stop=False, skip_group_check=True)
                return last

            def window(bank, b, first):
                for st in range(NT):
                    for j in range(J):
                        last = nc.tensor.matmul(bank[:, st * R * WIN:(st + 1) * R * WIN],
                                                onehot_s[:, b, j, st * P:(st + 1) * P],
                                                onehot_d[:, b, j, :, :].rearrange("p r d -> p (r d)"),
                                                start=(first and st == 0 and j == 0), stop=False,
                                                skip_group_check=True)
                return last

            def self_product(t, r):
                u = mr.first[("self", 0, r)]
                pe.wait_ge(mr.dve, t * NTY + mr.count(u - 3, "D"))
                split_product(mr.bank(("self", 0, r))[:], f"s{r}", bass.ds(t * P, P), sel_row[:, r, :])\
                    .then_inc(mr.filled, 1)

            pe.wait_ge(s_const, 1)
            for task in TASKS:
                kind, i = task[0], task[-1]
                if kind == "turn":
                    m = task[1]
                    wait_stage(pe, m)
                    turn(task, [stage_of(m)[:, oc, i * P:(i + 1) * P] for oc in range(KC)])
                elif kind == "x":
                    pe.wait_ge(s_ln, i + 1)
                    turn(task, row_chunks(xs[:, i, :]))
                elif kind == "mm":
                    m, bias = task[1], None
                    if m == "k":
                        tr.wait_emptied(pe, ("x", i))
                    if m == "r0" and i == 0:
                        pe.wait_ge(s_blo, 1)
                        pe.wait_ge(s_const, 3)
                    if i == 0:
                        wait_split(pe, m)
                    if m[0] == "r" and i == NT - 1:
                        bias = sel_rel[:, int(m[1]), :]
                    mr.wait_free(pe, task)
                    split_product(mr.bank(task)[:], m, slice(i * P, (i + 1) * P), bias).then_inc(mr.filled, 1)
                elif kind == "kv":
                    mr.wait_free(pe, task)
                    mr.wait_emptied(pe, ("mm", "k", NT - 1))
                    mr.wait_emptied(pe, ("mm", "v", NT - 1))
                    for g in range(HP):
                        c = slice(g * P, (g + 1) * P)
                        for t in range(NT):
                            last = nc.tensor.matmul(mr.bank(task)[:, c], v_sb[:, t, c], k_sb[:, t, c],
                                                    start=(t == 0), stop=(t == NT - 1))
                    last.then_inc(mr.filled, 1)
                elif kind == "ks":
                    pe.wait_ge(s_const, 3)
                    mr.wait_free(pe, task)
                    pe.wait_ge(s_ksum, 1)
                    nc.tensor.matmul(mr.bank(task)[:], onesf[:], k_sum, start=True, stop=True)\
                        .then_inc(mr.filled, 1)
                elif kind == "qt":
                    pe.wait_ge(s_qn, i + 1)
                    turn(task, row_chunks(q_sb[:, i, :]))
                    if i == 0:
                        pe.wait_ge(s_cnt, 1)
                        nc.tensor.matmul(abank[0][:, 0:NW], onesf[:], cnt[:], start=True, stop=True)\
                            .then_inc(s_cntp, 1)
                elif kind == "p":
                    if i == 0:
                        mr.wait_emptied(pe, ("kv",))
                        tr.wait_emptied(pe, ("turn", "p", KC - 1))
                    mr.wait_free(pe, task)
                    nc.tensor.matmul(mr.bank(task)[:], attnT[:, i, :], projT[:, i, :], start=True,
                                     stop=True).then_inc(mr.filled, 1)
                elif kind == "y":
                    if i == 0:
                        mr.wait_emptied(pe, ("p", HP - 1))
                        tr.wait_emptied(pe, ("qt", NT - 1))
                    mr.wait_free(pe, task)
                    for g in range(HP):
                        nc.tensor.matmul(mr.bank(task)[:], qnT[:, g, i * P:(i + 1) * P], Pm[:, g, :],
                                         start=(g == 0), stop=False, skip_group_check=True)
                    for part in (brow_hi, brow_lo):
                        last = nc.tensor.matmul(mr.bank(task)[:], sel_row[:, NTY, :], part[:],
                                                start=False, stop=False, skip_group_check=True)
                    last.then_inc(mr.filled, 1)
                elif kind == "ab":
                    for r in range(NTY):
                        wait_split(pe, f"s{r}")
                    pe.wait_ge(s_lim, 1)
                    ordered = pe.value_load(limi[0:1, NW:NW + 1], min_val=0, max_val=1)
                    with pe.If(ordered > 0):
                        with pe.Fori(0, NT) as t:
                            for i in range(WT):
                                if i < NTY:
                                    self_product(t, i)
                                pe.wait_ge(s_abf, t * WT + i + 1)
                                pe.wait_ge(s_oh, t * WT + i + 1)
                                window(abank[i % 2], i % 2, True).then_inc(s_ohf, 1)
                    with pe.Else():
                        with pe.Fori(0, NW // 2) as pair:
                            for b in range(2):
                                pe.wait_ge(s_abf, pair * 2 + b + 1)
                                for o in range(2):
                                    pe.wait_ge(s_oh, (pair * 2 + b) * NG + o + 1)
                                    window(abank[b], o, o == 0).then_inc(s_ohf, 1)
                                with pe.Fori(1, NG // 2) as gp:
                                    for o in range(2):
                                        pe.wait_ge(s_oh, (pair * 2 + b) * NG + gp * 2 + o + 1)
                                        window(abank[b], o, False).then_inc(s_ohf, 1)
                        with pe.Fori(0, NT) as t:
                            for r in range(NTY):
                                self_product(t, r)
                elif kind == "sw":
                    tr.wait_free(pe, task)
                    for kc in range(KC):
                        last = nc.tensor.transpose(tr.bank(task)[:, 0, kc * EX:(kc + 1) * EX],
                                                   sw_sb[:, kc * P:(kc + 1) * P], ident[0:EX, 0:EX])
                    last.then_inc(tr.filled, 1)
                elif kind == "agg":
                    u, t, count = task[0:2], task[1], R * NT // AGGPARTS
                    if t == 0 and i == 0:
                        mr.wait_emptied(pe, ("mm", f"r{R - 1}", NT - 1))
                        pe.wait_ge(s_abf, NW + 2)
                    if i == 0:
                        mr.wait_free(pe, u)
                    for n in range(i * count, (i + 1) * count):
                        for part in range(2):
                            last = nc.tensor.matmul(mr.bank(u)[:], at_sb[:, n, t * P:(t + 1) * P],
                                                    xr[:, part, n, :], start=(n == 0 and part == 0),
                                                    stop=(n == R * NT - 1 and part == 1))
                    if i == AGGPARTS - 1:
                        last.then_inc(mr.filled, 1)
                elif kind == "lx":
                    pe.wait_ge(s_ln, NT + i + 1)
                    turn(task, row_chunks(xs[:, i, :]))
                elif kind == "lo":
                    tr.wait_emptied(pe, ("lx", i))
                    for kc in range(KC):
                        last = nc.tensor.matmul(abank[0][:, i * EX:(i + 1) * EX], xfT[:, i % 2, kc, :],
                                                swT[:, kc, :], start=(kc == 0), stop=(kc == KC - 1))
                    last.then_inc(s_lgp, 1)
                elif kind == "pos":
                    pe.wait_ge(s_const, 5)
                    pe.wait_ge(s_oh16, i + 1)
                    for t in range(*BATCHES[i]):
                        for o in range(t + 1):
                            last = nc.tensor.matmul(abank[1][:, t * EX:(t + 1) * EX],
                                                    tri16[:] if o == t else ones16[:], oh16[:, o, :],
                                                    start=(o == 0), stop=(o == t))
                    last.then_inc(s_cum, 1)
                elif kind == "dp":
                    _, half, part, kc = task
                    pe.wait_ge(s_xlo if part else s_xhi, NT)
                    pe.wait_ge(s_sel, NT)
                    tr.wait_free(pe, task)
                    for t in range(NT):
                        n = rows(t)
                        last = nc.tensor.matmul(slots_in(task), xf[0:n, part, t, kc * P:(kc + 1) * P],
                                                slot_of[0:n, t, half * EH * CS:(half + 1) * EH * CS],
                                                start=(t == 0), stop=(t == NT - 1))
                    last.then_inc(tr.filled, 1)
                elif kind == "ex":
                    e, u = task[1], ("ex", task[1])
                    if i == 0:
                        if e % EH == 0:
                            for part in range(2):
                                tr.wait_emptied(pe, ("dp", e // EH, part, KC - 1))
                        wait_split(pe, f"e{e}")
                        mr.wait_free(pe, u)
                    for n, w in enumerate((hi_of(f"e{e}"), lo_of(f"e{e}"))):
                        last = nc.tensor.matmul(mr.bank(u)[0:HALF + CS, :], bT[:, i, e, 0:HALF + CS], w[:, i, :],
                                                start=(i == 0 and n == 0), stop=(i == KC - 1 and n == 1))
                    if i == KC - 1:
                        last.then_inc(mr.filled, 1)

        @block.scalar
        def _(act):
            def flat(bank):
                return bank[:].rearrange("p k n -> p (k n)")

            act.wait_ge(s_mv, 1)
            nc.scalar.activation(sd[:, 1, :], sd[:, 0, :], ACT.Sqrt).then_inc(s_sd, 1)
            for task in TASKS:
                kind, i = task[0], task[-1]
                if kind in ("turn", "x", "qt", "sw", "lx"):
                    if kind == "turn" and i == 0 and task[1] != "p":
                        wait_place(act, task[1])
                    if kind == "lx" and i >= 2:
                        act.wait_ge(s_lgp, i - 1)
                    tr.wait_filled(act, task)
                    bank = tr.bank(task)
                    if kind == "turn" and task[1] == "p":
                        ins = nc.scalar.activation(projT[:, i, :], flat(bank), ACT.Copy)
                    elif kind == "turn":
                        ins = nc.scalar.activation(hi_of(task[1])[:, i, :], flat(bank), ACT.Copy, scale=WS)
                    elif kind == "x":
                        ins = nc.scalar.activation(xhi[:, :, i * P:(i + 1) * P], bank[:], ACT.Copy)
                    elif kind == "qt":
                        ins = nc.scalar.activation(qnT[:, :, i * P:(i + 1) * P], bank[:], ACT.Copy)
                    elif kind == "sw":
                        ins = nc.scalar.activation(swT[:].rearrange("p k e -> p (k e)"), bank[:, 0, 0:KC * EX],
                                                   ACT.Copy)
                    else:
                        ins = nc.scalar.activation(xfT[:, i % 2, :, :], bank[:], ACT.Copy)
                    ins.then_inc(tr.act, 1)
                    if kind == "lx":
                        nc.scalar.activation(xf[:, 0, i, :], xs[:, i, :], ACT.Copy, scale=WS).then_inc(s_xhi, 1)
                elif kind == "dp" and task[1:3] != (0, 1):
                    if task[1:] == (0, 0, 0):
                        mr.wait_emptied(act, ("agg", NT - 1))
                    tr.wait_filled(act, task)
                    nc.scalar.activation(dispatched(task), slots_in(task).rearrange("p (e c) -> p e c", e=EH),
                                         ACT.Copy).then_inc(tr.act, 1)
                elif kind == "direct":
                    m = task[1]
                    if i == 0:
                        wait_place(act, m)
                        wait_stage(act, m)
                    c = slice(i * KC // 2, (i + 1) * KC // 2)
                    nc.scalar.activation(hi_of(m)[:, c, :], stage_of(m)[:, c, :], ACT.Copy, scale=WS)\
                        .then_inc(s_dhi, 1)
                elif kind == "bias":
                    act.wait_ge(s_par, 9 * 16)
                    nc.scalar.activation(brow_hi[:], brow[:], ACT.Copy, scale=WS).then_inc(s_bhi, 1)
                elif kind == "mm" and task[1][0] in "kqr":
                    m = task[1]
                    mr.wait_filled(act, task)
                    if m[0] == "r":
                        nc.scalar.activation(xr[:, 0, int(m[1]) * NT + i, :], mr.bank(task)[:], ACT.Copy,
                                             scale=RS).then_inc(mr.act, 1)
                    else:
                        nc.scalar.activation((k_sb if m == "k" else q_sb)[:, i, :], mr.bank(task)[:], ACT.Relu,
                                             scale=RS * RS).then_inc(mr.act, 1)
                elif kind == "ks":
                    mr.wait_filled(act, task)
                    nc.scalar.activation(ksumB, mr.bank(task)[:], ACT.Copy).then_inc(mr.act, 1)
                elif kind == "p":
                    mr.wait_filled(act, task)
                    nc.scalar.activation(Pm[:, i, :], mr.bank(task)[:], ACT.Copy).then_inc(mr.act, 1)
                elif kind == "ab":
                    act.sem_inc(s_abf, 2)
                    act.wait_ge(s_kst, 64)
                    counts = at_sb[:].rearrange("p (r s) n -> p s r n", s=NT)

                    def empty_window(w, b):
                        v = abank[b][:, 0:NT * R * WIN].rearrange("p (s r d) -> p s r d", s=NT, r=R)
                        nc.scalar.activation(counts[:, :, :, bass.ds(w * WIN, WIN)], v, ACT.Copy)\
                            .then_inc(s_abf, 1)

                    act.wait_ge(s_lim, 1)
                    ordered = act.value_load(limi[0:1, NW:NW + 1], min_val=0, max_val=1)
                    with act.If(ordered > 0):
                        with act.Fori(0, NT) as t:
                            for i in range(WT):
                                act.wait_ge(s_ohf, t * WT + i + 1 + 2)
                                empty_window(t * WT + i, i % 2)
                    with act.Else():
                        with act.Fori(0, NW // 2) as pair:
                            for b in range(2):
                                act.wait_ge(s_ohf, (pair * 2 + b + 1) * NG + 2)
                                empty_window(pair * 2 + b, b)
                elif kind == "dev":
                    act.wait_ge(s_mv, i + 2)
                    nc.scalar.activation(sd[:, 1, i:i + 1], sd[:, 0, i:i + 1], ACT.Sqrt).then_inc(s_sd, 1)
                elif kind == "route":
                    if i == 1:
                        act.wait_ge(s_exd, 2)
                        nc.scalar.activation(lg[:, 3, :, :], lg[:, 2, :, :], ACT.Exp).then_inc(s_exp, 1)
                elif kind == "ex" and i == KC - 1:
                    e, u = task[1], ("ex", task[1])
                    if e >= 2:
                        mr.wait_emptied(act, ("ex", e - 2))
                    mr.wait_filled(act, u)
                    nc.scalar.activation(ylow[0:CS, e % 2, :], mr.bank(u)[HALF:HALF + CS, :], ACT.Copy,
                                         scale=RS * RS).then_inc(mr.act, 1)

        @block.vector
        def _(dve):
            steps = [0]

            def link(ins):
                steps[0] += 1
                ins.then_inc(s_step, 1)
                dve.wait_ge(s_step, steps[0])

            V = nc.vector

            def deviation(c, n):
                link(V.reciprocal(sd[:, 2, c:c + n], sd[:, 1, c:c + n]))
                link(V.tensor_tensor(sd[:, 2, c:c + n], sd[:, 2, c:c + n], sd[:, 0, c:c + n], ALU.mult))
                link(V.tensor_tensor(sd[:, 2, c:c + n], sd[:, 2, c:c + n], sd[:, 1, c:c + n], ALU.add))
                link(V.reciprocal(sd[:, 3, c:c + n], sd[:, 2, c:c + n]))

            def turned_low(task, low, high, scale):
                tr.wait_act(dve, task)
                V.scalar_tensor_tensor(out=low, in0=tr.bank(task)[:], scalar=scale, in1=high, op0=ALU.mult,
                                       op1=ALU.subtract).then_inc(tr.dve, 1)

            def kcn(ap):
                return ap.rearrange("p (k n) -> p k n", k=KC)

            for t in range(NT):
                dve.wait_ge(s_x[t], 16)
                link(V.bn_stats(stats[:, t, :], x_sb[:, t, :]))
                V.bn_aggr(mv[:, t, :], stats[:, t, :]).then_inc(s_step, 1)
                steps[0] += 1
            dve.wait_ge(s_step, steps[0])
            V.tensor_scalar(sd[:, 0, :], mv[:, :, 1], EPS, None, ALU.add).then_inc(s_mv, 1)
            dve.wait_ge(s_sd, 1)
            deviation(0, NT)
            link(V.tensor_scalar(sd[:, 3, :], sd[:, 3, :], 2.0 * WS, None, ALU.mult))
            for t in range(NT):
                V.tensor_scalar(xs[:, t, :], x_sb[:, t, :], mv[:, t, 0:1], sd[:, 3, t:t + 1], ALU.subtract,
                                ALU.mult).then_inc(s_ln, 1)

            def edge_keys():
                link(V.memset(cnt[:], 0.0))
                dve.wait_ge(s_edge, 5 * 16)
                V.tensor_copy(ef[0:EP, 0, :], edges[0:EP, 0, :])
                V.tensor_copy(ef[0:EP, 1, :], edges[0:EP, 1, :])
                V.tensor_copy(ef[0:EP, 2, :], edges[0:EP, 2, :])
                link(V.tensor_copy(cmp[0:EP, 0, :], edges[0:EP, 3, :]))
                V.scalar_tensor_tensor(out=ef[0:EP, 3, :], in0=cmp[0:EP, 0, :], scalar=float(NP),
                                       in1=ef[0:EP, 1, :], op0=ALU.mult, op1=ALU.add).then_inc(s_ekey, 1)
                for w in range(NW - 1):
                    link(V.tensor_scalar(cmp[0:EP, 1, :], ef[0:EP, 1, :], float(WIN * (w + 1)), 0.0, ALU.is_lt,
                                         ALU.add, accum_out=cnt[0:EP, w:w + 1]))
                dve.wait_ge(s_ekey, 1)
                link(V.tensor_tensor(cmp[0:EP, 0, :], ef[0:EP, 1, :], ef[0:EP, 2, :], ALU.is_gt))
                V.tensor_reduce(cnt[0:EP, NW - 1:NW], cmp[0:EP, 0, :], AX.X, ALU.add).then_inc(s_cnt, 1)

            def edge_limits():
                link(V.memset(lim[:], 0.0))
                dve.wait_ge(s_cntp, 1)
                link(V.tensor_copy(lim[:, 1:NW], abank[0][0:1, 0:NW - 1]))
                link(V.memset(lim[:, NW:NW + 1], float(NE)))
                link(V.tensor_tensor(num[:], lim[:, 1:NW + 1], lim[:, 0:NW], ALU.subtract))
                link(V.tensor_reduce(lim[:, NW + 1:NW + 2], num[:], AX.X, ALU.max))
                link(V.tensor_scalar(lim[:, NW + 2:NW + 3], lim[:, NW + 1:NW + 2], float(GE), None, ALU.is_le))
                link(V.tensor_scalar(lim[:, NW + 3:NW + 4], abank[0][0:1, NW - 1:NW], 0.0, None, ALU.is_equal))
                link(V.tensor_tensor(lim[:, NW:NW + 1], lim[:, NW + 2:NW + 3], lim[:, NW + 3:NW + 4], ALU.mult))
                V.tensor_copy(limi[:], lim[:, 0:NW + 1]).then_inc(s_lim, 1)

            def onehots(b, w, keys_s, keys_d):
                V.tensor_tensor(onehot_d[:, b], iota_d[:, :, bass.ds(w * WIN, WIN)].unsqueeze(1)
                                .to_broadcast([P, J, R, WIN]),
                                keys_d.unsqueeze(3).to_broadcast([P, J, R, WIN]), ALU.is_equal)
                for j in range(J):
                    last = V.tensor_scalar(onehot_s[:, b, j, 0:N], iota_s[:, 0:N], keys_s[:, :, j], None,
                                           ALU.is_equal)
                last.then_inc(s_oh, 1)

            def self_term(t, r):
                u = mr.first[("self", 0, r)]
                bank, mask = mr.bank(("self", 0, r))[:], nmask[:, r, bass.ds(t, 1)]
                mine = xs[:, bass.ds(t, 1), :].rearrange("p t d -> p (t d)")
                dve.wait_ge(mr.filled, t * NTY + u + 1)
                if r == 0:
                    V.tensor_scalar(mine, bank, mask, None, ALU.mult).then_inc(mr.dve, 1)
                else:
                    dve.wait_ge(mr.dve, t * NTY + mr.count(u, "D") - 1)
                    V.scalar_tensor_tensor(out=mine, in0=bank, scalar=mask, in1=mine, op0=ALU.mult,
                                           op1=ALU.add).then_inc(mr.dve, 1)

            for task in TASKS:
                kind, i = task[0], task[-1]
                if kind == "turn" and task[1] != "p":
                    turned_low(task, kcn(lo_of(task[1])[:, i, :]), kcn(hi_of(task[1])[:, i, :]), WS)
                elif kind == "direct":
                    m = task[1]
                    c = slice(i * KC // 2, (i + 1) * KC // 2)
                    dve.wait_ge(s_dhi, DIRECT.index(task) + 1)
                    V.scalar_tensor_tensor(out=lo_of(m)[:, c, :], in0=stage_of(m)[:, c, :], scalar=WS,
                                           in1=hi_of(m)[:, c, :], op0=ALU.mult,
                                           op1=ALU.subtract).then_inc(s_dlo, 1)
                elif kind == "x":
                    c = slice(i * P, (i + 1) * P)
                    turned_low(task, xlo[:, :, c], xhi[:, :, c], 1.0)
                elif kind == "bias":
                    dve.wait_ge(s_bhi, 1)
                    V.scalar_tensor_tensor(out=brow_lo[:], in0=brow[:], scalar=WS, in1=brow_hi[:], op0=ALU.mult,
                                           op1=ALU.subtract).then_inc(s_blo, 1)
                    link(V.tensor_copy(rt[:, 0, :], nt_i[:]))
                    for r in range(NTY):
                        V.tensor_scalar(nmask[:, r, :], rt[:, 0, :], float(r), RS * RS, ALU.is_equal, ALU.mult)\
                            .then_inc(s_step, 1)
                        steps[0] += 1
                    dve.wait_ge(s_step, steps[0])
                elif kind == "edge":
                    edge_keys()
                elif kind == "lim":
                    edge_limits()
                elif kind == "mm" and task[1] == "v":
                    mr.wait_filled(dve, task)
                    V.tensor_scalar(v_sb[:, i, :], mr.bank(task)[:], RS * RS, None, ALU.mult).then_inc(mr.dve, 1)
                elif kind == "mm" and task[1][0] == "r":
                    n = int(task[1][1]) * NT + i
                    mr.wait_act(dve, task)
                    V.scalar_tensor_tensor(out=xr[:, 1, n, :], in0=mr.bank(task)[:], scalar=RS,
                                           in1=xr[:, 0, n, :], op0=ALU.mult, op1=ALU.subtract)\
                        .then_inc(mr.dve, 1)
                elif kind == "kv":
                    dve.wait_ge(s_const, 3)
                    dve.wait_ge(s_par, 9 * 16)
                    mr.wait_filled(dve, task)
                    for h in range(2):
                        c = slice(h * DH, (h + 1) * DH)
                        last = V.tensor_tensor(attnT[c, :, c], kcn(mr.bank(task)[:])[c, :, c],
                                               temp[c, :].unsqueeze(2).to_broadcast([DH, HP, DH]), ALU.mult)
                    last.then_inc(mr.dve, 1)
                elif kind == "den":
                    if i == 0:
                        mr.wait_act(dve, ("ks",))
                        mr.wait_act(dve, ("mm", "q", NT - 1))
                    link(V.tensor_tensor(prod[:, i % 2, :], q_sb[:, i, :], ksumB, ALU.mult))
                    link(V.tensor_reduce(den[:, 0, i, :], prod[:, i % 2, :].rearrange("p (h d) -> p h d", h=H),
                                         AX.X, ALU.add))
                    link(V.tensor_scalar(den[:, 0, i, :], den[:, 0, i, :], 100.0, None, ALU.max))
                    link(V.reciprocal(den[:, 1, i, :], den[:, 0, i, :]))
                    qv = q_sb[:, i, :].rearrange("p (h d) -> p h d", h=H)
                    V.tensor_tensor(qv, qv, den[:, 1, i, :].unsqueeze(2).to_broadcast([P, H, DH]), ALU.mult)\
                        .then_inc(s_qn, 1)
                elif kind == "y":
                    mr.wait_filled(dve, task)
                    V.tensor_tensor(x_sb[:, i, :], mr.bank(task)[:], x_sb[:, i, :], ALU.add).then_inc(mr.dve, 1)
                elif kind == "ab":
                    link(V.memset(onehot_s[:, :, :, N:N + 1], 1.0))
                    V.memset(onehot_s[:, :, :, N + 1:NP], 0.0).then_inc(s_ohf, 2)
                    dve.wait_ge(s_const, 4)
                    dve.wait_ge(s_wk, 16 * NW)
                    dve.wait_ge(s_gk, 32)
                    ordered = dve.value_load(limi[0:1, NW:NW + 1], min_val=0, max_val=1)
                    with dve.If(ordered > 0):
                        with dve.Fori(0, NT) as t:
                            for i in range(WT):
                                dve.wait_ge(s_ohf, t * WT + i + 1)
                                kw = wkeys[:, bass.ds(t * WT + i, 1), :, :]
                                onehots(i % 2, t * WT + i, kw[:, :, 0, :],
                                        kw[:, :, 1, :].rearrange("p w j -> p j w"))
                                if i >= 1:
                                    self_term(t, i - 1)
                    with dve.Else():
                        with dve.Fori(0, NW) as w:
                            with dve.Fori(0, NG // 2) as gp:
                                for o in range(2):
                                    dve.wait_ge(s_ohf, w * NG + gp * 2 + o + 1)
                                    kg = gkeys[:, :, bass.ds(gp * 2 + o, 1), :]
                                    onehots(o, w, kg[:, 0], kg[:, 1].rearrange("p w j -> p j w"))
                        with dve.Fori(0, NT) as t:
                            for r in range(NTY):
                                self_term(t, r)
                elif kind == "agg" and i == AGGPARTS - 1:
                    u, t = task[0:2], task[1]
                    if t == 0:
                        mr.wait_emptied(dve, ("self", NT - 1, NTY - 1))
                    mr.wait_filled(dve, u)
                    V.scalar_tensor_tensor(out=xs[:, t, :], in0=mr.bank(u)[:], scalar=RS, in1=xs[:, t, :],
                                           op0=ALU.mult, op1=ALU.add).then_inc(mr.dve, 1)
                    mr.wait_emptied(dve, u)
                    link(V.scalar_tensor_tensor(out=x_sb[:, t, :], in0=xs[:, t, :], scalar=0.0,
                                                in1=x_sb[:, t, :], op0=ALU.max, op1=ALU.add))
                    link(V.bn_stats(stats[:, t, :], x_sb[:, t, :]))
                    link(V.bn_aggr(mv[:, t, :], stats[:, t, :]))
                    V.tensor_scalar(sd[:, 0, t:t + 1], mv[:, t, 1:2], EPS, None, ALU.add).then_inc(s_mv, 1)
                elif kind == "dev":
                    dve.wait_ge(s_sd, i + 2)
                    deviation(i, 1)
                    link(V.tensor_scalar(sd[:, 3, i:i + 1], sd[:, 3, i:i + 1], 2.0, None, ALU.mult))
                    V.tensor_scalar(xs[:, i, :], x_sb[:, i, :], mv[:, i, 0:1], sd[:, 3, i:i + 1],
                                    ALU.subtract, ALU.mult).then_inc(s_ln, 1)
                elif kind == "xl":
                    dve.wait_ge(s_xhi, i + 1)
                    V.scalar_tensor_tensor(out=xf[:, 1, i, :], in0=xs[:, i, :], scalar=WS, in1=xf[:, 0, i, :],
                                           op0=ALU.mult, op1=ALU.subtract).then_inc(s_xlo, 1)
                elif kind == "cum":
                    a, b = BATCHES[i]
                    tt = slice(a, b)
                    dve.wait_ge(s_lgp, b)
                    link(V.tensor_tensor(lg[:, 0, tt, :],
                                         abank[0][:, a * EX:b * EX].rearrange("p (t e) -> p t e", e=EX),
                                         swb[:].unsqueeze(1).to_broadcast([P, b - a, EX]), ALU.add))
                    link(V.tensor_reduce(rt[:, 1, tt], lg[:, 0, tt, :], AX.X, ALU.max))
                    top = rt[:, 1, tt].unsqueeze(2).to_broadcast([P, b - a, EX])
                    link(V.tensor_tensor(lg[:, 1, tt, :], lg[:, 0, tt, :], top, ALU.is_equal))
                    ie = iota_e[:].unsqueeze(1).to_broadcast([P, b - a, EX])
                    link(V.tensor_tensor(lg[:, 1, tt, :], lg[:, 1, tt, :], ie, ALU.mult))
                    link(V.tensor_reduce(rt[:, 2, tt], lg[:, 1, tt, :], AX.X, ALU.min))
                    V.tensor_tensor(oh16[:, tt, :], ie, rt[:, 2, tt].unsqueeze(2).to_broadcast([P, b - a, EX]),
                                    ALU.is_equal).then_inc(s_oh16, 1)
                    V.tensor_tensor(lg[:, 2, tt, :], lg[:, 0, tt, :], top, ALU.subtract).then_inc(s_exd, 1)
                    link(V.tensor_scalar(rt[:, 5, tt], rt[:, 2, tt], float(EX), None, ALU.add))
                elif kind == "route":
                    a, b = BATCHES[i]
                    tt = slice(a, b)
                    dve.wait_ge(s_cum, i + 1)
                    dve.wait_ge(s_oh16, i + 1)
                    link(V.tensor_tensor(lg[:, 1, tt, :], oh16[:, tt, :],
                                         abank[1][:, a * EX:b * EX].rearrange("p (t e) -> p t e", e=EX), ALU.mult))
                    link(V.tensor_reduce(rt[:, 3, tt], lg[:, 1, tt, :], AX.X, ALU.add))
                    V.tensor_scalar(rt[:, 6, tt], rt[:, 3, tt], float(CAP - 1), None, ALU.min)
                    link(V.tensor_scalar(rt[:, 4, tt], rt[:, 3, tt], float(CAP), None, ALU.is_lt))
                    V.tensor_scalar(rt[:, 8, tt], rt[:, 4, tt], -float(OOB), float(OOB), ALU.mult, ALU.add)
                    link(V.scalar_tensor_tensor(out=rt[:, 7, tt], in0=rt[:, 5, tt], scalar=float(CS),
                                                in1=rt[:, 6, tt], op0=ALU.mult, op1=ALU.add))
                    link(V.tensor_tensor(rt[:, 9, tt], rt[:, 8, tt], rt[:, 7, tt], ALU.add))
                    for t in range(a, b):
                        V.tensor_scalar(slot_of[:, t, :], iota_s[:], rt[:, 9, t:t + 1], None, ALU.is_equal)\
                            .then_inc(s_sel, 1)
                    V.scalar_tensor_tensor(out=rt[:, 3, tt], in0=rt[:, 5, tt], scalar=float(HALF),
                                           in1=rt[:, 6, tt], op0=ALU.mult, op1=ALU.add)
                    link(V.tensor_copy(slots[:, 1, tt], rt[:, 5, tt]))
                    if i == 0:
                        V.tensor_tensor(slots[:, 0, tt], rt[:, 3, tt], rt[:, 8, tt], ALU.add).then_inc(s_slot, 1)
                        continue
                    dve.wait_ge(s_exp, 1)
                    link(V.tensor_reduce(rt[:, 10, :], lg[:, 3, :, :], AX.X, ALU.add))
                    link(V.reciprocal(rt[:, 11, :], rt[:, 10, :]))
                    dve.wait_ge(s_const, 7)
                    V.tensor_copy(token[:, :, 1], rt[:, 11, :])
                    link(V.tensor_tensor(rt[:, 0, :], rt[:, 11, :], rt[:, 4, :], ALU.mult))
                    V.tensor_tensor(slots[:, 0, tt], rt[:, 3, tt], rt[:, 8, tt], ALU.add).then_inc(s_slot, 1)
                    link(V.tensor_tensor(rt[:, 1, :], rt[:, 11, :], rt[:, 0, :], ALU.subtract))
                elif kind == "dp" and task[1:3] == (0, 1):
                    tr.wait_filled(dve, task)
                    V.tensor_copy(dispatched(task), slots_in(task).rearrange("p (e c) -> p e c", e=EH))\
                        .then_inc(tr.dve, 1)
                elif kind == "base":
                    link(V.scalar_tensor_tensor(out=x_sb[:, i, :], in0=xs[:, i, :], scalar=rt[:, 1, i:i + 1],
                                                in1=x_sb[:, i, :], op0=ALU.mult, op1=ALU.add))
                    if i == 0:
                        dve.wait_ge(s_bt, 16 * NT)
                    n = rows(i)
                    V.scalar_tensor_tensor(out=x_sb[0:n, i, :], in0=bias_tok[0:n, i, :], scalar=rt[0:n, 0, i:i + 1],
                                           in1=x_sb[0:n, i, :], op0=ALU.mult, op1=ALU.add).then_inc(s_base, 1)
                elif kind == "ex" and i == KC - 1:
                    e, u = task[1], ("ex", task[1])
                    at = (e % 2) * HALF
                    if e % 2 == 0 and e >= 4:
                        dve.wait_ge(s_add[e // 2 % 2], 16 * (e // 4))
                    mr.wait_act(dve, u)
                    V.scalar_tensor_tensor(out=yexp[at:at + CS, e // 2 % 2, :], in0=mr.bank(u)[0:CS, :],
                                           scalar=RS * RS, in1=ylow[0:CS, e % 2, :], op0=ALU.mult, op1=ALU.add)\
                        .then_inc(mr.dve, 1)
                    if e % 2 == 1:
                        if e == 1:
                            dve.wait_ge(s_own, 16)
                        mr.wait_emptied(dve, u)
                        mine = yexp[0:HALF + CS, e // 2 % 2, :]
                        V.tensor_scalar(mine, mine, owner[0:HALF + CS, e // 2, 1:2], None, ALU.mult)\
                            .then_inc(s_scaled, 1)


_INS = ['x', 'src', 'dst', 'edge_type_3', 'node_type_3', 'L0_gnn_W_rel', 'L0_gnn_b_rel', 'L0_gnn_W_self',
        'L0_gnn_b_self', 'L0_mix_Wqkv', 'L0_mix_temperature', 'L0_mix_Wproj', 'L0_mix_bproj', 'L0_ffn_switch_w',
        'L0_ffn_switch_b', 'L0_ffn_expert_w', 'L0_ffn_expert_b']


def kernel(**inputs):
    import numpy as _np
    import concourse.bacc as _bacc
    from concourse import mybir as _mybir
    from concourse.bass_utils import run_bass_kernel_spmd as _run

    nc = _bacc.Bacc("TRN2", target_bir_lowering=False, num_devices=1)
    arrays, args = {}, []
    for name in _INS:
        a = _np.ascontiguousarray(inputs[name])
        arrays[f"in_{name}_dram"] = a
        args.append(nc.dram_tensor(f"in_{name}_dram", a.shape, _mybir.dt.from_np(a.dtype), kind="ExternalInput").ap())
    shape = inputs['x'].shape
    args.append(nc.dram_tensor("out_0_dram", shape, _mybir.dt.float32, kind="ExternalOutput").ap())
    gps_layer_kernel(nc, *args)
    r = _run(nc, [arrays], core_ids=[0])
    return r.results[0]["out_0_dram"]
```

```python
import concourse.bass as bass
from concourse import mybir
from contextlib import ExitStack


def gps_layer_kernel(
    nc: bass.Bass,
    x: bass.AP,
    src: bass.AP,
    dst: bass.AP,
    edge_type: bass.AP,
    node_type: bass.AP,
    W_rel: bass.AP,
    b_rel: bass.AP,
    W_self: bass.AP,
    b_self: bass.AP,
    Wqkv: bass.AP,
    temperature: bass.AP,
    Wproj: bass.AP,
    bproj: bass.AP,
    switch_w: bass.AP,
    switch_b: bass.AP,
    expert_w: bass.AP,
    expert_b: bass.AP,
    out: bass.AP,
):
    F32, F16, I32, U32 = mybir.dt.float32, mybir.dt.float16, mybir.dt.int32, mybir.dt.uint32
    ALU = mybir.AluOpType
    ACT = mybir.ActivationFunctionType
    AX = mybir.AxisListType

    P = 128
    N, D = x.shape
    NE = src.shape[0]
    R = W_rel.shape[0]
    NTY = W_self.shape[0]
    H = temperature.shape[0]
    DH = D // H
    EX = switch_w.shape[0]
    CAP = int(1.2 * N / EX)
    NT = (N + P - 1) // P
    TAIL = N - (NT - 1) * P
    NP = NT * P
    KC = D // P
    HP = D // P
    EPS = 1e-5
    WS = 256.0
    RS = 1.0 / WS
    OS = 16.0
    assert (NT - 1) * P == D

    WIN = 32
    NW = NP // WIN
    WT = NW // NT
    J = 5
    GE = J * P
    NG = -(-NE // GE)
    NG += NG % 2
    EPAD = NG * GE
    EC = 85
    EP = NE // EC
    assert EP * EC == NE and EP <= P and NE + GE <= EPAD
    NOKEY = 5000.0

    CS = 48
    HALF = 64
    NBT = EX // 2
    EH = EX // 2
    assert CAP <= CS and EH * CS <= D
    OOB = 100000

    ctx = ExitStack()
    with ctx:
        def sb(name, shape, dt):
            return ctx.enter_context(nc.sbuf_tensor(name, shape, dt))

        def sem(name):
            return ctx.enter_context(nc.semaphore(name))

        NSTAGE, NSPLIT = 3, 4
        x_sb = sb("x_sb", [P, NT, D], F32)
        xs = sb("xs", [P, NT, D], F32)
        xhi = sb("xhi", [P, KC, NP], F16)
        xlo = sb("xlo", [P, KC, NP], F16)
        stage = [sb(f"stage{i}", [P, KC, D], F32) for i in range(NSTAGE)]
        whi = [sb(f"whi{i}", [P, KC, D], F16) for i in range(NSPLIT)]
        wlo = [sb(f"wlo{i}", [P, KC, D], F16) for i in range(NSPLIT)]
        early = sb("early", [P, 12288], F32)
        k_sb = early[:, 0:2560].rearrange("p (t d) -> p t d", t=NT)
        v_sb = early[:, 2560:5120].rearrange("p (t d) -> p t d", t=NT)
        q_sb = early[:, 5120:7680].rearrange("p (t d) -> p t d", t=NT)
        qnT = early[:, 7680:10240].rearrange("p (g n) -> p g n", g=HP)
        oT = early[:, 0:2560].bitcast(F16).rearrange("p (h g n) -> p h g n", h=2, g=HP)
        onehot_s = early[:, 0:3200].bitcast(F16).rearrange("p (b j n) -> p b j n", b=2, j=J)
        onehot_d = early[:, 3200:3680].bitcast(F16).rearrange("p (b j r d) -> p b j r d", b=2, j=J, r=R)
        slot_of = early[:, 0:NT * EX * CS // 2].bitcast(F16).rearrange("p (t s) -> p t s", t=NT)
        xf = early[:, 2560:5120].bitcast(F16).rearrange("p (h t d) -> p h t d", h=2, t=NT)
        xfT = early[:, 5120:6144].rearrange("p (b k n) -> p b k n", b=2, k=KC)
        NY = 4
        yexp = early[:, 5120:7168].rearrange("p (b d) -> p b d", b=NY)
        ylow = early[:, 7168:8192].rearrange("p (b d) -> p b d", b=2)
        prod = xs[:, 0:2, :]
        xr = sb("xr", [P, 2, R * NT, D], F16)
        bias_tok = xr[:].rearrange("p h t d -> p (h t d)")[:, 0:NT * D * 2].bitcast(F32)\
            .rearrange("p (t d) -> p t d", t=NT)
        at_sb = sb("at_sb", [P, R * NT, NP], F16)
        bT = at_sb[:].rearrange("p t n -> p (t n)")[:, 0:KC * EX * P]\
            .rearrange("p (k e c) -> p k e c", k=KC, e=EX)
        attn = sb("attn", [P, HP, P], F32)
        ksumB = xs[:, NT - 1, :]
        k_sum = xs[:, NT - 2, :]
        pre = at_sb[:].rearrange("p t n -> p (t n)").bitcast(F32)
        edges = pre[:, 0:4 * EC].bitcast(I32).rearrange("p (a c) -> p a c", a=4)
        ef = pre[:, 4 * EC:8 * EC].rearrange("p (a c) -> p a c", a=4)
        cmp = pre[:, 8 * EC:10 * EC].rearrange("p (a c) -> p a c", a=2)
        padk = pre[0:1, 10 * EC:10 * EC + EPAD - NE]
        o = 10 * EC + EPAD - NE
        types_i = pre[0:NTY, o:o + NP].bitcast(I32)
        types_f = pre[0:NTY, o + NP:o + 2 * NP]
        bproj_all = pre[:, o + 2 * NP:o + 2 * NP + D]
        ident = sb("ident", [P, P], F32)
        onesf = sb("onesf", [P, P], F32)
        ones16 = sb("ones16", [P, P], F16)
        tri16 = sb("tri16", [P, P], F16)
        iota_s = sb("iota_s", [P, EX * CS], F16)
        iota_d = sb("iota_d", [P, R, NP], F16)
        iota_e = sb("iota_e", [P, EX], F32)
        sel_rel = sb("sel_rel", [P, R, P], F16)
        sel_type = sb("sel_type", [NTY, P], F16)
        brow = sb("brow", [P, D], F32)
        brow_hi = sb("brow_hi", [P, D], F16)
        brow_lo = sb("brow_lo", [P, D], F16)
        type_of = brow[0:NTY, 0:NP // 2].bitcast(F16)
        SELF_ROW = P - 8
        row_index = sb("row_index", [P, 1], F32)
        temp = sb("temp", [P, HP], F32)
        swb = sb("swb", [P, EX], F32)
        sw_sb = sb("sw_sb", [EX, D], F32)
        swT = sb("swT", [P, KC, EX], F32)
        cnt = sb("cnt", [P, NW], F32)
        lim = sb("lim", [1, NW + 4], F32)
        num = sb("num", [1, NW], F32)
        limi = sb("limi", [1, NW + 1], I32)
        wkeys = sb("wkeys", [P, NW, 2, J], F32)
        gkeys = sb("gkeys", [P, 2, NG, J], F32)
        nt_i = sb("nt_i", [P, NT], I32)
        nmask = sb("nmask", [P, NTY, NT], F32)
        stats = sb("stats", [P, NT, 6], F32)
        mv = sb("mv", [P, NT, 2], F32)
        sd = sb("sd", [P, 4, NT], F32)
        den = sb("den", [P, 2, NT, H], F32)
        lg = sb("lg", [P, 4, NT, EX], F32)
        oh16 = sb("oh16", [P, NT, EX], F16)
        rt = sb("rt", [P, 12, NT], F32)
        slots = sb("slots", [P, 2, NT], I32)
        token = sb("token", [P, NT, 2], F32)
        owner = sb("owner", [P, NBT, 2], F32)
        nobody = sb("nobody", [P, NBT, 2], I32)

        tbank = [ctx.enter_context(nc.psum_tensor(f"tbank{i}", [P, KC, P], F32)) for i in range(3)]
        mbank = [ctx.enter_context(nc.psum_tensor(f"mbank{i}", [P, D], F32)) for i in range(3)]
        abank = [ctx.enter_context(nc.psum_tensor(f"abank{i}", [P, D], F32)) for i in range(2)]

        key_dram = nc.dram_tensor("key_scratch", (2, EPAD), F32, kind="Internal").ap()
        owner_dram = nc.dram_tensor("owner_scratch", (NBT * P, 2), F32, kind="Internal").ap()

        EXPERTS = [f"e{e}" for e in range(EX)]
        MATS = ["k", "v", "q", "r0", "p", "r1", "r2", "s0", "s1", "s2"] + EXPERTS

        def turns(m):
            return [("turn", m, kc) for kc in range(KC)]

        def directs(m):
            return [("direct", m, h) for h in range(2)]

        def tiles(kind, *rest):
            return [(kind, *rest, t) for t in range(NT)]

        def weave(main, between):
            done, mixed = 0, []
            for i, task in enumerate(main):
                upto = min(len(between), -(-len(between) * (i + 1) // (len(main) - 1)))
                mixed += [task] + between[done:upto]
                done = upto
            return mixed

        def expert(e):
            return [("ex", e, kc) for kc in range(KC)]

        AHEAD = 9
        V = turns("v")
        TASKS = [("norm", 0)] + turns("k") + [("norm", 1), ("norm", 2), ("x", 0), ("norm", 3), ("norm", 4), ("x", 1)]
        TASKS += [("mm", "k", 0), ("x", 2), ("mm", "k", 1), ("x", 3), V[0], ("mm", "k", 2), ("x", 4), V[1],
                  ("mm", "k", 3), V[2], V[3], ("mm", "k", 4)]
        TASKS += weave(tiles("mm", "v"), turns("q") + [("bias",)])
        TASKS += [("ks",), ("kv",)]
        TASKS += weave(tiles("mm", "q"), directs("r0") + turns("p") + [("edge",)])
        DEN, R1, R2, QT = tiles("den"), directs("r1"), directs("r2"), tiles("qt")
        TASKS += [("mm", "r0", 0), *R1, ("mm", "r0", 1), DEN[0], ("mm", "r0", 2), DEN[1], ("mm", "r0", 3), DEN[2],
                  ("count",), ("mm", "r0", 4), DEN[3],
                  ("mm", "r1", 0), ("lim",), DEN[4], ("mm", "r1", 1), QT[0], R2[0], ("mm", "r1", 2),
                  QT[1], QT[2], ("mm", "r1", 3), QT[3], R2[1], ("mm", "r1", 4)]
        TASKS += [("ot", g) for g in range(HP)] + [QT[4], ("mm", "r2", 0), ("ot", HP)]
        TASKS += weave(tiles("y"), directs("s0") + directs("s1") + directs("s2"))
        TASKS += weave(tiles("mm", "r2")[1:-1] + [("ab",)], [("order",), ("sw",)] + turns("e0") + turns("e1")[0:2])
        E1 = turns("e1")
        TASKS += E1[2:3] + [("mm", "r2", NT - 1)] + E1[3:4]
        AGGPARTS = 5
        BATCHES = [(0, 2), (2, NT)]
        beside_turns = {0: 5, 1: 5, 2: 4, 3: 2, 4: 3}
        between = turns("e2") + turns("e3") + turns("e4") + turns("e5") + turns("e6")
        TASKS += between[0:1]
        between = between[1:]
        for t in range(NT):
            for part in range(AGGPARTS):
                TASKS += [("agg", t, part)]
                if AGGPARTS - beside_turns[t] <= part + (t == NT - 1) < AGGPARTS:
                    TASKS += between[0:1]
                    between = between[1:]
                if t >= 1 and part == 0:
                    TASKS += [("dev", t - 1)]
                if 1 <= t < NT - 1 and part == 3:
                    TASKS += [("lx", t - 1), ("xl", t - 1)]
                if 1 <= t < NT - 1 and part == 4:
                    TASKS += [("lo", t - 1)]
                if t == NT - 2:
                    TASKS += {0: [("cum", 0)], 3: [("pos", 0), ("route", 0)]}.get(part, [])
        E7, E8 = turns("e7"), turns("e8")
        TASKS += [("lx", NT - 2), ("lo", NT - 2), ("dev", NT - 1), E7[0], E7[1], ("lx", NT - 1), E7[2],
                  ("lo", NT - 1), ("cum", 1), E7[3], ("pos", 1), ("route", 1), E8[0], E8[1], ("xl", NT - 2),
                  ("xl", NT - 1)]

        def dispatch(half):
            order = [(0, 0), (0, 1), (1, 0), (1, 1)] + [(part, kc) for kc in range(2, KC) for part in range(2)]
            return [("dp", half, *pk) for pk in order]

        TASKS += dispatch(0)[0:2] + E8[2:3] + dispatch(0)[2:4] + E8[3:4] + dispatch(0)[4:]
        beside = dispatch(1)
        TASKS += beside[0:1]
        for e in range(EX):
            later = (e + 1) // 2 - 1 + AHEAD
            other = turns(f"e{later}")[(1 - e % 2) * 2:][:2] if 1 <= e and later < EX else []
            other = other + beside[e + 1:e + 2]
            TASKS += weave(expert(e), other)
            TASKS += [("base", t) for t in range(NT) if t + 1 == e]

        class Ring:

            def __init__(self, banks, name):
                self.banks, self.readers, self.first = banks, [], {}
                self.filled, self.act, self.dve = sem(name + "_filled"), sem(name + "_act"), sem(name + "_dve")

            def add(self, task, readers):
                self.first[task] = len(self.readers)
                self.readers.append(readers)

            def bank(self, task):
                return self.banks[self.first[task] % len(self.banks)]

            def count(self, u, reader):
                return sum(reader in r for r in self.readers[:u + 1])

            def wait_filled(self, eng, task):
                eng.wait_ge(self.filled, self.first[task] + 1)

            def wait_act(self, eng, task):
                eng.wait_ge(self.act, self.count(self.first[task], "A"))

            def wait_free(self, eng, task):
                u = self.first[task] - len(self.banks)
                if u >= 0:
                    self.wait_use(eng, u)

            def wait_emptied(self, eng, task):
                self.wait_use(eng, self.first[task])

            def wait_use(self, eng, u):
                if "D" in self.readers[u]:
                    eng.wait_ge(self.dve, self.count(u, "D"))
                else:
                    eng.wait_ge(self.act, self.count(u, "A"))

        tr, mr = Ring(tbank, "turn"), Ring(mbank, "prod")
        MM_READERS = {"k": "A", "q": "A", "v": "D", "r": "AD", "s": "D"}
        for task in TASKS:
            kind = task[0]
            if kind == "turn":
                tr.add(task, "AD")
            elif kind == "x":
                tr.add(task, "AD")
            elif kind == "dp":
                tr.add(task, "D" if task[1:3] == (0, 1) else "A")
            elif kind in ("qt", "sw", "lx"):
                tr.add(task, "A")
            elif kind == "mm":
                mr.add(task, MM_READERS[task[1][0]])
            elif kind in ("kv", "y"):
                mr.add(task, "D")
            elif kind == "agg" and task[2] == AGGPARTS - 1:
                mr.add(("agg", task[1]), "D")
            elif kind == "ks":
                mr.add(task, "A")
            elif kind == "ot":
                mr.add(task, "AD")
            elif kind == "ab":
                for t in range(NT):
                    for r in range(NTY):
                        mr.add(("self", t, r), "D")
            elif kind == "ex" and task[2] == KC - 1:
                mr.add(("ex", task[1]), "AD")
        DIRECT = [task for task in TASKS if task[0] == "direct"]

        place = [(whi[i][:], wlo[i][:]) for i in range(NSPLIT)]

        def kdn(ap):
            return ap.rearrange("p (k n) -> p k n", k=KC)

        for o in (8192, 10240):
            place.append((kdn(early[:, o:o + 1024].bitcast(F16)), kdn(early[:, o + 1024:o + 2048].bitcast(F16))))
        place.append((kdn(xhi[:].rearrange("p k n -> p (k n)")[:, 0:KC * D]),
                      kdn(xlo[:].rearrange("p k n -> p (k n)")[:, 0:KC * D])))
        xr_flat = xr[:].rearrange("p h t d -> p (h t d)")
        for i in range(2):
            o = NT * D * 2 + i * 2 * KC * D
            place.append((kdn(xr_flat[:, o:o + KC * D]), kdn(xr_flat[:, o + KC * D:o + 2 * KC * D])))
        PLACE = {"k": 0, "v": 1, "q": 2, "r0": 3, "p": 5, "r1": 0, "r2": 1, "s0": 2, "s1": 3, "s2": 0,
                 "e0": 4, "e1": 5, "e2": 1, "e3": 2, "e4": 3, "e5": 0, "e6": 6, "e7": 7, "e8": 8}
        for e in range(AHEAD, EX):
            PLACE[f"e{e}"] = PLACE[f"e{e - AHEAD}"]
        FREED = {4: ("y", NT - 1), 6: ("mm", f"r{R - 1}", NT - 1), 7: ("agg", NT - 1),
                 8: ("agg", NT - 1)}

        def last_use(m):
            if m[0] == "e":
                return ("ex", int(m[1:]))
            if m == "p":
                return ("y", NT - 1)
            return ("self", NT - 1, int(m[1])) if m[0] == "s" else ("mm", m, NT - 1)

        BEFORE = {}
        for m in MATS:
            BEFORE[m] = FREED.get(PLACE[m])
            FREED[PLACE[m]] = last_use(m)

        s_x = [sem(f"x_in{t}") for t in range(NT)]
        s_w = [sem(f"weights_in{i}") for i in range(NSTAGE)]
        s_first = [sem(f"first_weights_in{i}") for i in range(KC)]
        s_par = sem("params_in")
        s_const = sem("constants")
        s_edge = sem("edges_in")
        s_step = sem("dve_step")
        s_mv = sem("variance_ready")
        s_sd = sem("deviation_ready")
        s_norm = sem("scale_and_shift_ready")
        s_lnd = sem("even_tile_normalised")
        s_lna = sem("odd_tile_normalised")
        s_ln = sem("normalised_again")
        s_dhi = sem("direct_hi")
        s_dlo = sem("direct_lo")
        s_bhi = sem("bias_hi")
        s_blo = sem("bias_lo")
        s_ekey = sem("edge_keys")
        s_cnt = sem("edge_counts")
        s_cntp = sem("edge_totals")
        s_lim = sem("window_limits")
        s_kst = sem("keys_stored")
        s_wk = sem("window_keys_in")
        s_gk = sem("group_keys_in")
        s_oh = sem("onehots_ready")
        s_ohf = sem("onehots_free")
        s_abf = sem("window_bank_free")
        s_ksum = sem("keys_summed")
        s_qn = sem("queries_scaled")
        s_lgp = sem("logits_ready")
        s_oh16 = sem("routes_ready")
        s_cum = sem("positions_ready")
        s_exd = sem("logits_shifted")
        s_exp = sem("exp_ready")
        s_slot = sem("slots_ready")
        s_xhi = sem("tokens_hi")
        s_xlo = sem("tokens_lo")
        s_sel = sem("slot_onehots_ready")
        s_init = sem("owners_cleared")
        s_scat = sem("owners_scattered")
        s_own = sem("owners_in")
        s_bt = sem("token_bias_in")
        s_base = sem("base_ready")
        s_add = [sem(f"results_added{i}") for i in range(NY)]
        s_scaled = sem("results_scaled")
        s_out = sem("stored")

        s_pool = sem("pool_step")
        s_bproj = sem("bproj_added")
        s_types = sem("type_rows_ready")
        PARAMS = 10
        block = ctx.enter_context(nc.Block())

        def rows(t):
            return TAIL if t == NT - 1 else P

        def stage_of(m):
            return stage[MATS.index(m) % NSTAGE]

        def wait_stage(eng, m):
            i = MATS.index(m)
            eng.wait_ge(s_w[i % NSTAGE], 16 * (i // NSTAGE + (i % NSTAGE > 0)))

        def hi_of(m):
            return place[PLACE[m]][0]

        def lo_of(m):
            return place[PLACE[m]][1]

        def wait_split(eng, m):
            if ("turn", m, KC - 1) in tr.first:
                tr.wait_emptied(eng, ("turn", m, KC - 1))
            else:
                eng.wait_ge(s_dlo, DIRECT.index(("direct", m, 1)) + 1)

        def wait_place(eng, m):
            if BEFORE[m] is not None:
                mr.wait_filled(eng, BEFORE[m])

        def outputs_in(task):
            bank = mr.bank(task)
            return bank[:] if task[1] < HP else bank[:].rearrange("p (g n) -> p g n", g=HP)

        def outputs_to(part, i):
            return oT[:, part, i, 0:D] if i < HP else oT[:, part, :, D:NP]

        def slots_in(task):
            return tr.bank(task)[:].rearrange("p k n -> p (k n)")[:, 0:EH * CS]

        def dispatched(task):
            _, half, part, kc = task
            return bT[:, kc, half * EH:(half + 1) * EH, part * HALF:part * HALF + CS]

        @block.sync
        def _(sp):
            for t in range(NT):
                if t == NT - 1:
                    sp.wait_ge(s_const, 2)
                sp.dma_start(x_sb[0:rows(t), t, :], x[t * P:t * P + rows(t), :]).then_inc(s_x[t], 16)
            source = {"k": Wqkv[D:2 * D], "v": Wqkv[2 * D:3 * D], "q": Wqkv[0:D], "p": Wproj}
            for r in range(R):
                source[f"r{r}"] = W_rel[r]
            for r in range(NTY):
                source[f"s{r}"] = W_self[r]
            for e in range(EX):
                source[f"e{e}"] = expert_w[e]
            for i, m in enumerate(MATS):
                if i >= NSTAGE:
                    old = MATS[i - NSTAGE]
                    if ("turn", old, KC - 1) in tr.first:
                        tr.wait_filled(sp, ("turn", old, KC - 1))
                    else:
                        sp.wait_ge(s_dlo, DIRECT.index(("direct", old, 1)) + 1)
                if m == f"e{EX - 2}":
                    for t in range(NT):
                        sp.wait_ge(s_base, t + 1)
                        sp.dma_start(out[t * P:t * P + rows(t), :], x_sb[0:rows(t), t, :]).then_inc(s_out, 16)
                if i == 0:
                    for kc in range(KC):
                        sp.dma_start(stage_of(m)[:, kc, :], source[m][kc * P:(kc + 1) * P, :])\
                          .then_inc(s_first[kc], 16)
                else:
                    sp.dma_start(stage_of(m)[:], source[m].rearrange("(k p) n -> p k n", p=P))\
                      .then_inc(s_w[i % NSTAGE], 16)
            sp.wait_ge(s_out, 16 * NT)
            for i in range(NY):
                sp.wait_ge(s_add[i], 16 * NBT // NY)

        @block.gpsimd
        def _(pool):
            steps = [0]

            def link(ins):
                steps[0] += 1
                ins.then_inc(s_pool, 1)
                pool.wait_ge(s_pool, steps[0])

            link(nc.gpsimd.memset(ident[:], 0.0))
            nc.gpsimd.affine_select(out=ident[:], in_=ident[:], compare_op=ALU.not_equal, fill=1.0, base=0,
                                    pattern=[[-1, P]], channel_multiplier=1).then_inc(s_const, 1)
            nc.gpsimd.memset(x_sb[:, NT - 1, :], 0.0).then_inc(s_const, 1)
            link(nc.gpsimd.memset(edges[:, 2, :], 2 ** 20))
            flat = "(p c) -> p c"
            pool.dma_start(edges[0:EP, 1, :], dst.rearrange(flat, c=EC)).then_inc(s_edge, 16)
            pool.dma_start(edges[0:EP - 1, 2, :], dst[1:1 + (EP - 1) * EC].rearrange(flat, c=EC)).then_inc(s_edge, 16)
            pool.dma_start(edges[EP - 1:EP, 2, 0:EC - 1], dst[1 + (EP - 1) * EC:NE].unsqueeze(0)).then_inc(s_edge, 16)
            pool.dma_start(edges[0:EP, 0, :], src.rearrange(flat, c=EC)).then_inc(s_edge, 16)
            pool.dma_start(edges[0:EP, 3, :], edge_type.rearrange(flat, c=EC)).then_inc(s_edge, 16)
            link(nc.gpsimd.memset(brow[:], 0.0))
            link(nc.gpsimd.memset(nt_i[:], 0))
            link(nc.gpsimd.memset(types_i, -1))
            pool.dma_start(brow[0:R, :], b_rel).then_inc(s_par, 16)
            pool.dma_start(brow[SELF_ROW:SELF_ROW + NTY, :], b_self).then_inc(s_par, 16)
            pool.dma_start(bproj_all, bproj.unsqueeze(0).to_broadcast([P, D])).then_inc(s_par, 16)
            pool.dma_start(types_i[:, 0:N], node_type.unsqueeze(0).to_broadcast([NTY, N])).then_inc(s_par, 16)
            pool.dma_start(nt_i[:, 0:NT - 1], node_type[0:(NT - 1) * P].rearrange("(t p) -> p t", p=P),
                           allow_slow_non_contiguous=True).then_inc(s_par, 16)
            pool.dma_start(nt_i[0:TAIL, NT - 1:NT], node_type[(NT - 1) * P:N].unsqueeze(1)).then_inc(s_par, 16)
            tv = temperature.rearrange("(g h) a b -> h (a b g)", h=2)
            for h in range(2):
                pool.dma_start(temp[h * DH:(h + 1) * DH, :], tv[h:h + 1, :].to_broadcast([DH, HP]),
                               allow_slow_non_contiguous=True).then_inc(s_par, 16)
            pool.dma_start(swb[:], switch_b.unsqueeze(0).to_broadcast([P, EX])).then_inc(s_par, 16)
            pool.dma_start(sw_sb[:], switch_w).then_inc(s_par, 16)
            assert NP - N > NTY and SELF_ROW > TAIL + R
            link(nc.gpsimd.memset(sel_rel[:], 0.0))
            link(nc.gpsimd.memset(sel_type[:], 0.0))
            link(nc.gpsimd.affine_select(out=sel_rel[:], in_=sel_rel[:], compare_op=ALU.not_equal, fill=WS,
                                         base=-TAIL, pattern=[[-1000, R], [1, P]], channel_multiplier=1000))
            link(nc.gpsimd.affine_select(out=sel_rel[:, 0, :], in_=sel_rel[:, 0, :], compare_op=ALU.not_equal,
                                         fill=WS, base=SELF_ROW - TAIL - 1, pattern=[[1, P]],
                                         channel_multiplier=-1))
            nc.gpsimd.affine_select(out=sel_type[:], in_=sel_type[:], compare_op=ALU.not_equal, fill=1.0,
                                    base=-TAIL - 1, pattern=[[1, P]], channel_multiplier=-1)
            nc.gpsimd.iota(row_index[:], [[0, 1]], base=0, channel_multiplier=1,
                           allow_small_or_imprecise_dtypes=True)
            nc.gpsimd.memset(attn[:], 0.0)
            nc.gpsimd.memset(onesf[:], 1.0).then_inc(s_const, 1)
            nc.gpsimd.iota(iota_s[:], [[1, EX * CS]], base=0, channel_multiplier=0,
                           allow_small_or_imprecise_dtypes=True)
            nc.gpsimd.iota(iota_d[:], [[NP, R], [1, NP]], base=0, channel_multiplier=0,
                           allow_small_or_imprecise_dtypes=True).then_inc(s_const, 1)
            tr.wait_filled(pool, ("x", NT - 1))
            for t in range(1, NT):
                mr.wait_emptied(pool, ("mm", "k", t))
                link(nc.gpsimd.tensor_tensor(k_sum, k_sb[:, 0, :] if t == 1 else k_sum, k_sb[:, t, :], ALU.add))
            pool.sem_inc(s_ksum, 1)
            pool.wait_ge(s_lnd, (NT + 1) // 2)
            pool.wait_ge(s_lna, NT // 2)
            pool.wait_ge(s_par, PARAMS * 16)
            for t in range(NT):
                nc.gpsimd.tensor_tensor(x_sb[:, t, :], x_sb[:, t, :], bproj_all, ALU.add).then_inc(s_bproj, 1)
            nc.gpsimd.iota(iota_e[:], [[1, EX]], base=-EX, channel_multiplier=0,
                           allow_small_or_imprecise_dtypes=True)
            link(nc.gpsimd.memset(ones16[:], 1.0))
            nc.gpsimd.affine_select(out=tri16[:], in_=ones16[:], compare_op=ALU.is_gt, fill=0.0, base=0,
                                    pattern=[[1, P]], channel_multiplier=-1).then_inc(s_const, 1)
            link(nc.gpsimd.memset(padk, NOKEY))
            pool.wait_ge(s_ekey, 1)
            pool.dma_start(key_dram[0, 0:NE].rearrange(flat, c=EC), ef[0:EP, 0, :]).then_inc(s_kst, 16)
            pool.dma_start(key_dram[1, 0:NE].rearrange(flat, c=EC), ef[0:EP, 3, :]).then_inc(s_kst, 16)
            for k in range(2):
                pool.dma_start(key_dram[k:k + 1, NE:EPAD], padk).then_inc(s_kst, 16)
            pool.wait_ge(s_kst, 64)
            for k in range(2):
                pool.dma_start(gkeys[:, k, :, :], key_dram[k].rearrange("(g p j) -> p g j", p=P, j=J))\
                    .then_inc(s_gk, 16)
            pool.wait_ge(s_lim, 1)
            with pool.Fori(0, NW) as w:
                start = pool.value_load(limi[0:1, bass.ds(w, 1)], min_val=0, max_val=NE)
                pool.dma_start(wkeys[:, bass.ds(w, 1), :, :].rearrange("p w k j -> p (w k) j"),
                               key_dram[:, bass.ds(start, GE)].rearrange("k (p j) -> p k j", j=J))\
                    .then_inc(s_wk, 16)
            nc.gpsimd.memset(nobody[:], OOB).then_inc(s_const, 1)
            nc.gpsimd.iota(token[:, :, 0].bitcast(I32), [[P, NT]], base=0, channel_multiplier=1)\
                .then_inc(s_const, 1)
            pool.wait_ge(s_const, 7)
            pool.dma_start(owner_dram.rearrange("(i p) c -> p i c", p=P), nobody[:].bitcast(F32))\
                .then_inc(s_init, 16)
            pool.wait_ge(s_init, 16)
            pool.wait_ge(s_slot, len(BATCHES))
            for t in range(NT):
                n = rows(t)
                pool.indirect_dma_start(bias_tok[0:n, t, :], None, expert_b,
                                        bass.IndirectOffsetOnAxis(ap=slots[0:n, 1, t:t + 1].bitcast(U32), axis=0),
                                        bounds_check=EX - 1, oob_is_err=False).then_inc(s_bt, 16)
            for t in range(NT):
                n = rows(t)
                pool.indirect_dma_start(owner_dram,
                                        bass.IndirectOffsetOnAxis(ap=slots[0:n, 0, t:t + 1].bitcast(U32), axis=0),
                                        token[0:n, t, :], None, bounds_check=NBT * P - 1, oob_is_err=False)\
                    .then_inc(s_scat, 16)
            pool.wait_ge(s_scat, 16 * NT)
            pool.dma_start(owner[:], owner_dram.rearrange("(i p) c -> p i c", p=P)).then_inc(s_own, 16)
            pool.wait_ge(s_own, 16)
            for i in range(NBT):
                if i == 0:
                    pool.wait_ge(s_out, 16 * NT)
                pool.wait_ge(s_scaled, i + 1)
                pool.indirect_dma_start(out,
                                        bass.IndirectOffsetOnAxis(ap=owner[0:HALF + CS, i, 0:1].bitcast(U32), axis=0),
                                        yexp[0:HALF + CS, i % NY, :], None, bounds_check=N - 1, oob_is_err=False,
                                        compute_op=ALU.add).then_inc(s_add[i % NY], 16)

        @block.tensor
        def _(pe):
            def turn(task, chunks):
                tr.wait_free(pe, task)
                for i, chunk in enumerate(chunks):
                    last = nc.tensor.transpose(tr.bank(task)[:, i, :], chunk, ident[:])
                last.then_inc(tr.filled, 1)

            def row_chunks(rows_of):
                return [rows_of[:, kc * P:(kc + 1) * P] for kc in range(KC)]

            def split_product(bank, m, cols, bias):
                first = True
                for kc in range(KC):
                    a, b = xhi[:, kc, cols], xlo[:, kc, cols]
                    for lhs, rhs in ((a, hi_of(m)), (a, lo_of(m)), (b, hi_of(m))):
                        last = nc.tensor.matmul(bank, lhs, rhs[:, kc, :], start=first, stop=False,
                                                skip_group_check=True)
                        first = False
                if bias is not None:
                    for part in (brow_hi, brow_lo):
                        last = nc.tensor.matmul(bank, bias, part[:], start=False, stop=False, skip_group_check=True)
                return last

            def window(bank, b, w, first):
                if first:
                    at = (NT - 1) * R * WIN
                    nc.tensor.matmul(bank[:, at:at + WIN], sel_type[:], type_of[:, bass.ds(w * WIN, WIN)],
                                     start=True, stop=False, skip_group_check=True)
                for st in range(NT):
                    for j in range(J):
                        last = nc.tensor.matmul(bank[:, st * R * WIN:(st + 1) * R * WIN],
                                                onehot_s[:, b, j, st * P:(st + 1) * P],
                                                onehot_d[:, b, j, :, :].rearrange("p r d -> p (r d)"),
                                                start=False, stop=False,
                                                skip_group_check=True)
                return last

            def self_product(t, r):
                u = mr.first[("self", 0, r)]
                pe.wait_ge(mr.dve, t * NTY + mr.count(u - 3, "D"))
                split_product(mr.bank(("self", 0, r))[:], f"s{r}", bass.ds(t * P, P), None)\
                    .then_inc(mr.filled, 1)

            pe.wait_ge(s_const, 1)
            for task in TASKS:
                kind, i = task[0], task[-1]
                if kind == "turn":
                    m = task[1]
                    if m == MATS[0]:
                        pe.wait_ge(s_first[i], 16)
                    else:
                        wait_stage(pe, m)
                    turn(task, row_chunks(stage_of(m)[:, i, :]))
                elif kind == "x":
                    pe.wait_ge(s_lna if i % 2 else s_lnd, i // 2 + 1)
                    turn(task, row_chunks(xs[:, i, :]))
                elif kind == "mm":
                    m, bias = task[1], None
                    if m == "k":
                        tr.wait_emptied(pe, ("x", i))
                    if m == "r0" and i == 0:
                        pe.wait_ge(s_blo, 1)
                        pe.wait_ge(s_const, 3)
                    if i == 0:
                        wait_split(pe, m)
                    if m[0] == "r" and i == NT - 1:
                        bias = sel_rel[:, int(m[1]), :]
                    mr.wait_free(pe, task)
                    split_product(mr.bank(task)[:], m, slice(i * P, (i + 1) * P), bias).then_inc(mr.filled, 1)
                elif kind == "kv":
                    mr.wait_free(pe, task)
                    mr.wait_emptied(pe, ("mm", "k", NT - 1))
                    mr.wait_emptied(pe, ("mm", "v", NT - 1))
                    for g in range(HP):
                        c = slice(g * P, (g + 1) * P)
                        for t in range(NT):
                            last = nc.tensor.matmul(mr.bank(task)[:, c], k_sb[:, t, c], v_sb[:, t, c],
                                                    start=(t == 0), stop=(t == NT - 1))
                    last.then_inc(mr.filled, 1)
                elif kind == "ks":
                    pe.wait_ge(s_const, 3)
                    mr.wait_free(pe, task)
                    pe.wait_ge(s_ksum, 1)
                    nc.tensor.matmul(mr.bank(task)[:], onesf[:], k_sum, start=True, stop=True)\
                        .then_inc(mr.filled, 1)
                elif kind == "qt":
                    pe.wait_ge(s_qn, i + 1)
                    turn(task, row_chunks(q_sb[:, i, :]))
                elif kind == "count":
                    pe.wait_ge(s_cnt, 1)
                    nc.tensor.matmul(abank[0][:, 0:NW], onesf[:], cnt[:], start=True, stop=True)\
                        .then_inc(s_cntp, 1)
                elif kind == "ot":
                    if i == 0:
                        mr.wait_emptied(pe, ("kv",))
                        for t in range(NT - 1):
                            tr.wait_emptied(pe, ("qt", t))
                    mr.wait_free(pe, task)
                    if i < HP:
                        last = nc.tensor.matmul(mr.bank(task)[:], attn[:, i, :], qnT[:, i, 0:D], start=True, stop=True)
                    else:
                        tr.wait_emptied(pe, ("qt", NT - 1))
                        for g in range(HP):
                            last = nc.tensor.matmul(mr.bank(task)[:, g * P:(g + 1) * P], attn[:, g, :],
                                                    qnT[:, g, D:NP], start=True, stop=True)
                    last.then_inc(mr.filled, 1)
                elif kind == "y":
                    if i == 0:
                        wait_split(pe, "p")
                        mr.wait_emptied(pe, ("ot", HP - 1))
                    if i == NT - 1:
                        mr.wait_emptied(pe, ("ot", HP))
                    mr.wait_free(pe, task)
                    cols = slice(i * P, (i + 1) * P)
                    for g in range(HP):
                        for n, (part, w) in enumerate(((0, hi_of("p")), (0, lo_of("p")), (1, hi_of("p")))):
                            last = nc.tensor.matmul(mr.bank(task)[:], oT[:, part, g, cols], w[:, g, :],
                                                    start=(g == 0 and n == 0), stop=(g == HP - 1 and n == 2))
                    last.then_inc(mr.filled, 1)
                elif kind == "ab":
                    for r in range(NTY):
                        wait_split(pe, f"s{r}")
                    pe.wait_ge(s_types, 1)
                    with pe.If(ordered > 0):
                        with pe.Fori(0, NT) as t:
                            for i in range(WT):
                                if i < NTY:
                                    self_product(t, i)
                                pe.wait_ge(s_abf, t * WT + i + 1)
                                pe.wait_ge(s_oh, t * WT + i + 1)
                                window(abank[i % 2], i % 2, t * WT + i, True).then_inc(s_ohf, 1)
                    with pe.Else():
                        with pe.Fori(0, NW // 2) as pair:
                            for b in range(2):
                                pe.wait_ge(s_abf, pair * 2 + b + 1)
                                for o in range(2):
                                    pe.wait_ge(s_oh, (pair * 2 + b) * NG + o + 1)
                                    window(abank[b], o, pair * 2 + b, o == 0).then_inc(s_ohf, 1)
                                with pe.Fori(1, NG // 2) as gp:
                                    for o in range(2):
                                        pe.wait_ge(s_oh, (pair * 2 + b) * NG + gp * 2 + o + 1)
                                        window(abank[b], o, pair * 2 + b, False).then_inc(s_ohf, 1)
                        with pe.Fori(0, NT) as t:
                            for r in range(NTY):
                                self_product(t, r)
                elif kind == "order":
                    pe.wait_ge(s_lim, 1)
                    ordered = pe.value_load(limi[0:1, NW:NW + 1], min_val=0, max_val=1)
                elif kind == "sw":
                    tr.wait_free(pe, task)
                    for kc in range(KC):
                        last = nc.tensor.transpose(tr.bank(task)[:, 0, kc * EX:(kc + 1) * EX],
                                                   sw_sb[:, kc * P:(kc + 1) * P], ident[0:EX, 0:EX])
                    last.then_inc(tr.filled, 1)
                elif kind == "agg":
                    u, t, count = task[0:2], task[1], R * NT // AGGPARTS
                    if t == 0 and i == 0:
                        mr.wait_emptied(pe, ("mm", f"r{R - 1}", NT - 2))
                        pe.wait_ge(s_abf, NW + 2)
                    if t == 0 and i == AGGPARTS - 1:
                        mr.wait_emptied(pe, ("mm", f"r{R - 1}", NT - 1))
                    if i == 0:
                        mr.wait_free(pe, u)
                    for n in range(i * count, (i + 1) * count):
                        for part in range(2):
                            last = nc.tensor.matmul(mr.bank(u)[:], at_sb[:, n, t * P:(t + 1) * P],
                                                    xr[:, part, n, :], start=(n == 0 and part == 0),
                                                    stop=(n == R * NT - 1 and part == 1))
                    if i == AGGPARTS - 1:
                        last.then_inc(mr.filled, 1)
                elif kind == "lx":
                    pe.wait_ge(s_ln, i + 1)
                    turn(task, row_chunks(xs[:, i, :]))
                elif kind == "lo":
                    tr.wait_emptied(pe, ("lx", i))
                    for kc in range(KC):
                        last = nc.tensor.matmul(abank[0][:, i * EX:(i + 1) * EX], xfT[:, i % 2, kc, :],
                                                swT[:, kc, :], start=(kc == 0), stop=(kc == KC - 1))
                    last.then_inc(s_lgp, 1)
                elif kind == "pos":
                    pe.wait_ge(s_const, 5)
                    pe.wait_ge(s_oh16, i + 1)
                    for t in range(*BATCHES[i]):
                        for o in range(t + 1):
                            last = nc.tensor.matmul(abank[1][:, t * EX:(t + 1) * EX],
                                                    tri16[:] if o == t else ones16[:], oh16[:, o, :],
                                                    start=(o == 0), stop=(o == t))
                    last.then_inc(s_cum, 1)
                elif kind == "dp":
                    _, half, part, kc = task
                    pe.wait_ge(s_xlo if part else s_xhi, NT)
                    pe.wait_ge(s_sel, NT)
                    tr.wait_free(pe, task)
                    for t in range(NT):
                        n = rows(t)
                        last = nc.tensor.matmul(slots_in(task), xf[0:n, part, t, kc * P:(kc + 1) * P],
                                                slot_of[0:n, t, half * EH * CS:(half + 1) * EH * CS],
                                                start=(t == 0), stop=(t == NT - 1))
                    last.then_inc(tr.filled, 1)
                elif kind == "ex":
                    e, u = task[1], ("ex", task[1])
                    if i == 0:
                        if e % EH == 0:
                            for part in range(2):
                                tr.wait_emptied(pe, ("dp", e // EH, part, KC - 1))
                        wait_split(pe, f"e{e}")
                        mr.wait_free(pe, u)
                    for n, w in enumerate((hi_of(f"e{e}"), lo_of(f"e{e}"))):
                        last = nc.tensor.matmul(mr.bank(u)[0:HALF + CS, :], bT[:, i, e, 0:HALF + CS], w[:, i, :],
                                                start=(i == 0 and n == 0), stop=(i == KC - 1 and n == 1))
                    if i == KC - 1:
                        last.then_inc(mr.filled, 1)

        @block.scalar
        def _(act):
            act.wait_ge(s_mv, 1)
            nc.scalar.activation(sd[:, 1, :], sd[:, 0, :], ACT.Sqrt).then_inc(s_sd, 1)
            for task in TASKS:
                kind, i = task[0], task[-1]
                if kind in ("turn", "x", "qt", "sw", "lx"):
                    if kind == "turn" and i == 0:
                        wait_place(act, task[1])
                    if kind == "lx" and i >= 2:
                        act.wait_ge(s_lgp, i - 1)
                    tr.wait_filled(act, task)
                    bank = tr.bank(task)
                    if kind == "turn":
                        ins = nc.scalar.activation(hi_of(task[1])[:, :, i * P:(i + 1) * P], bank[:], ACT.Copy,
                                                   scale=WS)
                    elif kind == "x":
                        ins = nc.scalar.activation(xhi[:, :, i * P:(i + 1) * P], bank[:], ACT.Copy)
                    elif kind == "qt":
                        ins = nc.scalar.activation(qnT[:, :, i * P:(i + 1) * P], bank[:], ACT.Copy)
                    elif kind == "sw":
                        ins = nc.scalar.activation(swT[:].rearrange("p k e -> p (k e)"), bank[:, 0, 0:KC * EX],
                                                   ACT.Copy)
                    else:
                        ins = nc.scalar.activation(xfT[:, i % 2, :, :], bank[:], ACT.Copy)
                    ins.then_inc(tr.act, 1)
                    if kind == "lx":
                        act.wait_ge(s_ln, i + 1)
                        nc.scalar.activation(xf[:, 0, i, :], xs[:, i, :], ACT.Copy, scale=WS).then_inc(s_xhi, 1)
                elif kind == "dp" and task[1:3] != (0, 1):
                    if task[1:] == (0, 0, 0):
                        mr.wait_emptied(act, ("agg", NT - 1))
                    tr.wait_filled(act, task)
                    nc.scalar.activation(dispatched(task), slots_in(task).rearrange("p (e c) -> p e c", e=EH),
                                         ACT.Copy).then_inc(tr.act, 1)
                elif kind == "direct":
                    m = task[1]
                    if i == 0:
                        wait_place(act, m)
                        wait_stage(act, m)
                    c = slice(i * KC // 2, (i + 1) * KC // 2)
                    nc.scalar.activation(hi_of(m)[:, c, :], stage_of(m)[:, c, :], ACT.Copy, scale=WS)\
                        .then_inc(s_dhi, 1)
                elif kind == "norm" and i % 2 == 1:
                    act.wait_ge(s_norm, 1)
                    nc.scalar.activation(xs[:, i, :], x_sb[:, i, :], ACT.Identity, bias=sd[:, 2, i:i + 1],
                                         scale=sd[:, 3, i:i + 1]).then_inc(s_lna, 1)
                elif kind == "bias":
                    act.wait_ge(s_par, PARAMS * 16)
                    nc.scalar.activation(brow_hi[:], brow[:], ACT.Copy, scale=WS).then_inc(s_bhi, 1)
                elif kind == "mm" and task[1][0] in "kqr":
                    m = task[1]
                    mr.wait_filled(act, task)
                    if m[0] == "r":
                        nc.scalar.activation(xr[:, 0, int(m[1]) * NT + i, :], mr.bank(task)[:], ACT.Copy,
                                             scale=RS).then_inc(mr.act, 1)
                    else:
                        nc.scalar.activation((k_sb if m == "k" else q_sb)[:, i, :], mr.bank(task)[:], ACT.Relu,
                                             scale=RS * RS).then_inc(mr.act, 1)
                elif kind == "ks":
                    mr.wait_filled(act, task)
                    nc.scalar.activation(ksumB, mr.bank(task)[:], ACT.Copy).then_inc(mr.act, 1)
                elif kind == "ot":
                    mr.wait_filled(act, task)
                    nc.scalar.activation(outputs_to(0, i), outputs_in(task), ACT.Copy, scale=OS).then_inc(mr.act, 1)
                elif kind == "ab":
                    act.sem_inc(s_abf, 2)
                    act.wait_ge(s_kst, 64)
                    counts = at_sb[:].rearrange("p (r s) n -> p s r n", s=NT)

                    def empty_window(w, b):
                        v = abank[b][:, 0:NT * R * WIN].rearrange("p (s r d) -> p s r d", s=NT, r=R)
                        nc.scalar.activation(counts[:, :, :, bass.ds(w * WIN, WIN)], v, ACT.Copy)\
                            .then_inc(s_abf, 1)

                    with act.If(ordered > 0):
                        with act.Fori(0, NT) as t:
                            for i in range(WT):
                                act.wait_ge(s_ohf, t * WT + i + 1 + 2)
                                empty_window(t * WT + i, i % 2)
                    with act.Else():
                        with act.Fori(0, NW // 2) as pair:
                            for b in range(2):
                                act.wait_ge(s_ohf, (pair * 2 + b + 1) * NG + 2)
                                empty_window(pair * 2 + b, b)
                elif kind == "order":
                    act.wait_ge(s_lim, 1)
                    ordered = act.value_load(limi[0:1, NW:NW + 1], min_val=0, max_val=1)
                elif kind == "dev":
                    act.wait_ge(s_mv, i + 2)
                    nc.scalar.activation(sd[:, 1, i:i + 1], sd[:, 0, i:i + 1], ACT.Sqrt).then_inc(s_sd, 1)
                elif kind == "route":
                    if i == 1:
                        act.wait_ge(s_exd, 2)
                        nc.scalar.activation(lg[:, 3, :, :], lg[:, 2, :, :], ACT.Exp).then_inc(s_exp, 1)
                elif kind == "ex" and i == KC - 1:
                    e, u = task[1], ("ex", task[1])
                    if e >= 2:
                        mr.wait_emptied(act, ("ex", e - 2))
                    mr.wait_filled(act, u)
                    nc.scalar.activation(ylow[0:CS, e % 2, :], mr.bank(u)[HALF:HALF + CS, :], ACT.Copy,
                                         scale=RS * RS).then_inc(mr.act, 1)

        @block.vector
        def _(dve):
            steps = [0]

            def link(ins):
                steps[0] += 1
                ins.then_inc(s_step, 1)
                dve.wait_ge(s_step, steps[0])

            V = nc.vector

            def deviation(c, n):
                link(V.reciprocal(sd[:, 2, c:c + n], sd[:, 1, c:c + n]))
                link(V.tensor_tensor(sd[:, 2, c:c + n], sd[:, 2, c:c + n], sd[:, 0, c:c + n], ALU.mult))
                link(V.tensor_tensor(sd[:, 2, c:c + n], sd[:, 2, c:c + n], sd[:, 1, c:c + n], ALU.add))
                link(V.reciprocal(sd[:, 3, c:c + n], sd[:, 2, c:c + n]))

            def turned_low(task, low, high, scale):
                tr.wait_act(dve, task)
                V.scalar_tensor_tensor(out=low, in0=tr.bank(task)[:], scalar=scale, in1=high, op0=ALU.mult,
                                       op1=ALU.subtract).then_inc(tr.dve, 1)

            def kcn(ap):
                return ap.rearrange("p (k n) -> p k n", k=KC)

            for t in range(NT):
                dve.wait_ge(s_x[t], 16)
                link(V.bn_stats(stats[:, t, :], x_sb[:, t, :]))
                V.bn_aggr(mv[:, t, :], stats[:, t, :]).then_inc(s_step, 1)
                steps[0] += 1
            dve.wait_ge(s_step, steps[0])
            V.tensor_scalar(sd[:, 0, :], mv[:, :, 1], EPS, None, ALU.add).then_inc(s_mv, 1)
            dve.wait_ge(s_sd, 1)
            deviation(0, NT)
            link(V.tensor_scalar(sd[:, 3, :], sd[:, 3, :], 2.0 * WS, None, ALU.mult))
            V.scalar_tensor_tensor(out=sd[:, 2, :], in0=mv[:, :, 0], scalar=-1.0, in1=sd[:, 3, :], op0=ALU.mult,
                                   op1=ALU.mult).then_inc(s_norm, 1)

            def edge_keys():
                link(V.memset(cnt[:], 0.0))
                dve.wait_ge(s_edge, 5 * 16)
                V.tensor_copy(ef[0:EP, 0, :], edges[0:EP, 0, :])
                V.tensor_copy(ef[0:EP, 1, :], edges[0:EP, 1, :])
                V.tensor_copy(ef[0:EP, 2, :], edges[0:EP, 2, :])
                link(V.tensor_copy(cmp[0:EP, 0, :], edges[0:EP, 3, :]))
                V.scalar_tensor_tensor(out=ef[0:EP, 3, :], in0=cmp[0:EP, 0, :], scalar=float(NP),
                                       in1=ef[0:EP, 1, :], op0=ALU.mult, op1=ALU.add).then_inc(s_ekey, 1)
                for w in range(NW - 1):
                    link(V.tensor_scalar(cmp[0:EP, 1, :], ef[0:EP, 1, :], float(WIN * (w + 1)), 0.0, ALU.is_lt,
                                         ALU.add, accum_out=cnt[0:EP, w:w + 1]))
                dve.wait_ge(s_ekey, 1)
                link(V.tensor_tensor(cmp[0:EP, 0, :], ef[0:EP, 1, :], ef[0:EP, 2, :], ALU.is_gt))
                V.tensor_reduce(cnt[0:EP, NW - 1:NW], cmp[0:EP, 0, :], AX.X, ALU.add).then_inc(s_cnt, 1)

            def edge_limits():
                link(V.memset(lim[:], 0.0))
                dve.wait_ge(s_cntp, 1)
                link(V.tensor_copy(lim[:, 1:NW], abank[0][0:1, 0:NW - 1]))
                link(V.memset(lim[:, NW:NW + 1], float(NE)))
                link(V.tensor_tensor(num[:], lim[:, 1:NW + 1], lim[:, 0:NW], ALU.subtract))
                link(V.tensor_reduce(lim[:, NW + 1:NW + 2], num[:], AX.X, ALU.max))
                link(V.tensor_scalar(lim[:, NW + 2:NW + 3], lim[:, NW + 1:NW + 2], float(GE), None, ALU.is_le))
                link(V.tensor_scalar(lim[:, NW + 3:NW + 4], abank[0][0:1, NW - 1:NW], 0.0, None, ALU.is_equal))
                link(V.tensor_tensor(lim[:, NW:NW + 1], lim[:, NW + 2:NW + 3], lim[:, NW + 3:NW + 4], ALU.mult))
                V.tensor_copy(limi[:], lim[:, 0:NW + 1]).then_inc(s_lim, 1)

            def onehots(b, w, keys_s, keys_d):
                V.tensor_tensor(onehot_d[:, b], iota_d[:, :, bass.ds(w * WIN, WIN)].unsqueeze(1)
                                .to_broadcast([P, J, R, WIN]),
                                keys_d.unsqueeze(3).to_broadcast([P, J, R, WIN]), ALU.is_equal)
                for j in range(J):
                    last = V.tensor_scalar(onehot_s[:, b, j, 0:N], iota_s[:, 0:N], keys_s[:, :, j], None,
                                           ALU.is_equal)
                last.then_inc(s_oh, 1)

            def self_term(t, r):
                u = mr.first[("self", 0, r)]
                bank, mask = mr.bank(("self", 0, r))[:], nmask[:, r, bass.ds(t, 1)]
                mine = xs[:, bass.ds(t, 1), :].rearrange("p t d -> p (t d)")
                dve.wait_ge(mr.filled, t * NTY + u + 1)
                if r == 0:
                    V.tensor_scalar(mine, bank, mask, None, ALU.mult).then_inc(mr.dve, 1)
                else:
                    dve.wait_ge(mr.dve, t * NTY + mr.count(u, "D") - 1)
                    V.scalar_tensor_tensor(out=mine, in0=bank, scalar=mask, in1=mine, op0=ALU.mult,
                                           op1=ALU.add).then_inc(mr.dve, 1)

            for task in TASKS:
                kind, i = task[0], task[-1]
                if kind == "turn":
                    c = slice(i * P, (i + 1) * P)
                    turned_low(task, lo_of(task[1])[:, :, c], hi_of(task[1])[:, :, c], WS)
                elif kind == "direct":
                    m = task[1]
                    c = slice(i * KC // 2, (i + 1) * KC // 2)
                    dve.wait_ge(s_dhi, DIRECT.index(task) + 1)
                    V.scalar_tensor_tensor(out=lo_of(m)[:, c, :], in0=stage_of(m)[:, c, :], scalar=WS,
                                           in1=hi_of(m)[:, c, :], op0=ALU.mult,
                                           op1=ALU.subtract).then_inc(s_dlo, 1)
                elif kind == "x":
                    c = slice(i * P, (i + 1) * P)
                    turned_low(task, xlo[:, :, c], xhi[:, :, c], 1.0)
                elif kind == "norm" and i % 2 == 0:
                    V.tensor_scalar(xs[:, i, :], x_sb[:, i, :], mv[:, i, 0:1], sd[:, 3, i:i + 1], ALU.subtract,
                                    ALU.mult).then_inc(s_lnd, 1)
                elif kind == "bias":
                    dve.wait_ge(s_bhi, 1)
                    V.scalar_tensor_tensor(out=brow_lo[:], in0=brow[:], scalar=WS, in1=brow_hi[:], op0=ALU.mult,
                                           op1=ALU.subtract).then_inc(s_blo, 1)
                    link(V.tensor_copy(types_f, types_i))
                    dve.wait_ge(s_blo, 1)
                    dve.wait_ge(s_const, 3)
                    V.tensor_scalar(type_of, types_f, row_index[0:NTY, :], None, ALU.is_equal).then_inc(s_types, 1)
                    link(V.tensor_copy(rt[:, 0, :], nt_i[:]))
                    for r in range(NTY):
                        V.tensor_scalar(nmask[:, r, :], rt[:, 0, :], float(r), RS * RS, ALU.is_equal, ALU.mult)\
                            .then_inc(s_step, 1)
                        steps[0] += 1
                    dve.wait_ge(s_step, steps[0])
                elif kind == "edge":
                    edge_keys()
                elif kind == "lim":
                    edge_limits()
                elif kind == "mm" and task[1] == "v":
                    mr.wait_filled(dve, task)
                    V.tensor_scalar(v_sb[:, i, :], mr.bank(task)[:], RS * RS, None, ALU.mult).then_inc(mr.dve, 1)
                elif kind == "mm" and task[1][0] == "r":
                    n = int(task[1][1]) * NT + i
                    mr.wait_act(dve, task)
                    V.scalar_tensor_tensor(out=xr[:, 1, n, :], in0=mr.bank(task)[:], scalar=RS,
                                           in1=xr[:, 0, n, :], op0=ALU.mult, op1=ALU.subtract)\
                        .then_inc(mr.dve, 1)
                elif kind == "kv":
                    dve.wait_ge(s_const, 3)
                    dve.wait_ge(s_par, PARAMS * 16)
                    mr.wait_filled(dve, task)
                    for h in range(2):
                        c = slice(h * DH, (h + 1) * DH)
                        last = V.tensor_tensor(attn[c, :, c], kcn(mr.bank(task)[:])[c, :, c],
                                               temp[c, :].unsqueeze(2).to_broadcast([DH, HP, DH]), ALU.mult)
                    last.then_inc(mr.dve, 1)
                elif kind == "den":
                    if i == 0:
                        mr.wait_act(dve, ("ks",))
                        mr.wait_act(dve, ("mm", "q", NT - 1))
                    link(V.tensor_tensor(prod[:, i % 2, :], q_sb[:, i, :], ksumB, ALU.mult))
                    link(V.tensor_reduce(den[:, 0, i, :], prod[:, i % 2, :].rearrange("p (h d) -> p h d", h=H),
                                         AX.X, ALU.add))
                    link(V.tensor_scalar(den[:, 0, i, :], den[:, 0, i, :], 100.0, None, ALU.max))
                    link(V.reciprocal(den[:, 1, i, :], den[:, 0, i, :]))
                    qv = q_sb[:, i, :].rearrange("p (h d) -> p h d", h=H)
                    V.tensor_tensor(qv, qv, den[:, 1, i, :].unsqueeze(2).to_broadcast([P, H, DH]), ALU.mult)\
                        .then_inc(s_qn, 1)
                elif kind == "y":
                    dve.wait_ge(s_bproj, i + 1)
                    mr.wait_filled(dve, task)
                    V.scalar_tensor_tensor(out=x_sb[:, i, :], in0=mr.bank(task)[:], scalar=RS / OS,
                                           in1=x_sb[:, i, :], op0=ALU.mult, op1=ALU.add).then_inc(mr.dve, 1)
                elif kind == "ot":
                    mr.wait_act(dve, task)
                    V.scalar_tensor_tensor(out=outputs_to(1, i), in0=outputs_in(task), scalar=OS,
                                           in1=outputs_to(0, i), op0=ALU.mult, op1=ALU.subtract).then_inc(mr.dve, 1)
                elif kind == "order":
                    link(V.memset(onehot_s[:, :, :, N:N + 1], 1.0))
                    V.memset(onehot_s[:, :, :, N + 1:NP], 0.0).then_inc(s_ohf, 2)
                    dve.wait_ge(s_lim, 1)
                    ordered = dve.value_load(limi[0:1, NW:NW + 1], min_val=0, max_val=1)
                elif kind == "ab":
                    dve.wait_ge(s_const, 4)
                    dve.wait_ge(s_wk, 16 * NW)
                    dve.wait_ge(s_gk, 32)
                    with dve.If(ordered > 0):
                        with dve.Fori(0, NT) as t:
                            for i in range(WT):
                                dve.wait_ge(s_ohf, t * WT + i + 1)
                                kw = wkeys[:, bass.ds(t * WT + i, 1), :, :]
                                onehots(i % 2, t * WT + i, kw[:, :, 0, :],
                                        kw[:, :, 1, :].rearrange("p w j -> p j w"))
                                if i >= 1:
                                    self_term(t, i - 1)
                    with dve.Else():
                        with dve.Fori(0, NW) as w:
                            with dve.Fori(0, NG // 2) as gp:
                                for o in range(2):
                                    dve.wait_ge(s_ohf, w * NG + gp * 2 + o + 1)
                                    kg = gkeys[:, :, bass.ds(gp * 2 + o, 1), :]
                                    onehots(o, w, kg[:, 0], kg[:, 1].rearrange("p w j -> p j w"))
                        with dve.Fori(0, NT) as t:
                            for r in range(NTY):
                                self_term(t, r)
                elif kind == "agg" and i == AGGPARTS - 1:
                    u, t = task[0:2], task[1]
                    if t == 0:
                        mr.wait_emptied(dve, ("self", NT - 1, NTY - 1))
                    mr.wait_filled(dve, u)
                    V.scalar_tensor_tensor(out=xs[:, t, :], in0=mr.bank(u)[:], scalar=RS, in1=xs[:, t, :],
                                           op0=ALU.mult, op1=ALU.add).then_inc(mr.dve, 1)
                    mr.wait_emptied(dve, u)
                    link(V.scalar_tensor_tensor(out=x_sb[:, t, :], in0=xs[:, t, :], scalar=0.0,
                                                in1=x_sb[:, t, :], op0=ALU.max, op1=ALU.add))
                    link(V.bn_stats(stats[:, t, :], x_sb[:, t, :]))
                    link(V.bn_aggr(mv[:, t, :], stats[:, t, :]))
                    V.tensor_scalar(sd[:, 0, t:t + 1], mv[:, t, 1:2], EPS, None, ALU.add).then_inc(s_mv, 1)
                elif kind == "dev":
                    dve.wait_ge(s_sd, i + 2)
                    deviation(i, 1)
                    link(V.tensor_scalar(sd[:, 3, i:i + 1], sd[:, 3, i:i + 1], 2.0, None, ALU.mult))
                    V.tensor_scalar(xs[:, i, :], x_sb[:, i, :], mv[:, i, 0:1], sd[:, 3, i:i + 1],
                                    ALU.subtract, ALU.mult).then_inc(s_ln, 1)
                elif kind == "xl":
                    dve.wait_ge(s_xhi, i + 1)
                    V.scalar_tensor_tensor(out=xf[:, 1, i, :], in0=xs[:, i, :], scalar=WS, in1=xf[:, 0, i, :],
                                           op0=ALU.mult, op1=ALU.subtract).then_inc(s_xlo, 1)
                elif kind == "cum":
                    a, b = BATCHES[i]
                    tt = slice(a, b)
                    dve.wait_ge(s_lgp, b)
                    link(V.tensor_tensor(lg[:, 0, tt, :],
                                         abank[0][:, a * EX:b * EX].rearrange("p (t e) -> p t e", e=EX),
                                         swb[:].unsqueeze(1).to_broadcast([P, b - a, EX]), ALU.add))
                    link(V.tensor_reduce(rt[:, 1, tt], lg[:, 0, tt, :], AX.X, ALU.max))
                    top = rt[:, 1, tt].unsqueeze(2).to_broadcast([P, b - a, EX])
                    link(V.tensor_tensor(lg[:, 1, tt, :], lg[:, 0, tt, :], top, ALU.is_equal))
                    ie = iota_e[:].unsqueeze(1).to_broadcast([P, b - a, EX])
                    link(V.tensor_tensor(lg[:, 1, tt, :], lg[:, 1, tt, :], ie, ALU.mult))
                    link(V.tensor_reduce(rt[:, 2, tt], lg[:, 1, tt, :], AX.X, ALU.min))
                    V.tensor_tensor(oh16[:, tt, :], ie, rt[:, 2, tt].unsqueeze(2).to_broadcast([P, b - a, EX]),
                                    ALU.is_equal).then_inc(s_oh16, 1)
                    V.tensor_tensor(lg[:, 2, tt, :], lg[:, 0, tt, :], top, ALU.subtract).then_inc(s_exd, 1)
                    link(V.tensor_scalar(rt[:, 5, tt], rt[:, 2, tt], float(EX), None, ALU.add))
                elif kind == "route":
                    a, b = BATCHES[i]
                    tt = slice(a, b)
                    dve.wait_ge(s_cum, i + 1)
                    dve.wait_ge(s_oh16, i + 1)
                    link(V.tensor_tensor(lg[:, 1, tt, :], oh16[:, tt, :],
                                         abank[1][:, a * EX:b * EX].rearrange("p (t e) -> p t e", e=EX), ALU.mult))
                    link(V.tensor_reduce(rt[:, 3, tt], lg[:, 1, tt, :], AX.X, ALU.add))
                    V.tensor_scalar(rt[:, 6, tt], rt[:, 3, tt], float(CAP - 1), None, ALU.min)
                    link(V.tensor_scalar(rt[:, 4, tt], rt[:, 3, tt], float(CAP), None, ALU.is_lt))
                    V.tensor_scalar(rt[:, 8, tt], rt[:, 4, tt], -float(OOB), float(OOB), ALU.mult, ALU.add)
                    link(V.scalar_tensor_tensor(out=rt[:, 7, tt], in0=rt[:, 5, tt], scalar=float(CS),
                                                in1=rt[:, 6, tt], op0=ALU.mult, op1=ALU.add))
                    link(V.tensor_tensor(rt[:, 9, tt], rt[:, 8, tt], rt[:, 7, tt], ALU.add))
                    for t in range(a, b):
                        V.tensor_scalar(slot_of[:, t, :], iota_s[:], rt[:, 9, t:t + 1], None, ALU.is_equal)\
                            .then_inc(s_sel, 1)
                    V.scalar_tensor_tensor(out=rt[:, 3, tt], in0=rt[:, 5, tt], scalar=float(HALF),
                                           in1=rt[:, 6, tt], op0=ALU.mult, op1=ALU.add)
                    link(V.tensor_copy(slots[:, 1, tt], rt[:, 5, tt]))
                    if i == 0:
                        V.tensor_tensor(slots[:, 0, tt], rt[:, 3, tt], rt[:, 8, tt], ALU.add).then_inc(s_slot, 1)
                        continue
                    dve.wait_ge(s_exp, 1)
                    link(V.tensor_reduce(rt[:, 10, :], lg[:, 3, :, :], AX.X, ALU.add))
                    link(V.reciprocal(rt[:, 11, :], rt[:, 10, :]))
                    dve.wait_ge(s_const, 7)
                    V.tensor_copy(token[:, :, 1], rt[:, 11, :])
                    link(V.tensor_tensor(rt[:, 0, :], rt[:, 11, :], rt[:, 4, :], ALU.mult))
                    V.tensor_tensor(slots[:, 0, tt], rt[:, 3, tt], rt[:, 8, tt], ALU.add).then_inc(s_slot, 1)
                    link(V.tensor_tensor(rt[:, 1, :], rt[:, 11, :], rt[:, 0, :], ALU.subtract))
                elif kind == "dp" and task[1:3] == (0, 1):
                    tr.wait_filled(dve, task)
                    V.tensor_copy(dispatched(task), slots_in(task).rearrange("p (e c) -> p e c", e=EH))\
                        .then_inc(tr.dve, 1)
                elif kind == "base":
                    link(V.scalar_tensor_tensor(out=x_sb[:, i, :], in0=xs[:, i, :], scalar=rt[:, 1, i:i + 1],
                                                in1=x_sb[:, i, :], op0=ALU.mult, op1=ALU.add))
                    if i == 0:
                        dve.wait_ge(s_bt, 16 * NT)
                    n = rows(i)
                    V.scalar_tensor_tensor(out=x_sb[0:n, i, :], in0=bias_tok[0:n, i, :], scalar=rt[0:n, 0, i:i + 1],
                                           in1=x_sb[0:n, i, :], op0=ALU.mult, op1=ALU.add).then_inc(s_base, 1)
                elif kind == "ex" and i == KC - 1:
                    e, u = task[1], ("ex", task[1])
                    at = (e % 2) * HALF
                    if e % 2 == 0 and e >= 2 * NY:
                        dve.wait_ge(s_add[e // 2 % NY], 16 * (e // 2 // NY))
                    mr.wait_act(dve, u)
                    V.scalar_tensor_tensor(out=yexp[at:at + CS, e // 2 % NY, :], in0=mr.bank(u)[0:CS, :],
                                           scalar=RS * RS, in1=ylow[0:CS, e % 2, :], op0=ALU.mult, op1=ALU.add)\
                        .then_inc(mr.dve, 1)
                    if e % 2 == 1:
                        if e == 1:
                            dve.wait_ge(s_own, 16)
                        mr.wait_emptied(dve, u)
                        mine = yexp[0:HALF + CS, e // 2 % NY, :]
                        V.tensor_scalar(mine, mine, owner[0:HALF + CS, e // 2, 1:2], None, ALU.mult)\
                            .then_inc(s_scaled, 1)


_INS = ['x', 'src', 'dst', 'edge_type_3', 'node_type_3', 'L0_gnn_W_rel', 'L0_gnn_b_rel', 'L0_gnn_W_self',
        'L0_gnn_b_self', 'L0_mix_Wqkv', 'L0_mix_temperature', 'L0_mix_Wproj', 'L0_mix_bproj', 'L0_ffn_switch_w',
        'L0_ffn_switch_b', 'L0_ffn_expert_w', 'L0_ffn_expert_b']


def kernel(**inputs):
    import numpy as _np
    import concourse.bacc as _bacc
    from concourse import mybir as _mybir
    from concourse.bass_utils import run_bass_kernel_spmd as _run

    nc = _bacc.Bacc("TRN2", target_bir_lowering=False, num_devices=1)
    arrays, args = {}, []
    for name in _INS:
        a = _np.ascontiguousarray(inputs[name])
        arrays[f"in_{name}_dram"] = a
        args.append(nc.dram_tensor(f"in_{name}_dram", a.shape, _mybir.dt.from_np(a.dtype), kind="ExternalInput").ap())
    shape = inputs['x'].shape
    args.append(nc.dram_tensor("out_0_dram", shape, _mybir.dt.float32, kind="ExternalOutput").ap())
    gps_layer_kernel(nc, *args)
    r = _run(nc, [arrays], core_ids=[0])
    return r.results[0]["out_0_dram"]
```
